# Optimizing a Trainium2 kernel written in Bass

```python
import numpy as np
import jax
import jax.numpy as jnp

def _softmax(x, axis=-1):
    return jax.nn.softmax(x, axis=axis)

def _gelu(x):
    return jax.nn.gelu(x, approximate=True)

def _silu(x):
    return jax.nn.silu(x)

def _sigmoid(x):
    return jax.nn.sigmoid(x)

def _layernorm(x, axis=-1, eps=1e-05):
    m = jnp.mean(x, axis=axis, keepdims=True)
    v = jnp.var(x, axis=axis, keepdims=True)
    return (x - m) / jnp.sqrt(v + eps)

def _scatter_add(tgt, idx, src, axis=0):
    return tgt.at[idx].add(src)

def _segment_sum(src, seg, n):
    return jax.ops.segment_sum(src, seg, n)
kernel_name = 'mk_decoder_postln_d1_seqx_r8_3138d7'

def setup_inputs(seed: int=0):
    np.random.seed(seed)
    _w = jnp.asarray

    def _rec_inputs():
        import jax
        import jax.numpy as jnp
        _rk = jax.random.key(seed)
        x = -0.0003929 + 0.9999 * jax.random.normal(jax.random.fold_in(_rk, 1), (16, 256, 128), jnp.float32)
        _lenS = 256 - jax.random.randint(jax.random.fold_in(_rk, 7), (16,), 0, max(1, 256 // 4) + 1, jnp.int32)
        _lenS2 = 1601 - jax.random.randint(jax.random.fold_in(_rk, 8), (16,), 0, max(1, 1601 // 4) + 1, jnp.int32)
        _ctx_512P = jax.random.normal(jax.random.fold_in(_rk, 11), (16, 16, 64), jnp.float32)
        _ctx_512c = jax.random.dirichlet(jax.random.fold_in(_rk, 511), 0.3 * jnp.ones((16,), jnp.float32), (16, 1601))
        _ctx_512t = jnp.einsum('bsk,bkd->bsd', _ctx_512c, _ctx_512P)
        _ctx_512t = _ctx_512t * jax.lax.rsqrt(jnp.mean(jnp.square(_ctx_512t)) + 1e-12) * 0.953939
        ctx_512 = -1.39393e-06 + 0.999914 * (_ctx_512t + 0.3 * jax.random.normal(jax.random.fold_in(_rk, 611), (16, 1601, 64), jnp.float32))
        return (x, ctx_512)
    x, ctx_512 = _rec_inputs()

    def _L0_attn_setup():
        import jax, jax.numpy as jnp
        import numpy as np
        B_, L_, D_RES, D_INNER, N_STATE, K_CONV = (2, 128, 128, 64, 32, 3)

        def _causal_dwconv(x, w, b):
            xt = jnp.transpose(x, (0, 2, 1))
            k = w.shape[-1]
            out = jax.lax.conv_general_dilated(xt, w, (1,), [(k - 1, 0)], feature_group_count=w.shape[0])
            return jnp.transpose(out, (0, 2, 1)) + b

        def _s6(u, W_delta, b_delta, W_B, W_C, A_log, D):
            A = -jnp.exp(A_log)
            delta = jax.nn.softplus(u @ W_delta + b_delta)
            Bm = u @ W_B
            Cm = u @ W_C

            def step(h, inputs):
                u_t, d_t, b_t, c_t = inputs
                dA = jnp.exp(d_t[..., None] * A)
                h = dA * h + (d_t * u_t)[..., None] * b_t[:, None, :]
                y = jnp.einsum('bdn,bn->bd', h, c_t)
                return (h, y)
            h0 = jnp.zeros((u.shape[0], A.shape[0], A.shape[1]), u.dtype)
            xs = (jnp.swapaxes(u, 0, 1), jnp.swapaxes(delta, 0, 1), jnp.swapaxes(Bm, 0, 1), jnp.swapaxes(Cm, 0, 1))
            _, ys = jax.lax.scan(step, h0, xs)
            return jnp.swapaxes(ys, 0, 1) + u * D
        key = jax.random.key(seed)
        ks = jax.random.split(key, 8)
        s = lambda k, shp, sc: jax.random.normal(k, shp, dtype=jnp.float32) * sc
        return {'x': s(ks[0], (B_, L_, D_RES), 1.0), 'ln_gamma': jnp.ones((D_RES,), jnp.float32), 'ln_beta': jnp.zeros((D_RES,), jnp.float32), 'W_up': s(ks[1], (D_RES, 2 * D_INNER), 0.02), 'b_up': jnp.zeros((2 * D_INNER,), jnp.float32), 'conv_w': s(ks[2], (D_INNER, 1, K_CONV), 0.2), 'conv_b': jnp.zeros((D_INNER,), jnp.float32), 'W_delta': s(ks[3], (D_INNER, D_INNER), 0.02), 'b_delta': jnp.full((D_INNER,), -4.0, jnp.float32), 'W_B': s(ks[4], (D_INNER, N_STATE), 0.02), 'W_C': s(ks[5], (D_INNER, N_STATE), 0.02), 'A_log': jnp.log(jnp.broadcast_to(jnp.arange(1, N_STATE + 1, dtype=jnp.float32), (D_INNER, N_STATE))).copy(), 'D': jnp.ones((D_INNER,), jnp.float32), 'W_down': s(ks[6], (D_INNER, D_RES), 0.02), 'b_down': jnp.zeros((D_RES,), jnp.float32)}
    _L0_attn_all = _L0_attn_setup()
    _L0_attn_in = {k: v for k, v in _L0_attn_all.items() if k in ('ln_gamma', 'ln_beta', 'W_up', 'b_up', 'conv_w', 'conv_b', 'W_delta', 'b_delta', 'W_B', 'W_C', 'A_log', 'D', 'W_down', 'b_down')}
    del _L0_attn_all

    def _L0_xattn_setup():
        import jax, jax.numpy as jnp
        import numpy as np
        HEADS = 16
        D_MODEL = 128
        IMG_MODEL = 64
        D_K = D_MODEL // HEADS
        key = jax.random.key(seed)
        ks = jax.random.split(key, 12)
        B, LQ, LKV = (8, 256, 128)
        s_dm = 1.0 / np.sqrt(D_MODEL)
        s_im = 1.0 / np.sqrt(IMG_MODEL)
        return {'q': jax.random.normal(ks[0], (B, LQ, D_MODEL), jnp.float32), 'k': jax.random.normal(ks[1], (B, LKV, IMG_MODEL), jnp.float32), 'v': jax.random.normal(ks[2], (B, LKV, IMG_MODEL), jnp.float32), 'Wq': jax.random.normal(ks[3], (D_MODEL, D_MODEL), jnp.float32) * s_dm, 'bq': jnp.zeros((D_MODEL,), jnp.float32), 'Wk': jax.random.normal(ks[4], (IMG_MODEL, D_MODEL), jnp.float32) * s_im, 'bk': jnp.zeros((D_MODEL,), jnp.float32), 'Wv': jax.random.normal(ks[5], (IMG_MODEL, D_MODEL), jnp.float32) * s_im, 'bv': jnp.zeros((D_MODEL,), jnp.float32), 'Wo': jax.random.normal(ks[6], (D_MODEL, D_MODEL), jnp.float32) * s_dm, 'bo': jnp.zeros((D_MODEL,), jnp.float32)}
    _L0_xattn_all = _L0_xattn_setup()
    _L0_xattn_in = {k: v for k, v in _L0_xattn_all.items() if k in ('Wq', 'bq', 'Wk', 'bk', 'Wv', 'bv', 'Wo', 'bo')}
    del _L0_xattn_all

    def _L0_ffn_setup():
        import jax, jax.numpy as jnp
        import numpy as np
        DIM = 128
        HIDDEN = 512
        E = 8
        B, S = (2, 512)
        key = jax.random.key(seed)
        ks = jax.random.split(key, 8)
        sd = 1.0 / np.sqrt(DIM)
        sh = 1.0 / np.sqrt(HIDDEN)
        return {'x': jax.random.normal(ks[0], (B, S, DIM), dtype=jnp.float32), 'router_w': jax.random.uniform(ks[1], (DIM, E), jnp.float32, -sd, sd), 'router_b': jax.random.uniform(ks[2], (E,), jnp.float32, -sd, sd), 'w1': jax.random.uniform(ks[3], (E, DIM, 2 * HIDDEN), jnp.float32, -sd, sd), 'b1': jax.random.uniform(ks[4], (E, 2 * HIDDEN), jnp.float32, -sd, sd), 'w2': jax.random.uniform(ks[5], (E, HIDDEN, DIM), jnp.float32, -sh, sh), 'b2': jax.random.uniform(ks[6], (E, DIM), jnp.float32, -sh, sh)}
    _L0_ffn_all = _L0_ffn_setup()
    _L0_ffn_in = {k: v for k, v in _L0_ffn_all.items() if k in ('router_w', 'router_b', 'w1', 'b1', 'w2', 'b2')}
    del _L0_ffn_all
    return {'x': x, 'ctx_512': ctx_512, 'L0_attn_ln_gamma': _L0_attn_in['ln_gamma'], 'L0_attn_ln_beta': _L0_attn_in['ln_beta'], 'L0_attn_W_up': _L0_attn_in['W_up'], 'L0_attn_b_up': _L0_attn_in['b_up'], 'L0_attn_conv_w': _L0_attn_in['conv_w'], 'L0_attn_conv_b': _L0_attn_in['conv_b'], 'L0_attn_W_delta': _L0_attn_in['W_delta'], 'L0_attn_b_delta': _L0_attn_in['b_delta'], 'L0_attn_W_B': _L0_attn_in['W_B'], 'L0_attn_W_C': _L0_attn_in['W_C'], 'L0_attn_A_log': _L0_attn_in['A_log'], 'L0_attn_D': _L0_attn_in['D'], 'L0_attn_W_down': _L0_attn_in['W_down'], 'L0_attn_b_down': _L0_attn_in['b_down'], 'L0_xattn_Wq': _L0_xattn_in['Wq'], 'L0_xattn_bq': _L0_xattn_in['bq'], 'L0_xattn_Wk': _L0_xattn_in['Wk'], 'L0_xattn_bk': _L0_xattn_in['bk'], 'L0_xattn_Wv': _L0_xattn_in['Wv'], 'L0_xattn_bv': _L0_xattn_in['bv'], 'L0_xattn_Wo': _L0_xattn_in['Wo'], 'L0_xattn_bo': _L0_xattn_in['bo'], 'L0_ffn_router_w': _L0_ffn_in['router_w'], 'L0_ffn_router_b': _L0_ffn_in['router_b'], 'L0_ffn_w1': _L0_ffn_in['w1'], 'L0_ffn_b1': _L0_ffn_in['b1'], 'L0_ffn_w2': _L0_ffn_in['w2'], 'L0_ffn_b2': _L0_ffn_in['b2']}

def reference(x, ctx_512, L0_attn_ln_gamma, L0_attn_ln_beta, L0_attn_W_up, L0_attn_b_up, L0_attn_conv_w, L0_attn_conv_b, L0_attn_W_delta, L0_attn_b_delta, L0_attn_W_B, L0_attn_W_C, L0_attn_A_log, L0_attn_D, L0_attn_W_down, L0_attn_b_down, L0_xattn_Wq, L0_xattn_bq, L0_xattn_Wk, L0_xattn_bk, L0_xattn_Wv, L0_xattn_bv, L0_xattn_Wo, L0_xattn_bo, L0_ffn_router_w, L0_ffn_router_b, L0_ffn_w1, L0_ffn_b1, L0_ffn_w2, L0_ffn_b2):
    import jax
    import jax.numpy as jnp

    def _L0_attn_ref(x, ln_gamma, ln_beta, W_up, b_up, conv_w, conv_b, W_delta, b_delta, W_B, W_C, A_log, D, W_down, b_down):
        import jax, jax.numpy as jnp
        import numpy as np
        B_, L_, D_RES, D_INNER, N_STATE, K_CONV = (2, 128, 128, 64, 32, 3)

        def _causal_dwconv(x, w, b):
            xt = jnp.transpose(x, (0, 2, 1))
            k = w.shape[-1]
            out = jax.lax.conv_general_dilated(xt, w, (1,), [(k - 1, 0)], feature_group_count=w.shape[0])
            return jnp.transpose(out, (0, 2, 1)) + b

        def _s6(u, W_delta, b_delta, W_B, W_C, A_log, D):
            A = -jnp.exp(A_log)
            delta = jax.nn.softplus(u @ W_delta + b_delta)
            Bm = u @ W_B
            Cm = u @ W_C

            def step(h, inputs):
                u_t, d_t, b_t, c_t = inputs
                dA = jnp.exp(d_t[..., None] * A)
                h = dA * h + (d_t * u_t)[..., None] * b_t[:, None, :]
                y = jnp.einsum('bdn,bn->bd', h, c_t)
                return (h, y)
            h0 = jnp.zeros((u.shape[0], A.shape[0], A.shape[1]), u.dtype)
            xs = (jnp.swapaxes(u, 0, 1), jnp.swapaxes(delta, 0, 1), jnp.swapaxes(Bm, 0, 1), jnp.swapaxes(Cm, 0, 1))
            _, ys = jax.lax.scan(step, h0, xs)
            return jnp.swapaxes(ys, 0, 1) + u * D
        mu = jnp.mean(x, -1, keepdims=True)
        var = jnp.mean((x - mu) ** 2, -1, keepdims=True)
        y = (x - mu) * jax.lax.rsqrt(var + 1e-05) * ln_gamma + ln_beta
        up = y @ W_up + b_up
        left, right = jnp.split(up, 2, axis=-1)
        left = jax.nn.silu(_causal_dwconv(left, conv_w, conv_b))
        left = _s6(left, W_delta, b_delta, W_B, W_C, A_log, D)
        gated = left * jax.nn.silu(right)
        return x + gated @ W_down + b_down

    def _L0_xattn_ref(q, k, v, Wq, bq, Wk, bk, Wv, bv, Wo, bo):
        import jax, jax.numpy as jnp
        import numpy as np
        HEADS = 16
        D_MODEL = 128
        IMG_MODEL = 64
        D_K = D_MODEL // HEADS
        B, LQ, _ = q.shape
        LKV = k.shape[1]
        qh = (q @ Wq + bq).reshape(B, LQ, HEADS, D_K).transpose(0, 2, 1, 3)
        kh = (k @ Wk + bk).reshape(B, LKV, HEADS, D_K).transpose(0, 2, 1, 3)
        vh = (v @ Wv + bv).reshape(B, LKV, HEADS, D_K).transpose(0, 2, 1, 3)
        scale = 1.0 / np.sqrt(D_K)
        scores = jnp.einsum('bhqd,bhkd->bhqk', qh, kh) * scale
        attn = jax.nn.softmax(scores, axis=-1)
        out = jnp.einsum('bhqk,bhkd->bhqd', attn, vh)
        concat = out.transpose(0, 2, 1, 3).reshape(B, LQ, D_MODEL)
        return concat @ Wo + bo

    def _L0_ffn_ref(x, router_w, router_b, w1, b1, w2, b2):
        import jax, jax.numpy as jnp
        import numpy as np
        DIM = 128
        HIDDEN = 512
        E = 8
        B, S = (2, 512)
        logits = jnp.einsum('bsd,de->bse', x, router_w) + router_b
        probs = jax.nn.softmax(logits, axis=-1)
        top1 = jnp.argmax(probs, axis=-1)
        out = jnp.zeros_like(x)
        for i in range(E):
            h = jnp.einsum('bsd,df->bsf', x, w1[i]) + b1[i]
            a, g = jnp.split(h, 2, axis=-1)
            y = jnp.einsum('bsh,hd->bsd', a * jax.nn.sigmoid(g), w2[i]) + b2[i]
            out = out + jnp.where((top1 == i)[..., None], y, 0.0)
        return out
    x = _layernorm(x + _L0_attn_ref(x, L0_attn_ln_gamma, L0_attn_ln_beta, L0_attn_W_up, L0_attn_b_up, L0_attn_conv_w, L0_attn_conv_b, L0_attn_W_delta, L0_attn_b_delta, L0_attn_W_B, L0_attn_W_C, L0_attn_A_log, L0_attn_D, L0_attn_W_down, L0_attn_b_down), axis=-1)
    x = _layernorm(x + _L0_xattn_ref(x, ctx_512, ctx_512, L0_xattn_Wq, L0_xattn_bq, L0_xattn_Wk, L0_xattn_bk, L0_xattn_Wv, L0_xattn_bv, L0_xattn_Wo, L0_xattn_bo), axis=-1)
    x = _layernorm(x + _L0_ffn_ref(x, L0_ffn_router_w, L0_ffn_router_b, L0_ffn_w1, L0_ffn_b1, L0_ffn_w2, L0_ffn_b2), axis=-1)
    return x

_drawn_inputs = setup_inputs


def setup_inputs(seed=0):
    import zlib

    import numpy as np

    out = dict(_drawn_inputs(seed))
    spreads = {'L0_attn_ln_gamma': (1.0, 0.6),
     'L0_attn_ln_beta': (0.0, 0.8),
     'L0_attn_b_up': (0.0, 0.8),
     'L0_attn_conv_b': (0.0, 0.8),
     'L0_attn_b_delta': (-4.0, 0.6),
     'L0_attn_D': (1.0, 0.6),
     'L0_attn_b_down': (0.0, 0.1),
     'L0_xattn_bq': (0.0, 0.1),
     'L0_xattn_bk': (0.0, 0.8),
     'L0_xattn_bv': (0.0, 0.1),
     'L0_xattn_bo': (0.0, 0.1)}
    factors = {'L0_attn_W_up': 8.0,
     'L0_attn_conv_w': 8.0,
     'L0_attn_W_delta': 8.0,
     'L0_attn_W_B': 8.0,
     'L0_attn_W_C': 8.0,
     'L0_attn_A_log': 8.0,
     'L0_attn_W_down': 8.0,
     'L0_ffn_b1': 3.717}
    for name, (base, spread) in spreads.items():
        noise = np.random.default_rng([zlib.crc32(name.encode()), seed]).standard_normal(out[name].shape)
        drawn = base * np.exp(spread * noise) if base else spread * noise
        out[name] = jnp.asarray(drawn.astype(out[name].dtype))
    for name, factor in factors.items():
        out[name] = (out[name] * factor).astype(out[name].dtype)
    return out
```

```python
import concourse.bass as bass
from concourse import mybir
from contextlib import ExitStack

F32 = mybir.dt.float32
F32R = mybir.dt.float32r
I32 = mybir.dt.int32
ALU = mybir.AluOpType
ACT = mybir.ActivationFunctionType
AX = mybir.AxisListType

P = 128
NB, L, D = 16, 256, 128
NT = NB * L // P
PAD = 2
DI, NS, KC = 64, 32, 3
EPS = 1e-5
SERIES = (15, 13, 11, 9, 7, 5, 3)


def build_program(nc, a, out, stop=3):
    with ExitStack() as ctx:
        def sb(name, shape, dt=F32):
            return ctx.enter_context(nc.sbuf_tensor(name, shape, dt))

        X = sb("X", [P, PAD + NT, D])
        ident = sb("ident", [P, P])
        ones = sb("ones", [1, P])
        mamba_stage(nc, a, X, ident, ones)
        if stop == 1:
            dump(nc, X, out)
            return
        attention_stage(nc, a, X, ident)
        if stop == 2:
            dump(nc, X, out)
            return
        experts_stage(nc, a, X, ident, ones, out)


def tokens(ap):
    return ap.rearrange("b (h p) d -> p (b h) d", p=P)


def dump(nc, X, out):
    with ExitStack() as ctx:
        dumped = ctx.enter_context(nc.semaphore("dumped"))
        block = ctx.enter_context(nc.Block())

        @block.sync
        def _(sp):
            sp.dma_start(tokens(out), X[:, PAD:, :]).then_inc(dumped, 16)
            sp.wait_ge(dumped, 16)


def variance(dve, st, mom, mean, ve, step, base, ready):
    dve.tensor_tensor(out=mom[:, 0, :], in0=st[:, :, 1], in1=st[:, :, 4], op=ALU.add)
    dve.tensor_tensor(out=mom[:, 1, :], in0=st[:, :, 1], in1=st[:, :, 4], op=ALU.subtract)
    dve.tensor_tensor(out=mom[:, 2, :], in0=st[:, :, 2], in1=st[:, :, 5], op=ALU.add).then_inc(step, 1)
    dve.wait_ge(step, base + 1)
    dve.tensor_scalar(mean[:, :], mom[:, 0, :], 0.5, None, ALU.mult)
    dve.tensor_tensor(out=mom[:, 3, :], in0=mom[:, 1, :], in1=mom[:, 1, :], op=ALU.mult)
    dve.tensor_scalar(mom[:, 4, :], mom[:, 2, :], 1.0 / D, EPS, ALU.mult, ALU.add).then_inc(step, 1)
    dve.wait_ge(step, base + 2)
    dve.scalar_tensor_tensor(out=ve[:, :], in0=mom[:, 3, :], scalar=0.25, in1=mom[:, 4, :],
                             op0=ALU.mult, op1=ALU.add).then_inc(ready, 1)


def newton(dve, out, v, r, t1, t2, step, base):
    dve.tensor_tensor(out=t1, in0=r, in1=r, op=ALU.mult).then_inc(step, 1)
    dve.wait_ge(step, base + 1)
    dve.tensor_tensor(out=t2, in0=t1, in1=v, op=ALU.mult).then_inc(step, 1)
    dve.wait_ge(step, base + 2)
    dve.tensor_scalar(t1, t2, -0.5, 1.5, ALU.mult, ALU.add).then_inc(step, 1)
    dve.wait_ge(step, base + 3)
    dve.tensor_tensor(out=out, in0=r, in1=t1, op=ALU.mult).then_inc(step, 1)
    dve.wait_ge(step, base + 4)


def mamba_stage(nc, a, X, ident, ones):
    PAIRS = NB // 2
    CH = 4
    NCH = NS // CH
    ND = 4 + len(SERIES)
    with ExitStack() as ctx:
        def sb(name, shape, dt=F32):
            return ctx.enter_context(nc.sbuf_tensor(name, shape, dt))

        def pb(name, shape):
            return ctx.enter_context(nc.psum_tensor(name, shape, F32))

        def sem(name):
            return ctx.enter_context(nc.semaphore(name))

        w_raw = sb("w_raw", [P, 4, DI])
        w_up = sb("w_up", [P, 4, DI])
        gam = sb("gam", [P, 1])
        bet = sb("bet", [P, 1])
        b_up = sb("b_up", [P, 2])
        b_eff = sb("b_eff", [P, 2])
        conv_w = sb("conv_w", [P, KC])
        conv_b = sb("conv_b", [P, 1])
        b_dl = sb("b_dl", [P, 1])
        d_skip = sb("d_skip", [P, 1])
        a_log = sb("a_log", [P, NS])
        a_exp = sb("a_exp", [P, NS])
        a_neg = sb("a_neg", [P, NS])
        w_dl = sb("w_dl", [P, P])
        w_bc = sb("w_bc", [P, 2, 2, 2, NS])
        w_dn = sb("w_dn", [P, 2, D])
        bd_row = sb("bd_row", [1, 4, D])
        pick0 = sb("pick0", [P, NS, P])
        pick = sb("pick", [P, NS, P], F32R)
        lo_rows = sb("lo_rows", [P, 1])
        stats = sb("stats", [P, NT, 6])
        mom = sb("mom", [P, 5, NT])
        mean = sb("mean", [P, NT])
        ve = sb("ve", [P, NT])
        lnv = sb("lnv", [P, NT])
        r0 = sb("r0", [P, NT])
        r1 = sb("r1", [P, NT])
        rstd = sb("rstd", [P, NT])
        y4 = sb("y4", [P, 4, D])
        yT = sb("yT", [P, 4 * P])
        left = sb("left", [P, L + KC - 1])
        right = sb("right", [P, L])
        c1 = sb("c1", [P, L])
        c2 = sb("c2", [P, L])
        c3 = sb("c3", [P, L])
        e_c = sb("e_c", [P, L])
        e_c1 = sb("e_c1", [P, L])
        s_c = sb("s_c", [P, L])
        u = sb("u", [P, L])
        e_r = sb("e_r", [P, L])
        e_r1 = sb("e_r1", [P, L])
        s_r = sb("s_r", [P, L])
        gate = sb("gate", [P, L])
        z = sb("z", [P, L])
        nz = sb("nz", [P, L])
        e_z = sb("e_z", [P, L])
        w_z = sb("w_z", [P, L])
        w_m = sb("w_m", [P, L])
        s_z = sb("s_z", [P, L])
        s2 = sb("s2", [P, L])
        pz = sb("pz", [P, 2, L])
        q_z = sb("q_z", [P, L])
        delta = sb("delta", [P, L])
        du = sb("du", [P, L])
        bc_hi = sb("bc_hi", [P, 2 * L], F32R)
        bc = sb("bc", [P, 2, L], F32R)
        dA = sb("dA", [P, 2, CH, L])
        dB = sb("dB", [P, CH, L])
        h = sb("h", [P, CH, L])
        hC = sb("hC", [P, 2, CH, L])
        y2 = sb("y2", [P, L])
        gated = sb("gated", [P, L])
        xn = sb("xn", [P, 4, D])
        st2 = sb("st2", [P, 4, 6])
        mom2 = sb("mom2", [P, 5, 4])
        mean2 = sb("mean2", [P, 4])
        ve2 = sb("ve2", [P, 4])
        lnv2 = sb("lnv2", [P, 4])
        rr = sb("rr", [P, 3, 4])
        rstd2 = sb("rstd2", [P, 4])

        ps_t = pb("ps_t", [P, 512])
        ps_up = pb("ps_up", [P, 512])
        ps_zy = pb("ps_zy", [P, 512])
        ps_bc = pb("ps_bc", [P, 512])
        ps_b = pb("ps_b", [P, CH, L])
        ps_c = pb("ps_c", [P, CH, L])

        names = ("zeroed set_done bd_done x_in w_in w_in2 id_done pick_done pick_r w_scaled beta_ps beta_add a_done a_ready "
                 "small rs_ln rs_exp y_ready yt_ps yt_sb up_ps up_sb conv conv_exp right_exp usteps rsteps s_ready u_ready z_ps bc_ps "
                 "zsteps nz_ready z_exp z_ln bc_ready dsteps delta_ready du_ready b_ps c_ps db_done "
                 "da_ready scanned hc_done n_summed y_ps gsteps gated_ready o_ps xn_steps ve_ready ve_ln r_ready x_done").split()
        S = {n: sem("m_" + n) for n in names}
        block = ctx.enter_context(nc.Block())
        N_IN = 21

        @block.sync
        def _(sp):
            sp.dma_start(X[:, PAD:, :], tokens(a["x"])).then_inc(S["x_in"], 16)
            n = 0
            W = a["L0_attn_W_up"]
            col = lambda v: v.rearrange("(p o) -> p o", o=1)
            for dst, src in (
                (w_raw[:, 0, :], W[:, 0:DI]), (w_raw[:, 1, :], W[:, 0:DI]),
                (w_raw[:, 2, :], W[:, DI:2 * DI]), (w_raw[:, 3, :], W[:, DI:2 * DI]),
                (gam[:, :], col(a["L0_attn_ln_gamma"])), (bet[:, :], col(a["L0_attn_ln_beta"])),
            ):
                sp.dma_start(dst, src).then_inc(S["w_in"], 16)
                n += 1
            for k in range(2):
                rows = slice(DI * k, DI * k + DI)
                for dst, src in (
                    (b_up[rows, 0:1], col(a["L0_attn_b_up"][0:DI])),
                    (b_up[rows, 1:2], col(a["L0_attn_b_up"][DI:2 * DI])),
                    (conv_w[rows, :], a["L0_attn_conv_w"].rearrange("d o k -> d (o k)")),
                    (conv_b[rows, :], col(a["L0_attn_conv_b"])),
                    (b_dl[rows, :], col(a["L0_attn_b_delta"])),
                    (d_skip[rows, :], col(a["L0_attn_D"])),
                    (a_log[rows, :], a["L0_attn_A_log"]),
                ):
                    sp.dma_start(dst, src).then_inc(S["w_in"], 16)
                    n += 1
            sp.dma_start(bd_row[:, 0, :], a["L0_attn_b_down"].rearrange("(o d) -> o d", o=1)).then_inc(S["w_in"], 16)
            n += 1
            assert n == N_IN
            sp.wait_ge(S["zeroed"], 4)
            for k in range(2):
                rows = slice(DI * k, DI * k + DI)
                sp.dma_start(w_dl[rows, DI * k:DI * k + DI], a["L0_attn_W_delta"]).then_inc(S["w_in2"], 16)
                sp.dma_start(w_dn[rows, k, :], a["L0_attn_W_down"]).then_inc(S["w_in2"], 16)
                for s, w in enumerate((a["L0_attn_W_B"], a["L0_attn_W_C"])):
                    for part in range(2):
                        sp.dma_start(w_bc[rows, s, part, k, :], w).then_inc(S["w_in2"], 16)
        N_IN2 = 12

        @block.gpsimd
        def _(pool):
            for n, m in enumerate((w_dl[:, :], w_dn[:, :, :], w_bc[:, :, :, :, :], ident[:, :], pick0[:, :, :])):
                if n:
                    pool.wait_ge(S["zeroed"], n)
                pool.memset(m, 0.0).then_inc(S["zeroed"], 1)
            pool.wait_ge(S["zeroed"], 5)
            pool.affine_select(out=ident[:, :], in_=ident[:, :], compare_op=ALU.not_equal, fill=1.0,
                               base=0, pattern=[[-1, P]], channel_multiplier=1).then_inc(S["id_done"], 1)
            pool.wait_ge(S["id_done"], 1)
            for q in range(4):
                v = pick0[NS * q:NS * q + NS, :, DI * (q % 2):DI * (q % 2) + DI]
                pool.affine_select(out=v, in_=v, compare_op=ALU.not_equal, fill=1.0, base=0,
                                   pattern=[[-1, NS], [0, DI]], channel_multiplier=1).then_inc(S["pick_done"], 1)
                pool.wait_ge(S["pick_done"], q + 1)
            pool.tensor_copy(pick[:, :, :], pick0[:, :, :]).then_inc(S["pick_r"], 1)


        @block.tensor
        def _(pe):
            pe.wait_ge(S["w_in"], 16 * N_IN)
            for s in range(2):
                last = pe.matmul(ps_up[:, s:s + 1], w_raw[:, 2 * s:2 * s + 2, :].rearrange("p k c -> p (k c)"), bet[:, :],
                                 start=True, stop=True)
            last.then_inc(S["beta_ps"], 1)
            pe.wait_ge(S["id_done"], 1)
            pe.wait_ge(S["w_in2"], 16 * N_IN2)
            pe.wait_ge(S["w_scaled"], 1)
            pe.wait_ge(S["set_done"], 1)
            pe.wait_ge(S["beta_add"], 1)
            pe.wait_ge(S["pick_r"], 1)
            pe.wait_ge(S["bd_done"], 1)
            with pe.Fori(0, PAIRS) as j:
                pe.wait_ge(S["y_ready"], j * 4 + 4)
                for t in range(4):
                    last = pe.transpose(ps_t[:, t * P:(t + 1) * P], y4[:, t, :], ident[:, :])
                last.then_inc(S["yt_ps"], 1)
                pe.wait_ge(S["yt_sb"], j + 1)
                for s in range(2):
                    for k in range(2):
                        last = pe.matmul(ps_up[DI * k:DI * k + DI, L * s:L * s + L], w_up[:, 2 * s + k, :],
                                         yT[:, L * k:L * k + L], start=True, stop=True)
                last.then_inc(S["up_ps"], 1)
                pe.wait_ge(S["u_ready"], j + 1)
                pe.matmul(ps_zy[:, 0:L], w_dl[:, :], u[:, :], start=True, stop=True).then_inc(S["z_ps"], 1)
                for s in range(2):
                    last = pe.matmul(ps_bc[:, L * s:L * s + L],
                                     w_bc[:, s, :, :, :].rearrange("p a b n -> p (a b n)"), u[:, :],
                                     start=True, stop=True)
                last.then_inc(S["bc_ps"], 1)
                pe.wait_ge(S["bc_ready"], j + 1)

                def spread(s, ps, c, done):
                    for n in range(CH):
                        last = pe.matmul(ps[:, n, :], pick[:, c * CH + n, :], bc[:, s, :], start=True, stop=True)
                    last.then_inc(S[done], 1)

                spread(0, ps_b, 0, "b_ps")
                spread(1, ps_c, 0, "c_ps")
                for c in range(NCH):
                    if c < NCH - 1:
                        pe.wait_ge(S["db_done"], j * NCH + c + 1)
                        spread(0, ps_b, c + 1, "b_ps")
                    pe.wait_ge(S["hc_done"], j * NCH + c + 1)
                    if c < NCH - 1:
                        spread(1, ps_c, c + 1, "c_ps")
                    for n in range(CH):
                        last = pe.matmul(ps_zy[:, L:2 * L], ident[:, :], hC[:, c % 2, n, :],
                                         start=(c == 0 and n == 0), stop=(c == NCH - 1 and n == CH - 1))
                    last.then_inc(S["n_summed"], 1)
                pe.matmul(ps_t[:, :], ones[0:1, :], bd_row[0:1, :, :].rearrange("o t d -> o (t d)"), start=True, stop=False, skip_group_check=True)
                pe.wait_ge(S["gated_ready"], j + 1)
                for t in range(4):
                    last = pe.matmul(ps_t[:, t * D:(t + 1) * D], gated[:, (t % 2) * P:(t % 2) * P + P], w_dn[:, t // 2, :],
                                     start=False, stop=True, skip_group_check=True)
                last.then_inc(S["o_ps"], 1)

        @block.scalar
        def _(act):
            act.preload_act_table_set("natural_log_exp_and_others")
            act.wait_ge(S["w_in"], 16 * N_IN)
            act.activation(a_exp[:, :], a_log[:, :], ACT.Exp).then_inc(S["a_done"], 1)
            act.wait_ge(S["ve_ready"], 1)
            act.activation(lnv[:, :], ve[:, :], ACT.Ln).then_inc(S["rs_ln"], 1)
            act.wait_ge(S["rs_ln"], 1)
            act.activation(r0[:, :], lnv[:, :], ACT.Exp, scale=-0.5).then_inc(S["rs_exp"], 1)
            act.wait_ge(S["beta_add"], 1)
            act.wait_ge(S["a_ready"], 1)
            act.wait_ge(S["set_done"], 1)
            with act.Fori(0, PAIRS) as j:
                act.wait_ge(S["yt_ps"], j + 1)
                act.activation(yT[:, :], ps_t[:, :], ACT.Copy).then_inc(S["yt_sb"], 1)
                act.wait_ge(S["up_ps"], j + 1)
                act.activation(left[:, KC - 1:], ps_up[:, 0:L], ACT.Identity, bias=b_eff[:, 0:1]).then_inc(S["up_sb"], 1)
                act.activation(right[:, :], ps_up[:, L:2 * L], ACT.Identity, bias=b_eff[:, 1:2]).then_inc(S["up_sb"], 1)
                act.wait_ge(S["conv"], j * 3 + 3)
                act.activation(e_c[:, :], c3[:, :], ACT.Exp, scale=-1.0).then_inc(S["conv_exp"], 1)
                act.wait_ge(S["up_sb"], j * 2 + 2)
                act.activation(e_r[:, :], right[:, :], ACT.Exp, scale=-1.0).then_inc(S["right_exp"], 1)
                act.wait_ge(S["nz_ready"], j * 2 + 2)
                act.activation(e_z[:, :], nz[:, :], ACT.Exp).then_inc(S["z_exp"], 1)
                act.wait_ge(S["delta_ready"], j + 1)
                for c in range(NCH):
                    if c >= 2:
                        act.wait_ge(S["scanned"], j * NCH + c - 1)
                    for n in range(CH):
                        k = c * CH + n
                        last = act.activation(dA[:, c % 2, n, 1:], delta[:, 1:], ACT.Exp, scale=a_neg[:, k:k + 1])
                    last.then_inc(S["da_ready"], 1)
                act.wait_ge(S["ve_ready"], j + 2)
                act.activation(lnv2[:, :], ve2[:, :], ACT.Ln).then_inc(S["ve_ln"], 1)
                act.wait_ge(S["ve_ln"], j + 1)
                act.activation(rr[:, 0, :], lnv2[:, :], ACT.Exp, scale=-0.5).then_inc(S["r_ready"], 1)

        @block.vector
        def _(dve):
            dve.memset(dA[:, :, :, 0:1], 0.0)
            dve.memset(left[:, 0:KC - 1], 0.0)
            dve.memset(ones[:, :], 1.0)
            dve.memset(lo_rows[0:DI, :], 0.0)
            dve.memset(lo_rows[DI:P, :], -1.0).then_inc(S["set_done"], 1)
            dve.wait_ge(S["x_in"], 16)
            for t in range(NT):
                last = dve.bn_stats(stats[:, t, :], X[:, PAD + t, :])
            last.then_inc(S["small"], 1)
            dve.wait_ge(S["small"], 1)
            variance(dve, stats, mom, mean, ve, S["small"], 1, S["ve_ready"])
            dve.wait_ge(S["w_in"], 16 * N_IN)
            dve.tensor_scalar(w_up[:, :, :], w_raw[:, :, :], gam[:, 0:1], None, ALU.mult).then_inc(S["w_scaled"], 1)
            for t in range(1, 4):
                last = dve.tensor_copy(bd_row[:, t, :], bd_row[:, 0, :])
            last.then_inc(S["bd_done"], 1)
            dve.wait_ge(S["beta_ps"], 1)
            dve.tensor_tensor(out=b_eff[:, :], in0=ps_up[:, 0:2], in1=b_up[:, :], op=ALU.add).then_inc(S["beta_add"], 1)
            dve.wait_ge(S["a_done"], 1)
            dve.tensor_scalar(a_neg[:, :], a_exp[:, :], -1.0, None, ALU.mult).then_inc(S["a_ready"], 1)
            dve.wait_ge(S["rs_exp"], 1)
            newton(dve, rstd[:, :], ve[:, :], r0[:, :], r1[:, :], lnv[:, :], S["small"], 3)
            with dve.Fori(0, PAIRS) as j:
                for t in range(4):
                    dve.tensor_scalar(y4[:, t, :], X[:, j * 4 + t + PAD, :], mean[:, bass.ds(j * 4 + t, 1)], rstd[:, bass.ds(j * 4 + t, 1)],
                                      ALU.subtract, ALU.mult).then_inc(S["y_ready"], 1)
                dve.wait_ge(S["up_sb"], j * 2 + 1)
                dve.tensor_scalar(c1[:, :], left[:, 2:2 + L], conv_w[:, 2:3], conv_b[:, 0:1], ALU.mult, ALU.add).then_inc(S["conv"], 1)
                dve.wait_ge(S["conv"], j * 3 + 1)
                dve.scalar_tensor_tensor(out=c2[:, :], in0=left[:, 1:1 + L], scalar=conv_w[:, 1:2], in1=c1[:, :],
                                         op0=ALU.mult, op1=ALU.add).then_inc(S["conv"], 1)
                dve.wait_ge(S["conv"], j * 3 + 2)
                dve.scalar_tensor_tensor(out=c3[:, :], in0=left[:, 0:L], scalar=conv_w[:, 0:1], in1=c2[:, :],
                                         op0=ALU.mult, op1=ALU.add).then_inc(S["conv"], 1)
                dve.wait_ge(S["conv_exp"], j + 1)
                dve.tensor_scalar(e_c1[:, :], e_c[:, :], 1.0, None, ALU.add).then_inc(S["usteps"], 1)
                dve.wait_ge(S["usteps"], j * 2 + 1)
                dve.reciprocal(s_c[:, :], e_c1[:, :]).then_inc(S["usteps"], 1)
                dve.wait_ge(S["usteps"], j * 2 + 2)
                dve.tensor_tensor(out=u[:, :], in0=c3[:, :], in1=s_c[:, :], op=ALU.mult).then_inc(S["u_ready"], 1)
                dve.wait_ge(S["z_ps"], j + 1)
                dve.tensor_scalar(z[:, :], ps_zy[:, 0:L], b_dl[:, 0:1], None, ALU.add).then_inc(S["nz_ready"], 1)
                dve.wait_ge(S["nz_ready"], j * 2 + 1)
                dve.scalar_tensor_tensor(out=nz[:, :], in0=z[:, :], scalar=-1.0, in1=z[:, :],
                                         op0=ALU.mult, op1=ALU.min).then_inc(S["nz_ready"], 1)
                dve.wait_ge(S["bc_ps"], j + 1)
                dve.tensor_copy(bc_hi[:, :], ps_bc[:, :]).then_inc(S["zsteps"], 1)
                dve.wait_ge(S["zsteps"], j + 1)
                dve.scalar_tensor_tensor(out=bc[:, :, :].rearrange("p s l -> p (s l)"), in0=bc_hi[:, :].bitcast(F32), scalar=lo_rows[:, 0:1],
                                         in1=ps_bc[:, :], op0=ALU.mult, op1=ALU.add).then_inc(S["bc_ready"], 1)
                dve.wait_ge(S["right_exp"], j + 1)
                dve.tensor_scalar(e_r1[:, :], e_r[:, :], 1.0, None, ALU.add).then_inc(S["gsteps"], 1)
                dve.wait_ge(S["gsteps"], j * 4 + 1)
                dve.reciprocal(s_r[:, :], e_r1[:, :]).then_inc(S["gsteps"], 1)
                dve.wait_ge(S["gsteps"], j * 4 + 2)
                dve.tensor_tensor(out=gate[:, :], in0=right[:, :], in1=s_r[:, :], op=ALU.mult).then_inc(S["gsteps"], 1)
                dve.wait_ge(S["z_exp"], j + 1)
                dve.tensor_scalar(w_z[:, :], e_z[:, :], 2.0, None, ALU.add).then_inc(S["dsteps"], 1)
                dve.wait_ge(S["dsteps"], j * ND + 1)
                dve.reciprocal(s_r[:, :], w_z[:, :]).then_inc(S["rsteps"], 1)
                dve.wait_ge(S["rsteps"], j + 1)
                dve.tensor_tensor(out=s_z[:, :], in0=e_z[:, :], in1=s_r[:, :], op=ALU.mult).then_inc(S["s_ready"], 1)
                dve.wait_ge(S["s_ready"], j + 1)
                dve.tensor_tensor(out=s2[:, :], in0=s_z[:, :], in1=s_z[:, :], op=ALU.mult).then_inc(S["dsteps"], 1)
                dve.wait_ge(S["dsteps"], j * ND + 2)
                dve.tensor_scalar(pz[:, 0, :], s2[:, :], 1.0 / SERIES[0], None, ALU.mult).then_inc(S["dsteps"], 1)
                for k, odd in enumerate(SERIES[1:]):
                    dve.wait_ge(S["dsteps"], j * ND + 3 + k)
                    dve.scalar_tensor_tensor(out=pz[:, (k + 1) % 2, :], in0=pz[:, k % 2, :], scalar=1.0 / odd, in1=s2[:, :],
                                             op0=ALU.add, op1=ALU.mult).then_inc(S["dsteps"], 1)
                dve.wait_ge(S["dsteps"], j * ND + 2 + len(SERIES))
                dve.scalar_tensor_tensor(out=w_m[:, :], in0=pz[:, (len(SERIES) - 1) % 2, :], scalar=1.0, in1=s_z[:, :],
                                         op0=ALU.add, op1=ALU.mult).then_inc(S["dsteps"], 1)
                dve.wait_ge(S["dsteps"], j * ND + ND - 1)
                dve.tensor_scalar(q_z[:, :], w_m[:, :], 2.0, None, ALU.mult).then_inc(S["dsteps"], 1)
                dve.wait_ge(S["dsteps"], j * ND + ND)
                dve.scalar_tensor_tensor(out=delta[:, :], in0=z[:, :], scalar=0.0, in1=q_z[:, :],
                                         op0=ALU.max, op1=ALU.add).then_inc(S["delta_ready"], 1)
                dve.wait_ge(S["delta_ready"], j + 1)
                dve.tensor_tensor(out=du[:, :], in0=delta[:, :], in1=u[:, :], op=ALU.mult).then_inc(S["du_ready"], 1)
                dve.wait_ge(S["du_ready"], j + 1)
                du_b = du[:, :].unsqueeze(1).to_broadcast([P, CH, L])
                for c in range(NCH):
                    dve.wait_ge(S["b_ps"], j * NCH + c + 1)
                    dve.tensor_tensor(out=dB[:, :, :], in0=du_b, in1=ps_b[:, :, :], op=ALU.mult).then_inc(S["db_done"], 1)
                    dve.wait_ge(S["da_ready"], j * NCH + c + 1)
                    dve.wait_ge(S["db_done"], j * NCH + c + 1)
                    dve.tensor_tensor_scan(h[:, :, :].rearrange("p n l -> p (n l)"), dA[:, c % 2, :, :].rearrange("p n l -> p (n l)"),
                                           dB[:, :, :].rearrange("p n l -> p (n l)"), 0.0, ALU.mult, ALU.add).then_inc(S["scanned"], 1)
                    dve.wait_ge(S["c_ps"], j * NCH + c + 1)
                    dve.wait_ge(S["scanned"], j * NCH + c + 1)
                    if c >= 2:
                        dve.wait_ge(S["n_summed"], j * NCH + c - 1)
                    dve.tensor_tensor(out=hC[:, c % 2, :, :], in0=h[:, :, :], in1=ps_c[:, :, :], op=ALU.mult).then_inc(S["hc_done"], 1)
                dve.wait_ge(S["n_summed"], j * NCH + NCH)
                dve.scalar_tensor_tensor(out=y2[:, :], in0=u[:, :], scalar=d_skip[:, 0:1], in1=ps_zy[:, L:2 * L],
                                         op0=ALU.mult, op1=ALU.add).then_inc(S["gsteps"], 1)
                dve.wait_ge(S["gsteps"], j * 4 + 4)
                dve.tensor_tensor(out=gated[:, :], in0=y2[:, :], in1=gate[:, :], op=ALU.mult).then_inc(S["gated_ready"], 1)
                dve.wait_ge(S["o_ps"], j + 1)
                dve.scalar_tensor_tensor(out=xn[:, :, :].rearrange("p t d -> p (t d)"), in0=X[:, bass.ds(j * 4 + PAD, 4), :].rearrange("p t d -> p (t d)"), scalar=2.0,
                                         in1=ps_t[:, :], op0=ALU.mult, op1=ALU.add).then_inc(S["xn_steps"], 1)
                dve.wait_ge(S["xn_steps"], j * 8 + 1)
                for t in range(4):
                    last = dve.bn_stats(st2[:, t, :], xn[:, t, :])
                last.then_inc(S["xn_steps"], 1)
                dve.wait_ge(S["xn_steps"], j * 8 + 2)
                variance(dve, st2, mom2, mean2, ve2, S["xn_steps"], j * 8 + 2, S["ve_ready"])
                dve.wait_ge(S["r_ready"], j + 1)
                newton(dve, rstd2[:, :], ve2[:, :], rr[:, 0, :], rr[:, 1, :], rr[:, 2, :], S["xn_steps"], j * 8 + 4)
                for t in range(4):
                    last = dve.tensor_scalar(X[:, j * 4 + t + PAD, :], xn[:, t, :], mean2[:, t:t + 1], rstd2[:, t:t + 1],
                                             ALU.subtract, ALU.mult)
                last.then_inc(S["x_done"], 1)


H, DK = 16, 8
LK, DC = 1601, 64
KT = -(-LK // P)
KR = LK - (KT - 1) * P
HG, G4 = 4, H // 4
STEPS = G4 * KT
UNITS = 32
BUNITS = G4 * UNITS
AHEAD = UNITS + 7
QUARTER = [(0, 400), (400, 400), (800, 400), (LK - 402, 402)]
KCH = [(c * 512, min(512, LK - c * 512)) for c in range(4)]
SR = 3 * 32

FIRST_ROUNDS = ([("ctx", c) for c in range(4)] + [("x", 0)] + [("k", c) for c in range(4)] + [("q", 0)]
                + [("v", c) for c in range(4)] + [("max", 0)])
ROUNDS = {1: ("norm", 3), 3: ("concat", 0), 5: ("out", 0), 6: ("x", 0), 7: ("q", 0), 8: ("ctx", 0), 9: ("ctx", 1),
          10: ("max", 1), 11: ("ctx", 2), 12: ("ctx", 3), 14: ("k", 0), 15: ("k", 1), 16: ("norm", 0), 17: ("k", 2),
          18: ("k", 3), 20: ("v", 0), 21: ("v", 1), 23: ("max", 2), 24: ("v", 2), 25: ("v", 3), 28: ("norm", 1),
          36: ("max", 3), 41: ("norm", 2), 49: ("max", 4)}
ORDER = [ROUNDS[s] for s in sorted(ROUNDS)]


def first_round(kind, n):
    return FIRST_ROUNDS.index((kind, n)) + 1


def round_of(b, kind, n):
    return b * len(ORDER) + len(FIRST_ROUNDS) + ORDER.index((kind, n)) + 1


def units_at(s):
    return [AHEAD + v for v in range(BUNITS * s // STEPS, BUNITS * (s + 1) // STEPS)]


def attention_stage(nc, a, X, ident):
    with ExitStack() as ctx:
        def sb(name, shape, dt=F32):
            return ctx.enter_context(nc.sbuf_tensor(name, shape, dt))

        def pb(name, shape):
            return ctx.enter_context(nc.psum_tensor(name, shape, F32))

        wq = sb("wq", [P, P])
        wk = sb("wk", [DC, P])
        wv = sb("wv", [DC, P])
        wo = sb("wo", [P, P])
        bq = sb("bq", [P, 1])
        bk = sb("bk", [P, 1])
        bv = sb("bv", [P, P])
        bo = sb("bo", [P, D])
        keys = sb("keys", [P, KT + 1, DC])
        ctxT = sb("ctxT", [DC, LK])
        xs = sb("xs", [P, 2, D])
        xT = sb("xT", [P, L])
        kq = sb("kq", [P, LK + L])
        parts = sb("parts", [P, 2 * (LK + L)], F32R)
        k_lo, q_hi = parts[:, 0:LK], parts[:, LK:LK + L]
        k_hi, q_lo = parts[:, LK + L:2 * LK + L], parts[:, 2 * LK + L:]
        stack = sb("stack", [P, G4, LK + L], F32R)
        qblk = sb("qblk", [P, G4, HG, L], F32R)
        own = sb("own", [SR, HG, 1])
        unit_col = sb("unit_col", [P, 1])
        vn = sb("vn", [P, KT, P])
        V = sb("V", [P, KT, H, 32])
        pT = sb("pT", [P, 2, HG, L])
        mx = sb("mx", [P, 2, 2 * HG, 4])
        neg = sb("neg", [P, 2, 2 * HG])
        negT = sb("negT", [2 * HG, P], F32R)
        oS = sb("oS", [P, L])
        rden = sb("rden", [P, 2, HG])
        cc = sb("cc", [P, 2, H, DK])
        ccT = sb("ccT", [P, L])
        xa = sb("xa", [P, 2, D])
        xb = sb("xb", [P, 2, D])
        st = sb("a_st", [P, 2, 6])
        mom = sb("a_mom", [P, 5, 2])
        mean = sb("a_mean", [P, 2])
        ve = sb("a_ve", [P, 2])
        lnv = sb("a_lnv", [P, 2])
        rr = sb("a_rr", [P, 3, 2])
        rstd = sb("a_rstd", [P, 2])

        ps_s = pb("ps_s", [P, 2, HG, L])
        ps_m = pb("ps_m", [P, 2, 512])
        ps_o = pb("ps_o", [P, 2, L])
        ps_x = pb("ps_x", [P, 512])

        names = ("w_in zero_done set_done own_done scores exps pv units reduced neg_ready bank_full bank_free row_in "
                 "xs_ready parts_ready qblk_ready v_ready keys_in o_copied o_rec xa_done ln_steps ve_ready lnv_done "
                 "r_ready x_done").split()
        S = {n: ctx.enter_context(nc.semaphore("a_" + n)) for n in names}
        stack_in = [ctx.enter_context(nc.semaphore(f"a_stack_in{g}")) for g in range(G4)]
        block = ctx.enter_context(nc.Block())
        N_W = 8
        CREDIT = 2

        @block.sync
        def _(sp):
            row = lambda v: v.rearrange("(o d) -> o d", o=1)
            col = lambda v: v.rearrange("(p o) -> p o", o=1)
            for dst, src in ((wq[:, :], a["L0_xattn_Wq"]), (wk[:, :], a["L0_xattn_Wk"]), (wv[:, :], a["L0_xattn_Wv"]),
                             (wo[:, :], a["L0_xattn_Wo"]), (bq[:, :], col(a["L0_xattn_bq"])),
                             (bk[:, :], col(a["L0_xattn_bk"])),
                             (bv[:, :], row(a["L0_xattn_bv"]).to_broadcast([P, P])),
                             (bo[:, :], row(a["L0_xattn_bo"]).to_broadcast([P, D]))):
                sp.dma_start(dst, src).then_inc(S["w_in"], 16)

            def load_keys(n):
                c = a["ctx_512"][n, :, :] if isinstance(n, int) else a["ctx_512"][bass.ds(n, 1), :, :].rearrange("o k d -> (o k) d")
                sp.dma_start(keys[:, 0:KT - 1, :], c[0:(KT - 1) * P, :].rearrange("(t p) d -> p t d", p=P)).then_inc(S["keys_in"], 16)
                sp.dma_start(keys[0:KR, KT - 1, :], c[(KT - 1) * P:LK, :]).then_inc(S["keys_in"], 16)

            def fill_stack(n, g):
                stack_w = stack[:, :, :].bitcast(F32)
                rows = slice(32 * g, 32 * g + 32)
                sp.dma_start(stack_w[0:32, g, 0:LK], k_hi[rows, :].bitcast(F32)).then_inc(stack_in[g], 16)
                sp.dma_start(stack_w[0:32, g, LK:], q_hi[rows, :].bitcast(F32)).then_inc(stack_in[g], 16)
                sp.dma_start(stack_w[32:64, g, :], parts[rows, 0:LK + L].bitcast(F32)).then_inc(stack_in[g], 16)
                sp.dma_start(stack_w[64:96, g, :], parts[rows, LK + L:].bitcast(F32)).then_inc(stack_in[g], 16)

            def fill_row(rounds, g):
                sp.wait_ge(S["bank_free"], rounds)
                sp.dma_start(qblk[SR:SR + 1, g, :, :].rearrange("o h l -> o (h l)").bitcast(F32), negT[:, :].bitcast(F32)).then_inc(S["row_in"], 16)

            load_keys(0)
            sp.wait_ge(S["bank_full"], first_round("ctx", 3))
            load_keys(1)
            sp.wait_ge(S["parts_ready"], 4)
            for g in range(G4):
                fill_stack(0, g)
            fill_row(first_round("max", 0), 0)
            with sp.Fori(0, NB) as b:
                fill_row_at = lambda k: fill_row(round_of(b, "max", k), k % G4)
                fill_row_at(1)
                sp.wait_ge(S["bank_full"], round_of(b, "ctx", 3))
                load_keys(nc_mod(sp, b + 2))
                fill_row_at(2)
                sp.wait_ge(S["parts_ready"], b * 4 + 8)
                fill_stack(b + 1, 0)
                sp.wait_ge(S["scores"], b * STEPS + 2 * KT)
                fill_stack(b + 1, 1)
                fill_row_at(3)
                sp.wait_ge(S["scores"], b * STEPS + 3 * KT)
                fill_stack(b + 1, 2)
                fill_row_at(4)
                sp.wait_ge(S["scores"], b * STEPS + 4 * KT)
                fill_stack(b + 1, 3)
            for g in range(G4):
                sp.wait_ge(stack_in[g], 64 * (NB + 1))
            sp.wait_ge(S["row_in"], 16 * (G4 * NB + 1))
            sp.wait_ge(S["keys_in"], 32 * (NB + 2))

        @block.gpsimd
        def _(pool):
            pool.memset(own[:, :, :], 0.0).then_inc(S["own_done"], 1)
            pool.wait_ge(S["own_done"], 1)
            for part in range(3):
                v = own[32 * part:32 * part + 32, :, 0]
                pool.affine_select(out=v, in_=v, compare_op=ALU.is_gt, fill=1.0, base=0,
                                   pattern=[[DK, HG]], channel_multiplier=-1).then_inc(S["own_done"], 1)
                pool.wait_ge(S["own_done"], 2 + 2 * part)
                pool.affine_select(out=v, in_=v, compare_op=ALU.is_gt, fill=0.0, base=DK,
                                   pattern=[[DK, HG]], channel_multiplier=-1).then_inc(S["own_done"], 1)
                pool.wait_ge(S["own_done"], 3 + 2 * part)
            pool.wait_ge(S["set_done"], 1)

            def copy_x(n, count):
                src = X[:, PAD:PAD + 2, :] if isinstance(n, int) else X[:, bass.ds(n * 2 + PAD, 2), :]
                pool.tensor_tensor(out=xs[:, :, :], in0=src, in1=unit_col[:, 0:1].unsqueeze(2).to_broadcast([P, 2, D]),
                                   op=ALU.mult).then_inc(S["xs_ready"], 1)
                pool.wait_ge(S["xs_ready"], count)

            def split(base):
                for n, (dst, src, hi) in enumerate((
                    (k_hi, kq[:, 0:LK], None), (q_hi, kq[:, LK:], None),
                    (k_lo, kq[:, 0:LK], k_hi), (q_lo, kq[:, LK:], q_hi),
                )):
                    if hi is None:
                                pool.tensor_tensor(out=dst, in0=src, in1=unit_col[:, 0:1].to_broadcast([P, src.shape[1]]), op=ALU.mult).then_inc(S["parts_ready"], 1)
                    else:
                        pool.tensor_tensor(out=dst, in0=src, in1=hi.bitcast(F32), op=ALU.subtract).then_inc(S["parts_ready"], 1)
                    pool.wait_ge(S["parts_ready"], base + n + 1)

            def spread_q(g, count):
                pool.tensor_tensor(out=qblk[0:SR, g, :, :], in0=stack[0:SR, g, LK:].bitcast(F32).unsqueeze(1).to_broadcast([SR, HG, L]),
                                   in1=own[:, :, :].to_broadcast([SR, HG, L]), op=ALU.mult).then_inc(S["qblk_ready"], 1)
                pool.wait_ge(S["qblk_ready"], count)

            def spread_v(g, count):
                heads = slice(HG * g, HG * g + HG)
                cols = slice(32 * g, 32 * g + 32)
                b_v = bv[:, cols].rearrange("p (h d) -> p h d", d=DK)
                for t0, t1, p in ((0, KT - 1, P), (KT - 1, KT, KR)):
                    for t in range(t0, t1):
                        pool.tensor_tensor(out=V[0:p, t, heads, 0:DK], in0=vn[0:p, t, cols].rearrange("p (h d) -> p h d", d=DK),
                                           in1=b_v[0:p], op=ALU.add).then_inc(S["v_ready"], 1)
                pool.wait_ge(S["v_ready"], count)

            copy_x(0, 1)
            pool.wait_ge(S["bank_free"], first_round("q", 0))
            split(0)
            pool.wait_ge(S["bank_free"], first_round("v", 3))
            for g in range(G4):
                pool.wait_ge(stack_in[g], 64)
                spread_q(g, g + 1)
                spread_v(g, KT * (g + 1))
            with pool.Fori(0, NB) as b:
                pool.wait_ge(S["bank_full"], b * len(ORDER) + len(FIRST_ROUNDS))
                copy_x(nc_mod(pool, b + 1), b + 2)
                for g in range(G4):
                    pool.wait_ge(stack_in[g], b * 64 + 64)
                pool.wait_ge(S["bank_free"], round_of(b, "k", 3))
                split(b * 4 + 4)
                pool.wait_ge(S["bank_free"], round_of(b, "v", 3))
                for g in range(G4):
                    pool.wait_ge(stack_in[g], b * 64 + 128)
                    pool.wait_ge(S["scores"], b * STEPS + KT * (g + 1))
                    spread_q(g, b * 4 + g + 5)
                    pool.wait_ge(S["pv"], b * STEPS + KT * (g + 1) + CREDIT)
                    spread_v(g, b * (4 * KT) + KT * (g + 5))

        @block.tensor
        def _(pe):
            pe.wait_ge(S["w_in"], 16 * N_W)
            pe.wait_ge(S["set_done"], 1)
            pe.sem_inc(S["pv"], CREDIT)

            def bank_round(kind, n, rounds, b):
                if not (isinstance(rounds, int) and rounds == 1):
                    pe.wait_ge(S["bank_free"], rounds - 1)
                if kind == "ctx":
                    if n == 0:
                        pe.wait_ge(S["keys_in"], 32 if b is None else b * 32 + 64)
                    for i, t in enumerate(range(4 * n, min(4 * n + 4, KT))):
                        r = P if t < KT - 1 else KR
                        w = 1 if i else 2
                        last = pe.transpose(ps_x[0:w * DC, P * i:P * i + r], keys[0:r, t:t + w, :].rearrange("p t d -> p (t d)"), ident[0:r, 0:r])
                elif kind == "x":
                    pe.wait_ge(S["xs_ready"], 1 if b is None else b + 2)
                    for t in range(2):
                        last = pe.transpose(ps_x[:, P * t:P * t + P], xs[:, t, :], ident[:, :])
                elif kind == "k":
                    k0, w = KCH[n]
                    last = pe.matmul(ps_x[:, 0:w], wk[:, :], ctxT[:, k0:k0 + w], start=True, stop=True)
                elif kind == "q":
                    last = pe.matmul(ps_x[:, 0:L], wq[:, :], xT[:, :], start=True, stop=True)
                elif kind == "v":
                    for i, t in enumerate(range(4 * n, min(4 * n + 4, KT))):
                        r = P if t < KT - 1 else KR
                        last = pe.matmul(ps_x[0:r, P * i:P * i + P], ctxT[:, P * t:P * t + r], wv[:, :], start=True, stop=True)
                elif kind == "max":
                    pe.wait_ge(S["neg_ready"], 1 if b is None else b * G4 + n + 1)
                    last = pe.transpose(ps_x[0:2 * HG, 0:P], neg[:, n % 2, :], ident[:, :])
                elif kind == "norm":
                    pe.wait_ge(S["o_copied"], (b * G4 if n == 3 else b * G4 + n + 1) + CREDIT)
                    for t in range(2):
                        last = pe.transpose(ps_x[:, P * t:P * t + P], oS[:, P * t:P * t + P], ident[:, :])
                elif kind == "concat":
                    for t in range(2):
                        last = pe.transpose(ps_x[:, P * t:P * t + P], cc[:, t, :, :].rearrange("p h d -> p (h d)"), ident[:, :])
                elif kind == "out":
                    for t in range(2):
                        last = pe.matmul(ps_x[:, D * t:D * t + D], ccT[:, P * t:P * t + P], wo[:, :], start=True, stop=True)
                last.then_inc(S["bank_full"], 1)

            def unit(w, b):
                g, u = w // UNITS % G4, w % UNITS
                head, tile, quarter = u // 8, u // 4 % 2, u % 4
                k0, cols = QUARTER[quarter]
                if u == 0:
                    pe.wait_ge(S["qblk_ready"], b * G4 + w // UNITS + 1)
                pe.wait_ge(S["reduced"], b * BUNITS + w + 1)
                pe.matmul(ps_m[:, w % 2, 0:cols], qblk[0:SR, g, head, P * tile:P * tile + P], stack[0:SR, g, k0:k0 + cols],
                          start=True, stop=True).then_inc(S["units"], 1)

            def attend(b, g, kt):
                s = KT * g + kt
                r = P if kt < KT - 1 else KR
                if kt == 0:
                    pe.wait_ge(S["v_ready"], b * (4 * KT) + KT * (g + 1))
                    pe.wait_ge(S["o_copied"], b * G4 + g + CREDIT)
                pe.wait_ge(S["exps"], b * STEPS + s + 1 + CREDIT)
                for h in range(HG):
                    last = pe.matmul(ps_o[32 * h:32 * h + 32, g % 2, :], V[0:r, kt, HG * g + h, :], pT[0:r, s % 2, h, :],
                                     start=(kt == 0), stop=(kt == KT - 1))
                last.then_inc(S["pv"], 1)

            for kind, n in FIRST_ROUNDS[:-1]:
                bank_round(kind, n, first_round(kind, n), None)
            for w in range(AHEAD):
                unit(w, 0)
                if w == UNITS:
                    bank_round("max", 0, first_round("max", 0), None)
            with pe.Fori(0, NB) as b:
                for s in range(STEPS):
                    g, kt = s // KT, s % KT
                    r = P if kt < KT - 1 else KR
                    if kt == 0:
                        pe.wait_ge(S["row_in"], b * (16 * G4) + 16 * (g + 1))
                    pe.wait_ge(S["exps"], b * STEPS + s + 1)
                    todo = units_at(s)
                    for i in range(2):
                        last = pe.matmul(ps_s[0:r, s % 2, 2 * i:2 * i + 2, :], stack[0:SR + 1, g, P * kt:P * kt + r],
                                         qblk[0:SR + 1, g, 2 * i:2 * i + 2, :], start=True, stop=True)
                        if i:
                            last.then_inc(S["scores"], 1)
                        if todo:
                            unit(todo.pop(0), b)
                    if s:
                        attend(b, (s - 1) // KT, (s - 1) % KT)
                    for w in todo:
                        unit(w, b)
                    if s in ROUNDS:
                        kind, n = ROUNDS[s]
                        bank_round(kind, n, round_of(b, kind, n), b)
                attend(b, G4 - 1, KT - 1)
            for kind, n in ORDER[:3]:
                bank_round(kind, n, round_of(NB, kind, n), NB)

        @block.scalar
        def _(act):
            act.preload_act_table_set("natural_log_exp_and_others")
            act.wait_ge(S["w_in"], 16 * N_W)
            act.wait_ge(S["set_done"], 1)
            act.sem_inc(S["exps"], CREDIT)
            act.sem_inc(S["o_copied"], CREDIT)

            def drain(kind, n, rounds, b):
                if kind not in ("ctx", "x", "k", "q", "v", "concat"):
                    return
                if kind == "v" and n == 0 and b is not None:
                    act.wait_ge(S["v_ready"], b * (4 * KT) + 4 * KT)
                act.wait_ge(S["bank_full"], rounds)
                if kind == "ctx":
                    k0, w = KCH[n]
                    last = act.activation(ctxT[:, k0:k0 + w], ps_x[0:DC, 0:w], ACT.Copy)
                elif kind == "x":
                    last = act.activation(xT[:, :], ps_x[:, 0:L], ACT.Copy)
                elif kind == "k":
                    k0, w = KCH[n]
                    last = act.activation(kq[:, k0:k0 + w], ps_x[:, 0:w], ACT.Identity, bias=bk[:, 0:1])
                elif kind == "q":
                    last = act.activation(kq[:, LK:], ps_x[:, 0:L], ACT.Identity, bias=bq[:, 0:1])
                elif kind == "v":
                    if n < 3:
                        last = act.activation(vn[:, 4 * n:4 * n + 4, :].rearrange("p t c -> p (t c)"), ps_x[:, :], ACT.Copy)
                    else:
                        last = act.activation(vn[0:KR, KT - 1, :], ps_x[0:KR, 0:P], ACT.Copy)
                elif kind == "concat":
                    last = act.activation(ccT[:, :], ps_x[:, 0:L], ACT.Copy)
                last.then_inc(S["bank_free"], 1)

            def copy_o(b, g):
                act.wait_ge(S["pv"], b * STEPS + KT * (g + 1) + CREDIT)
                act.wait_ge(S["bank_full"], round_of(b, "out", 0) if g == 0 else round_of(b, "norm", g - 1))
                act.activation(oS[:, :], ps_o[:, g % 2, :], ACT.Copy).then_inc(S["o_copied"], 1)

            def root(b):
                act.wait_ge(S["ve_ready"], b + 1)
                act.activation(lnv[:, :], ve[:, :], ACT.Ln).then_inc(S["lnv_done"], 1)
                act.wait_ge(S["lnv_done"], b + 1)
                act.activation(rr[:, 0, :], lnv[:, :], ACT.Exp, scale=-0.5).then_inc(S["r_ready"], 1)

            for kind, n in FIRST_ROUNDS[:-1]:
                drain(kind, n, first_round(kind, n), None)
            with act.Fori(0, NB) as b:
                for s in range(STEPS):
                    kt = s % KT
                    r = P if kt < KT - 1 else KR
                    act.wait_ge(S["scores"], b * STEPS + s + 1)
                    act.wait_ge(S["pv"], b * STEPS + s + 1)
                    act.activation(pT[0:r, s % 2, :, :], ps_s[0:r, s % 2, :, :], ACT.Exp, scale=DK ** -0.5).then_inc(S["exps"], 1)
                    if kt == 0 and s:
                        copy_o(b, s // KT - 1)
                    if s == 7:
                        root(b)
                    if s in ROUNDS:
                        kind, n = ROUNDS[s]
                        drain(kind, n, round_of(b, kind, n), b)
                copy_o(b, G4 - 1)
            for kind, n in ORDER[:3]:
                drain(kind, n, round_of(NB, kind, n), NB)
            root(NB)

        @block.vector
        def _(dve):
            dve.memset(V[:, :, :, :].rearrange("p t h c -> p (t h c)"), 0.0).then_inc(S["zero_done"], 1)
            dve.memset(oS[:, :], 1.0)
            dve.memset(unit_col[:, :], 1.0)
            dve.memset(keys[:, KT, :], 0.0)
            dve.memset(X[:, 0:PAD, :], 0.0)
            dve.wait_ge(S["zero_done"], 1)
            dve.memset(V[:, :, :, DK:DK + 1], 1.0)
            for g in range(G4):
                dve.memset(stack[SR:SR + 1, g, 0:LK].bitcast(F32), 1.0)
            dve.sem_inc(S["reduced"], CREDIT)
            dve.memset(cc[:, :, :, :], 1.0).then_inc(S["set_done"], 1)
            dve.wait_ge(S["set_done"], 1)

            def reduce(w, b):
                par, u = w // UNITS % 2, w % UNITS
                quarter = u % 4
                dve.wait_ge(S["units"], b * BUNITS + w + 1)
                dve.reduce_max(mx[:, par, u // 4, quarter:quarter + 1], ps_m[:, w % 2, 0:QUARTER[quarter][1]], AX.X).then_inc(S["reduced"], 1)
                if u == UNITS - 1:
                    dve.wait_ge(S["reduced"], b * BUNITS + w + 1 + CREDIT)
                    dve.tensor_reduce(out=neg[:, par, :], in_=mx[:, par, :, :], op=ALU.max, axis=AX.X, negate=True).then_inc(S["neg_ready"], 1)

            def drain(kind, n, rounds, b):
                if kind not in ("max", "norm", "out"):
                    return
                if kind == "max" and b is not None:
                    dve.wait_ge(S["row_in"], b * (16 * G4) + 16 * n)
                dve.wait_ge(S["bank_full"], rounds)
                if kind == "max":
                    dve.tensor_copy(negT[:, :], ps_x[0:2 * HG, 0:P]).then_inc(S["bank_free"], 1)
                elif kind == "norm":
                    v = ps_x[:, 0:L].rearrange("p (t h c) -> p t h c", t=2, h=HG)
                    dve.reciprocal(rden[:, :, :], v[:, :, :, DK]).then_inc(S["o_rec"], 1)
                    dve.wait_ge(S["o_rec"], b * G4 + (1 if n == 3 else n + 2))
                    dve.tensor_tensor(out=cc[:, :, HG * n:HG * n + HG, :], in0=v[:, :, :, 0:DK],
                                      in1=rden[:, :, :].unsqueeze(3).to_broadcast([P, 2, HG, DK]), op=ALU.mult).then_inc(S["bank_free"], 1)
                elif kind == "out":
                    tiles = X[:, bass.ds(b * 2, 2), :] if not isinstance(b, int) else X[:, 2 * b:2 * b + 2, :]
                    dve.tensor_tensor(out=xa[:, :, :], in0=tiles, in1=ps_x[:, 0:L].rearrange("p (t d) -> p t d", t=2),
                                      op=ALU.add).then_inc(S["bank_free"], 1)
                    dve.wait_ge(S["bank_free"], rounds)
                    dve.tensor_tensor(out=xb[:, :, :], in0=xa[:, :, :], in1=bo[:, :].unsqueeze(1).to_broadcast([P, 2, D]),
                                      op=ALU.add).then_inc(S["xa_done"], 1)
                    dve.wait_ge(S["xa_done"], b + 1)
                    for t in range(2):
                        last = dve.bn_stats(st[:, t, :], xb[:, t, :])
                    last.then_inc(S["ln_steps"], 1)
                    dve.wait_ge(S["ln_steps"], b * 7 + 1)
                    variance(dve, st, mom, mean, ve, S["ln_steps"], b * 7 + 1, S["ve_ready"])

            def finish(b):
                dve.wait_ge(S["r_ready"], b + 1)
                newton(dve, rstd[:, :], ve[:, :], rr[:, 0, :], rr[:, 1, :], rr[:, 2, :], S["ln_steps"], b * 7 + 3)
                for t in range(2):
                    dst = X[:, b * 2 + t, :]
                    last = dve.tensor_scalar(dst, xb[:, t, :], mean[:, t:t + 1], rstd[:, t:t + 1], ALU.subtract, ALU.mult)
                last.then_inc(S["x_done"], 1)
                dve.wait_ge(S["x_done"], b + 1)

            for w in range(AHEAD):
                reduce(w, 0)
                if w == UNITS:
                    drain("max", 0, first_round("max", 0), None)
            with dve.Fori(0, NB) as b:
                for s in range(STEPS):
                    for w in units_at(s):
                        reduce(w, b)
                    if s in ROUNDS:
                        kind, n = ROUNDS[s]
                        drain(kind, n, round_of(b, kind, n), b)
                    if s == 8:
                        finish(b)
            for kind, n in ORDER[:3]:
                drain(kind, n, round_of(NB, kind, n), NB)
            finish(NB)


def nc_mod(eng, n):
    return n % NB


E, HID = 8, 512
TE = NT + E - 1
UT = 3
GT = 4


def experts_stage(nc, a, X, ident, ones, out):
    assert TE % UT == 0
    with ExitStack() as ctx:
        def sb(name, shape, dt=F32):
            return ctx.enter_context(nc.sbuf_tensor(name, shape, dt))

        def pb(name, shape):
            return ctx.enter_context(nc.psum_tensor(name, shape, F32))

        x_slots = nc.dram_tensor("x_slots", (TE * P, D), F32, kind="Internal").ap()
        y_slots = nc.dram_tensor("y_slots", (TE * P, D), F32, kind="Internal").ap()

        w1 = sb("w1", [P, E, 2 * HID])
        w2 = sb("w2", [P, E, HID // P, D])
        b_raw = sb("b_raw", [2, E, 2 * HID])
        b2_raw = sb("b2_raw", [2, E, D])
        b1 = sb("b1", [2, E, 2 * HID], F32R)
        b2 = sb("b2", [2, E, D], F32R)
        two0 = sb("two0", [2, P])
        two = sb("two", [2, P], F32R)
        lo2 = sb("lo2", [2, 1])
        lo2i = sb("lo2i", [2, 1], I32)
        wr = sb("wr", [P, E])
        br = sb("br", [P, E])
        zero = sb("zero", [P, TE, D // 4])
        tri = sb("tri", [P, P])
        allone = sb("allone", [P, P])
        numi = sb("numi", [P, 64], I32)
        num = sb("num", [P, 64])
        xTr = sb("xTr", [P, 2, 4 * P])
        lg = sb("lg", [P, E, NT])
        best = sb("best", [P, NT])
        hit = sb("hit", [P, E, NT])
        first = sb("first", [P, NT])
        oh = sb("oh", [P, E, NT])
        more = sb("more", [P, E, NT])
        tot = sb("tot", [P, E, NT])
        incl = sb("incl", [P, E, NT])
        place = sb("place", [P, E, NT])
        full = sb("full", [P, E, NT])
        nt = sb("nt", [P, E])
        end = sb("end", [P, E])
        start = sb("start", [P, E])
        slotf = sb("slotf", [P, NT])
        slot = sb("slot", [P, NT], I32)
        past = sb("past", [P, TE, E])
        idf = sb("idf", [P, TE])
        tile_expert = sb("tile_expert", [P, TE], I32)
        xt = sb("xt", [P, UT, D])
        xT = sb("e_xT", [P, UT, P])
        sg = sb("sg", [P, UT, HID])
        act_ = sb("act_", [P, UT, HID])
        aT = sb("aT", [P, UT, HID // P, P])
        yt = sb("yt", [P, UT, D])
        Y = sb("Y", [P, NT, D])
        stt = sb("e_st", [P, NT, 6])
        mom = sb("e_mom", [P, 5, NT])
        mean = sb("e_mean", [P, NT])
        ve = sb("e_ve", [P, NT])
        lnv = sb("e_lnv", [P, NT])
        rr = sb("e_rr", [P, 3, NT])
        rstd = sb("e_rstd", [P, NT])

        ps_t = pb("e_ps_t", [P, 2, 512])
        ps_h = pb("e_ps_h", [P, 2, 2, HID])
        ps_y = pb("e_ps_y", [P, 512])
        ps_l = pb("e_ps_l", [P, 512])

        names = ("w_in e_in b_in zeroed consts iota_done set_done b_steps xtr_ps xtr_sb logits steps oh_ready counts "
                 "slots_ready scattered xt_in xt_ps xt_sb h_ps sg_done act_done at_ps at_sb y_ps y_sb y_out "
                 "yt_free sums stats_done ve_ready lnv_done r_ready z_done out_done").split()
        S = {n: ctx.enter_context(nc.semaphore("e_" + n)) for n in names}
        gathered = [ctx.enter_context(nc.semaphore(f"e_gathered{g}")) for g in range(NT // GT)]
        xt_in = [ctx.enter_context(nc.semaphore(f"e_xt_in{g}")) for g in range(UT)]
        y_out = [ctx.enter_context(nc.semaphore(f"e_y_out{g}")) for g in range(UT)]
        block = ctx.enter_context(nc.Block())

        @block.sync
        def _(sp):
            row = lambda v: v.rearrange("(o d) -> o d", o=1)
            sp.dma_start(wr[:, :], a["L0_ffn_router_w"]).then_inc(S["w_in"], 16)
            sp.dma_start(br[:, :], row(a["L0_ffn_router_b"]).to_broadcast([P, E])).then_inc(S["w_in"], 16)
            sp.wait_ge(S["consts"], 1)
            v = x_slots.rearrange("(p t) (q c) -> p t q c", p=P, q=4)
            for q in range(4):
                sp.dma_start(v[:, :, q, :], zero[:, :, :]).then_inc(S["zeroed"], 16)
            for k in range(2):
                sp.dma_start(b_raw[k:k + 1, :, :].rearrange("o e n -> o (e n)"), a["L0_ffn_b1"].rearrange("(o e) n -> o (e n)", o=1)).then_inc(S["b_in"], 16)
                sp.dma_start(b2_raw[k:k + 1, :, :].rearrange("o e n -> o (e n)"), a["L0_ffn_b2"].rearrange("(o e) n -> o (e n)", o=1)).then_inc(S["b_in"], 16)
            for e in range(E):
                sp.dma_start(w1[:, e, :], a["L0_ffn_w1"][e]).then_inc(S["e_in"], 16)
                sp.dma_start(w2[:, e, :, :], a["L0_ffn_w2"][e].rearrange("(j p) d -> p j d", p=P)).then_inc(S["e_in"], 16)
            sp.wait_ge(S["scattered"], 16 * NT)
            for k in range(UT):
                sp.dma_start(xt[:, k, :], x_slots[P * k:P * k + P, :]).then_inc(xt_in[k], 16)
            sp.sem_inc(S["yt_free"], UT)
            with sp.Fori(0, TE // UT) as i:
                for k in range(UT):
                    sp.wait_ge(S["xt_ps"], i * UT + k + 1)
                    sp.dma_start(xt[:, k, :], x_slots[bass.ds(((i + 1) % (TE // UT)) * (UT * P) + k * P, P), :]).then_inc(xt_in[k], 16)
                    sp.wait_ge(S["y_sb"], i * UT + k + 1)
                    sp.dma_start(y_slots[bass.ds(i * (UT * P) + k * P, P), :], yt[:, k, :]).then_inc(y_out[k], 16)
                for k in range(UT):
                    sp.wait_ge(y_out[k], i * 16 + 16)
                    sp.sem_inc(S["yt_free"], 1)
            for k in range(UT):
                sp.wait_ge(xt_in[k], 16 * (TE // UT + 1))
            for g in range(NT // GT):
                sp.wait_ge(S["z_done"], g + 1)
                sp.dma_start(tokens(out)[:, GT * g:GT * g + GT, :], Y[:, GT * g:GT * g + GT, :]).then_inc(S["out_done"], 16)
            sp.wait_ge(S["out_done"], 16 * (NT // GT))

        @block.gpsimd
        def _(pool):
            pool.memset(zero[:, :, :], 0.0).then_inc(S["consts"], 1)
            pool.wait_ge(S["consts"], 1)
            pool.iota(numi[:, :], pattern=[[1, 64]], base=0, channel_multiplier=0).then_inc(S["consts"], 1)
            pool.wait_ge(S["consts"], 2)
            pool.iota(lo2i[:, :], pattern=[[0, 1]], base=0, channel_multiplier=-1).then_inc(S["consts"], 1)
            pool.wait_ge(S["consts"], 3)
            pool.memset(tri[:, :], 1.0).then_inc(S["consts"], 1)
            pool.wait_ge(S["consts"], 4)
            pool.affine_select(out=tri[:, :], in_=tri[:, :], compare_op=ALU.is_gt, fill=0.0, base=0,
                               pattern=[[1, P]], channel_multiplier=-1).then_inc(S["consts"], 1)
            pool.wait_ge(S["zeroed"], 64)
            pool.wait_ge(S["slots_ready"], 1)
            for t in range(NT):
                pool.indirect_dma_start(x_slots[:, :], bass.IndirectOffsetOnAxis(ap=slot[:, t:t + 1], axis=0),
                                        X[:, PAD + t, :], None).then_inc(S["scattered"], 16)
            for k in range(UT):
                pool.wait_ge(y_out[k], 16 * (TE // UT))
            for t in range(NT):
                pool.indirect_dma_start(Y[:, t, :], None, y_slots[:, :],
                                        bass.IndirectOffsetOnAxis(ap=slot[:, t:t + 1], axis=0)).then_inc(gathered[t // GT], 16)

        @block.tensor
        def _(pe):
            pe.wait_ge(S["w_in"], 32)
            for r in range(NT // 4):
                if r >= 2:
                    pe.wait_ge(S["xtr_sb"], r - 1)
                for t in range(4):
                    last = pe.transpose(ps_t[:, r % 2, P * t:P * t + P], X[:, PAD + 4 * r + t, :], ident[:, :])
                last.then_inc(S["xtr_ps"], 1)
                pe.wait_ge(S["xtr_sb"], r + 1)
                for t in range(4):
                    c = (4 * r + t) * E
                    last = pe.matmul(ps_l[:, c:c + E], xTr[:, r % 2, P * t:P * t + P], wr[:, :], start=True, stop=True)
                last.then_inc(S["logits"], 1)
            pe.wait_ge(S["consts"], 5)
            pe.wait_ge(S["set_done"], 1)
            pe.wait_ge(S["oh_ready"], 1)
            ohf = oh[:, :, :].rearrange("p e t -> p (e t)")
            pe.matmul(ps_l[:, 0:E * NT], tri[:, :], ohf, start=True, stop=True)
            pe.matmul(ps_l[:, E * NT:], allone[:, :], ohf, start=True, stop=True).then_inc(S["counts"], 1)
            pe.wait_ge(S["e_in"], 16 * 2 * E)
            pe.wait_ge(S["b_steps"], 4)

            def up(k, i):
                count = i * UT + k
                e = pe.value_load(tile_expert[0:1, bass.ds(count, 1)], min_val=0, max_val=E - 1)
                pe.wait_ge(S["xt_sb"], count + 1)
                buf = k % 2
                for c in range(2):
                    pe.matmul(ps_h[:, 0, c, :], two[:, :], b1[:, bass.ds(e, 1), HID * c:HID * c + HID], start=True, stop=False)
                    last = pe.matmul(ps_h[:, 0, c, :], xT[:, k, :], w1[:, bass.ds(e, 1), HID * c:HID * c + HID], start=False, stop=True)
                last.then_inc(S["h_ps"], 1)
                return e

            pe.wait_ge(S["slots_ready"], 1)
            with pe.Fori(0, TE // UT) as i:
                for k in range(UT):
                    count = i * UT + k
                    pe.wait_ge(xt_in[k], i * 16 + 16)
                    pe.transpose(ps_t[:, 0, 0:P], xt[:, k, :], ident[:, :]).then_inc(S["xt_ps"], 1)
                    e = up(k, i)
                    pe.wait_ge(S["act_done"], count + 1)
                    for j in range(HID // P):
                        last = pe.transpose(ps_t[:, 1, P * j:P * j + P], act_[:, k, P * j:P * j + P], ident[:, :])
                    last.then_inc(S["at_ps"], 1)
                    pe.wait_ge(S["at_sb"], count + 1)
                    pe.matmul(ps_y[:, 0:D], two[:, :], b2[:, bass.ds(e, 1), :], start=True, stop=False)
                    for j in range(HID // P):
                        last = pe.matmul(ps_y[:, 0:D], aT[:, k, j, :], w2[:, bass.ds(e, 1), j, :], start=False, stop=(j == HID // P - 1))
                    last.then_inc(S["y_ps"], 1)

        @block.scalar
        def _(act):
            for r in range(NT // 4):
                act.wait_ge(S["xtr_ps"], r + 1)
                if r >= 2:
                    act.wait_ge(S["logits"], r - 1)
                act.activation(xTr[:, r % 2, :], ps_t[:, r % 2, :], ACT.Copy).then_inc(S["xtr_sb"], 1)
            act.preload_act_table(ACT.Sigmoid)
            with act.Fori(0, TE // UT) as i:
                for k in range(UT):
                    count = i * UT + k
                    act.wait_ge(S["xt_ps"], count + 1)
                    act.activation(xT[:, k, :], ps_t[:, 0, 0:P], ACT.Copy).then_inc(S["xt_sb"], 1)
                    act.wait_ge(S["h_ps"], count + 1)
                    act.activation(sg[:, k, :], ps_h[:, 0, 1, :], ACT.Sigmoid).then_inc(S["sg_done"], 1)
                    act.wait_ge(S["at_ps"], count + 1)
                    act.activation(aT[:, k, :, :].rearrange("p j t -> p (j t)"), ps_t[:, 1, :], ACT.Copy).then_inc(S["at_sb"], 1)
            act.preload_act_table_set("natural_log_exp_and_others")
            for g in range(NT // GT):
                act.wait_ge(S["ve_ready"], g + 1)
                act.activation(lnv[:, GT * g:GT * g + GT], ve[:, GT * g:GT * g + GT], ACT.Ln).then_inc(S["lnv_done"], 1)
                act.wait_ge(S["lnv_done"], g + 1)
                act.activation(rr[:, 0, GT * g:GT * g + GT], lnv[:, GT * g:GT * g + GT], ACT.Exp, scale=-0.5).then_inc(S["r_ready"], 1)

        @block.vector
        def _(dve):
            steps = [0]

            def link(ins):
                steps[0] += 1
                ins.then_inc(S["steps"], 1)
                dve.wait_ge(S["steps"], steps[0])

            def over(v):
                return v.unsqueeze(1).to_broadcast([P, E, NT])

            def along(v):
                return v.unsqueeze(2).to_broadcast([P, E, NT])

            dve.memset(allone[:, :], 1.0)
            dve.memset(two0[:, :], 1.0)
            link(dve.memset(more[:, :, :], 1.0))
            dve.memset(more[:, :, 0:1], 0.0)
            dve.tensor_copy(two[:, :], two0[:, :]).then_inc(S["set_done"], 1)
            dve.wait_ge(S["consts"], 3)
            link(dve.tensor_copy(num[:, :], numi[:, :]))
            link(dve.tensor_copy(lo2[:, :], lo2i[:, :]))
            dve.wait_ge(S["logits"], NT // 4)
            dve.wait_ge(S["w_in"], 32)
            link(dve.tensor_tensor(out=lg[:, :, :], in0=ps_l[:, 0:E * NT].rearrange("p (t e) -> p e t", e=E), in1=along(br[:, :]), op=ALU.add))
            link(dve.tensor_reduce(out=best[:, :], in_=lg[:, :, :].rearrange("p e t -> p t e"), op=ALU.max, axis=AX.X))
            link(dve.tensor_tensor(out=hit[:, :, :], in0=lg[:, :, :], in1=over(best[:, :]), op=ALU.is_lt))
            link(dve.scalar_tensor_tensor(out=place[:, :, :], in0=hit[:, :, :], scalar=float(E), in1=along(num[:, 0:E]),
                                          op0=ALU.mult, op1=ALU.add))
            link(dve.tensor_reduce(out=first[:, :], in_=place[:, :, :].rearrange("p e t -> p t e"), op=ALU.min, axis=AX.X))
            dve.tensor_tensor(out=oh[:, :, :], in0=along(num[:, 0:E]), in1=over(first[:, :]), op=ALU.is_equal).then_inc(S["oh_ready"], 1)
            dve.wait_ge(S["b_in"], 64)
            for raw, dst in ((b_raw, b1), (b2_raw, b2)):
                dve.tensor_copy(dst[:, :, :], raw[:, :, :]).then_inc(S["b_steps"], 1)
            dve.wait_ge(S["b_steps"], 2)
            for raw, dst in ((b_raw, b1), (b2_raw, b2)):
                fl = lambda v: v[:, :, :].rearrange("p e n -> p (e n)")
                dve.scalar_tensor_tensor(out=fl(dst), in0=fl(dst).bitcast(F32), scalar=lo2[:, 0:1], in1=fl(raw),
                                         op0=ALU.mult, op1=ALU.add).then_inc(S["b_steps"], 1)
            dve.wait_ge(S["counts"], 1)
            link(dve.tensor_copy(tot[:, :, :].rearrange("p e t -> p (e t)"), ps_l[:, E * NT:]))
            link(dve.tensor_tensor_scan(incl[:, :, :].rearrange("p e t -> p (e t)"), more[:, :, :].rearrange("p e t -> p (e t)"),
                                        tot[:, :, :].rearrange("p e t -> p (e t)"), 0.0, ALU.mult, ALU.add))
            link(dve.tensor_tensor(out=place[:, :, :], in0=incl[:, :, :], in1=tot[:, :, :], op=ALU.subtract))
            link(dve.tensor_tensor(out=hit[:, :, :].rearrange("p e t -> p (e t)"), in0=place[:, :, :].rearrange("p e t -> p (e t)"), in1=ps_l[:, 0:E * NT], op=ALU.add))
            link(dve.tensor_scalar(full[:, :, :], num[:, 0:NT].unsqueeze(1).to_broadcast([P, E, NT]), float(P), None, ALU.mult))
            link(dve.tensor_tensor(out=full[:, :, :], in0=full[:, :, :], in1=along(incl[:, :, NT - 1]), op=ALU.is_lt))
            link(dve.tensor_reduce(out=nt[:, :], in_=full[:, :, :], op=ALU.add, axis=AX.X))
            link(dve.tensor_tensor_scan(end[:, :], allone[:, 0:E], nt[:, :], 0.0, ALU.mult, ALU.add))
            link(dve.tensor_tensor(out=start[:, :], in0=end[:, :], in1=nt[:, :], op=ALU.subtract))
            link(dve.tensor_scalar(start[:, :], start[:, :], float(P), None, ALU.mult))
            link(dve.tensor_tensor(out=hit[:, :, :], in0=hit[:, :, :], in1=along(start[:, :]), op=ALU.add))
            link(dve.tensor_tensor(out=hit[:, :, :], in0=hit[:, :, :], in1=oh[:, :, :], op=ALU.mult))
            link(dve.tensor_reduce(out=slotf[:, :], in_=hit[:, :, :].rearrange("p e t -> p t e"), op=ALU.add, axis=AX.X))
            link(dve.tensor_copy(slot[:, :], slotf[:, :]))
            link(dve.tensor_tensor(out=past[:, :, :], in0=num[:, 0:TE].unsqueeze(2).to_broadcast([P, TE, E]),
                                   in1=end[:, :].unsqueeze(1).to_broadcast([P, TE, E]), op=ALU.is_ge))
            link(dve.tensor_reduce(out=idf[:, :], in_=past[:, :, :], op=ALU.add, axis=AX.X))
            link(dve.tensor_scalar(idf[:, :], idf[:, :], float(E - 1), None, ALU.min))
            dve.tensor_copy(tile_expert[:, :], idf[:, :]).then_inc(S["slots_ready"], 1)
            with dve.Fori(0, TE // UT) as i:
                for k in range(UT):
                    count = i * UT + k
                    dve.wait_ge(S["sg_done"], count + 1)
                    dve.tensor_tensor(out=act_[:, k, :], in0=sg[:, k, :], in1=ps_h[:, 0, 0, :], op=ALU.mult).then_inc(S["act_done"], 1)
                    dve.wait_ge(S["y_ps"], count + 1)
                    dve.wait_ge(S["yt_free"], count + 1)
                    dve.tensor_copy(yt[:, k, :], ps_y[:, 0:D]).then_inc(S["y_sb"], 1)
            for g in range(NT // GT):
                s = slice(GT * g, GT * g + GT)
                dve.wait_ge(gathered[g], 16 * GT)
                dve.tensor_tensor(out=Y[:, s, :], in0=Y[:, s, :], in1=X[:, PAD + GT * g:PAD + GT * g + GT, :], op=ALU.add).then_inc(S["sums"], 1)
                dve.wait_ge(S["sums"], g + 1)
                for t in range(GT * g, GT * g + GT):
                    last = dve.bn_stats(stt[:, t, :], Y[:, t, :])
                last.then_inc(S["stats_done"], 1)
                dve.wait_ge(S["stats_done"], g * 7 + 1)
                variance(dve, stt[:, s, :], mom[:, :, s], mean[:, s], ve[:, s], S["stats_done"], g * 7 + 1, S["ve_ready"])
                dve.wait_ge(S["r_ready"], g + 1)
                newton(dve, rstd[:, s], ve[:, s], rr[:, 0, s], rr[:, 1, s], rr[:, 2, s], S["stats_done"], g * 7 + 3)
                for t in range(GT * g, GT * g + GT):
                    last = dve.tensor_scalar(Y[:, t, :], Y[:, t, :], mean[:, t:t + 1], rstd[:, t:t + 1], ALU.subtract, ALU.mult)
                last.then_inc(S["z_done"], 1)


_OUT = ((16, 256, 128), "float32")


def kernel(**inputs):
    import numpy as _np
    import concourse.bacc as _bacc
    from concourse import mybir as _mybir
    from concourse.bass_utils import run_bass_kernel_spmd as _run

    nc = _bacc.Bacc("TRN2", target_bir_lowering=False, num_devices=1)
    arrays, args = {}, {}
    for name, value in inputs.items():
        v = _np.ascontiguousarray(value)
        arrays[f"in_{name}_dram"] = v
        args[name] = nc.dram_tensor(f"in_{name}_dram", v.shape, _mybir.dt.from_np(v.dtype), kind="ExternalInput").ap()
    out = nc.dram_tensor("out_0_dram", _OUT[0], _mybir.dt.from_np(_np.dtype(_OUT[1])), kind="ExternalOutput").ap()
    build_program(nc, args, out)
    r = _run(nc, [arrays], core_ids=[0])
    return r.results[0]["out_0_dram"]
```

```python
import concourse.bass as bass
from concourse import mybir
from contextlib import ExitStack

F32 = mybir.dt.float32
F32R = mybir.dt.float32r
I32 = mybir.dt.int32
ALU = mybir.AluOpType
ACT = mybir.ActivationFunctionType
AX = mybir.AxisListType

P = 128
NB, L, D = 16, 256, 128
NT = NB * L // P
PAD = 2
DI, NS, KC = 64, 32, 3
EPS = 1e-5
SERIES = (15, 13, 11, 9, 7, 5, 3)
E, HID = 8, 512
TE = NT + E - 1
BC1, BC2 = E * 2 * HID // P, E * D // P
BC = BC1 + BC2


def build_program(nc, a, out, stop=3):
    with ExitStack() as ctx:
        def sb(name, shape, dt=F32):
            return ctx.enter_context(nc.sbuf_tensor(name, shape, dt))

        X = sb("X", [P, PAD + NT, D])
        ident = sb("ident", [P, P])
        ones = sb("ones", [1, P])
        pre = Preloads()
        pre.w1 = sb("w1", [P, E, 2 * HID])
        pre.w2 = sb("w2", [P, E, HID // P, D])
        pre.b_parts = sb("b_parts", [P, 2, BC], F32R)
        pre.x_slots = nc.dram_tensor("x_slots", (TE * P, D), F32, kind="Internal").ap()
        for name in ("weights_in", "slots_zeroed"):
            pre.sems[name] = ctx.enter_context(nc.semaphore(name))
        mamba_stage(nc, a, X, ident, ones, pre)
        if stop == 1:
            dump(nc, X, out)
            return
        attention_stage(nc, a, X, ident)
        if stop == 2:
            dump(nc, X, out)
            return
        experts_stage(nc, a, X, ident, pre, out)


def tokens(ap):
    return ap.rearrange("b (h p) d -> p (b h) d", p=P)


def dump(nc, X, out):
    with ExitStack() as ctx:
        dumped = ctx.enter_context(nc.semaphore("dumped"))
        block = ctx.enter_context(nc.Block())

        @block.sync
        def _(sp):
            sp.dma_start(tokens(out), X[:, PAD:, :]).then_inc(dumped, 16)
            sp.wait_ge(dumped, 16)


def variance(dve, st, mom, mean, ve, step, base, ready):
    dve.tensor_tensor(out=mom[:, 0, :], in0=st[:, :, 1], in1=st[:, :, 4], op=ALU.add)
    dve.tensor_tensor(out=mom[:, 1, :], in0=st[:, :, 1], in1=st[:, :, 4], op=ALU.subtract)
    dve.tensor_tensor(out=mom[:, 2, :], in0=st[:, :, 2], in1=st[:, :, 5], op=ALU.add).then_inc(step, 1)
    dve.wait_ge(step, base + 1)
    dve.tensor_scalar(mean[:, :], mom[:, 0, :], 0.5, None, ALU.mult)
    dve.tensor_tensor(out=mom[:, 3, :], in0=mom[:, 1, :], in1=mom[:, 1, :], op=ALU.mult)
    dve.tensor_scalar(mom[:, 4, :], mom[:, 2, :], 1.0 / D, EPS, ALU.mult, ALU.add).then_inc(step, 1)
    dve.wait_ge(step, base + 2)
    dve.scalar_tensor_tensor(out=ve[:, :], in0=mom[:, 3, :], scalar=0.25, in1=mom[:, 4, :],
                             op0=ALU.mult, op1=ALU.add).then_inc(ready, 1)


def newton(dve, out, v, r, t1, t2, step, base):
    dve.tensor_tensor(out=t1, in0=r, in1=r, op=ALU.mult).then_inc(step, 1)
    dve.wait_ge(step, base + 1)
    dve.tensor_tensor(out=t2, in0=t1, in1=v, op=ALU.mult).then_inc(step, 1)
    dve.wait_ge(step, base + 2)
    dve.tensor_scalar(t1, t2, -0.5, 1.5, ALU.mult, ALU.add).then_inc(step, 1)
    dve.wait_ge(step, base + 3)
    dve.tensor_tensor(out=out, in0=r, in1=t1, op=ALU.mult).then_inc(step, 1)
    dve.wait_ge(step, base + 4)


class Preloads:
    def __init__(self):
        self.sems = {}


def mamba_stage(nc, a, X, ident, ones, pre):
    PAIRS = NB // 2
    CH = 4
    NCH = NS // CH
    ND = 4 + len(SERIES)
    with ExitStack() as ctx:
        def sb(name, shape, dt=F32):
            return ctx.enter_context(nc.sbuf_tensor(name, shape, dt))

        def pb(name, shape):
            return ctx.enter_context(nc.psum_tensor(name, shape, F32))

        def sem(name):
            return ctx.enter_context(nc.semaphore(name))

        w_raw = sb("w_raw", [P, 4, DI])
        w_up = sb("w_up", [P, 4, DI])
        gam = sb("gam", [P, 1])
        bet = sb("bet", [P, 1])
        b_up = sb("b_up", [P, 2])
        b_eff = sb("b_eff", [P, 2])
        conv_w = sb("conv_w", [P, KC])
        conv_b = sb("conv_b", [P, 1])
        b_dl = sb("b_dl", [P, 1])
        d_skip = sb("d_skip", [P, 1])
        a_log = sb("a_log", [P, NS])
        a_exp = sb("a_exp", [P, NS])
        a_neg = sb("a_neg", [P, NS])
        w_dl = sb("w_dl", [P, P])
        w_bc = sb("w_bc", [P, 2, 2, 2, NS])
        w_dn = sb("w_dn", [P, 2, D])
        bd_row = sb("bd_row", [1, 4, D])
        pick0 = sb("pick0", [P, NS, P])
        pick = sb("pick", [P, NS, P], F32R)
        lo_rows = sb("lo_rows", [P, 1])
        stats = sb("stats", [P, NT, 6])
        mom = sb("mom", [P, 5, NT])
        mean = sb("mean", [P, NT])
        ve = sb("ve", [P, NT])
        lnv = sb("lnv", [P, NT])
        r0 = sb("r0", [P, NT])
        r1 = sb("r1", [P, NT])
        rstd = sb("rstd", [P, NT])
        y4 = sb("y4", [P, 4, D])
        yT = sb("yT", [P, 4 * P])
        left = sb("left", [P, L + KC - 1])
        right = sb("right", [P, L])
        c1 = sb("c1", [P, L])
        c2 = sb("c2", [P, L])
        c3 = sb("c3", [P, L])
        e_c = sb("e_c", [P, L])
        e_c1 = sb("e_c1", [P, L])
        s_c = sb("s_c", [P, L])
        u = sb("u", [P, L])
        e_r = sb("e_r", [P, L])
        e_r1 = sb("e_r1", [P, L])
        s_r = sb("s_r", [P, L])
        gate = sb("gate", [P, L])
        z = sb("z", [P, L])
        nz = sb("nz", [P, L])
        e_z = sb("e_z", [P, L])
        w_z = sb("w_z", [P, L])
        w_m = sb("w_m", [P, L])
        s_z = sb("s_z", [P, L])
        s2 = sb("s2", [P, L])
        pz = sb("pz", [P, 2, L])
        q_z = sb("q_z", [P, L])
        delta = sb("delta", [P, L])
        du = sb("du", [P, L])
        bc_hi = sb("bc_hi", [P, 2 * L], F32R)
        bc = sb("bc", [P, 2, L], F32R)
        dA = sb("dA", [P, 2, CH, L])
        dB = sb("dB", [P, CH, L])
        h = sb("h", [P, CH, L])
        hC = sb("hC", [P, 2, CH, L])
        y2 = sb("y2", [P, L])
        gated = sb("gated", [P, L])
        xn = sb("xn", [P, 4, D])
        st2 = sb("st2", [P, 4, 6])
        mom2 = sb("mom2", [P, 5, 4])
        mean2 = sb("mean2", [P, 4])
        ve2 = sb("ve2", [P, 4])
        lnv2 = sb("lnv2", [P, 4])
        rr = sb("rr", [P, 3, 4])
        rstd2 = sb("rstd2", [P, 4])

        zero = sb("zero", [P, TE, D // 4])
        b_raw = sb("b_raw", [P, BC])

        ps_t = pb("ps_t", [P, 512])
        ps_up = pb("ps_up", [P, 512])
        ps_zy = pb("ps_zy", [P, 512])
        ps_bc = pb("ps_bc", [P, 512])
        ps_b = pb("ps_b", [P, CH, L])
        ps_c = pb("ps_c", [P, CH, L])

        names = ("zero_ready braw_in b_split zeroed set_done bd_done x_in w_in w_in2 id_done pick_done pick_r w_scaled beta_ps beta_add a_done a_ready "
                 "small rs_ln rs_exp y_ready yt_ps yt_sb up_ps up_sb conv conv_exp right_exp usteps rsteps s_ready u_ready z_ps bc_ps "
                 "zsteps nz_ready z_exp z_ln bc_ready dsteps delta_ready du_ready b_ps c_ps db_done "
                 "da_ready scanned hc_done n_summed y_ps gsteps gated_ready o_ps xn_steps ve_ready ve_ln r_ready x_done").split()
        S = {n: sem("m_" + n) for n in names}
        block = ctx.enter_context(nc.Block())
        N_IN = 21

        @block.sync
        def _(sp):
            sp.dma_start(X[:, PAD:, :], tokens(a["x"])).then_inc(S["x_in"], 16)
            n = 0
            W = a["L0_attn_W_up"]
            col = lambda v: v.rearrange("(p o) -> p o", o=1)
            for dst, src in (
                (w_raw[:, 0, :], W[:, 0:DI]), (w_raw[:, 1, :], W[:, 0:DI]),
                (w_raw[:, 2, :], W[:, DI:2 * DI]), (w_raw[:, 3, :], W[:, DI:2 * DI]),
                (gam[:, :], col(a["L0_attn_ln_gamma"])), (bet[:, :], col(a["L0_attn_ln_beta"])),
            ):
                sp.dma_start(dst, src).then_inc(S["w_in"], 16)
                n += 1
            for k in range(2):
                rows = slice(DI * k, DI * k + DI)
                for dst, src in (
                    (b_up[rows, 0:1], col(a["L0_attn_b_up"][0:DI])),
                    (b_up[rows, 1:2], col(a["L0_attn_b_up"][DI:2 * DI])),
                    (conv_w[rows, :], a["L0_attn_conv_w"].rearrange("d o k -> d (o k)")),
                    (conv_b[rows, :], col(a["L0_attn_conv_b"])),
                    (b_dl[rows, :], col(a["L0_attn_b_delta"])),
                    (d_skip[rows, :], col(a["L0_attn_D"])),
                    (a_log[rows, :], a["L0_attn_A_log"]),
                ):
                    sp.dma_start(dst, src).then_inc(S["w_in"], 16)
                    n += 1
            sp.dma_start(bd_row[:, 0, :], a["L0_attn_b_down"].rearrange("(o d) -> o d", o=1)).then_inc(S["w_in"], 16)
            n += 1
            assert n == N_IN
            sp.wait_ge(S["zeroed"], 4)
            for k in range(2):
                rows = slice(DI * k, DI * k + DI)
                sp.dma_start(w_dl[rows, DI * k:DI * k + DI], a["L0_attn_W_delta"]).then_inc(S["w_in2"], 16)
                sp.dma_start(w_dn[rows, k, :], a["L0_attn_W_down"]).then_inc(S["w_in2"], 16)
                for s, w in enumerate((a["L0_attn_W_B"], a["L0_attn_W_C"])):
                    for part in range(2):
                        sp.dma_start(w_bc[rows, s, part, k, :], w).then_inc(S["w_in2"], 16)
            sp.dma_start(b_raw[:, 0:BC1], a["L0_ffn_b1"].rearrange("e n -> (e n)").rearrange("(p c) -> p c", p=P)).then_inc(S["braw_in"], 16)
            sp.dma_start(b_raw[:, BC1:], a["L0_ffn_b2"].rearrange("e n -> (e n)").rearrange("(p c) -> p c", p=P)).then_inc(S["braw_in"], 16)
            for e in range(E):
                sp.dma_start(pre.w1[:, e, :], a["L0_ffn_w1"][e]).then_inc(pre.sems["weights_in"], 16)
                sp.dma_start(pre.w2[:, e, :, :], a["L0_ffn_w2"][e].rearrange("(j p) d -> p j d", p=P)).then_inc(pre.sems["weights_in"], 16)
            sp.wait_ge(S["zero_ready"], 1)
            v = pre.x_slots.rearrange("(p t) (q c) -> p t q c", p=P, q=4)
            for q in range(4):
                sp.dma_start(v[:, :, q, :], zero[:, :, :]).then_inc(pre.sems["slots_zeroed"], 16)
            sp.wait_ge(pre.sems["slots_zeroed"], 64)
        N_IN2 = 12

        @block.gpsimd
        def _(pool):
            for n, m in enumerate((w_dl[:, :], w_dn[:, :, :], w_bc[:, :, :, :, :], ident[:, :], pick0[:, :, :])):
                if n:
                    pool.wait_ge(S["zeroed"], n)
                pool.memset(m, 0.0).then_inc(S["zeroed"], 1)
            pool.wait_ge(S["zeroed"], 5)
            pool.affine_select(out=ident[:, :], in_=ident[:, :], compare_op=ALU.not_equal, fill=1.0,
                               base=0, pattern=[[-1, P]], channel_multiplier=1).then_inc(S["id_done"], 1)
            pool.wait_ge(S["id_done"], 1)
            for q in range(4):
                v = pick0[NS * q:NS * q + NS, :, DI * (q % 2):DI * (q % 2) + DI]
                pool.affine_select(out=v, in_=v, compare_op=ALU.not_equal, fill=1.0, base=0,
                                   pattern=[[-1, NS], [0, DI]], channel_multiplier=1).then_inc(S["pick_done"], 1)
                pool.wait_ge(S["pick_done"], q + 1)
            pool.tensor_copy(pick[:, :, :], pick0[:, :, :]).then_inc(S["pick_r"], 1)
            pool.wait_ge(S["pick_r"], 1)
            pool.memset(zero[:, :, :], 0.0).then_inc(S["zero_ready"], 1)
            pool.wait_ge(S["zero_ready"], 1)
            pool.wait_ge(S["braw_in"], 32)
            pool.tensor_copy(pre.b_parts[:, 0, :], b_raw[:, :]).then_inc(S["b_split"], 1)
            pool.wait_ge(S["b_split"], 1)
            pool.tensor_tensor(out=pre.b_parts[:, 1, :], in0=b_raw[:, :], in1=pre.b_parts[:, 0, :].bitcast(F32), op=ALU.subtract).then_inc(S["b_split"], 1)
            pool.wait_ge(S["b_split"], 2)

        @block.tensor
        def _(pe):
            pe.wait_ge(S["w_in"], 16 * N_IN)
            for s in range(2):
                last = pe.matmul(ps_up[:, s:s + 1], w_raw[:, 2 * s:2 * s + 2, :].rearrange("p k c -> p (k c)"), bet[:, :],
                                 start=True, stop=True)
            last.then_inc(S["beta_ps"], 1)
            pe.wait_ge(S["id_done"], 1)
            pe.wait_ge(S["w_in2"], 16 * N_IN2)
            pe.wait_ge(S["w_scaled"], 1)
            pe.wait_ge(S["set_done"], 1)
            pe.wait_ge(S["beta_add"], 1)
            pe.wait_ge(S["pick_r"], 1)
            pe.wait_ge(S["bd_done"], 1)
            with pe.Fori(0, PAIRS) as j:
                pe.wait_ge(S["y_ready"], j * 4 + 4)
                for t in range(4):
                    last = pe.transpose(ps_t[:, t * P:(t + 1) * P], y4[:, t, :], ident[:, :])
                last.then_inc(S["yt_ps"], 1)
                pe.wait_ge(S["yt_sb"], j + 1)
                for s in range(2):
                    for k in range(2):
                        last = pe.matmul(ps_up[DI * k:DI * k + DI, L * s:L * s + L], w_up[:, 2 * s + k, :],
                                         yT[:, L * k:L * k + L], start=True, stop=True)
                last.then_inc(S["up_ps"], 1)
                pe.wait_ge(S["u_ready"], j + 1)
                pe.matmul(ps_zy[:, 0:L], w_dl[:, :], u[:, :], start=True, stop=True).then_inc(S["z_ps"], 1)
                for s in range(2):
                    last = pe.matmul(ps_bc[:, L * s:L * s + L],
                                     w_bc[:, s, :, :, :].rearrange("p a b n -> p (a b n)"), u[:, :],
                                     start=True, stop=True)
                last.then_inc(S["bc_ps"], 1)
                pe.wait_ge(S["bc_ready"], j + 1)

                def spread(s, ps, c, done):
                    for n in range(CH):
                        last = pe.matmul(ps[:, n, :], pick[:, c * CH + n, :], bc[:, s, :], start=True, stop=True)
                    last.then_inc(S[done], 1)

                spread(0, ps_b, 0, "b_ps")
                spread(1, ps_c, 0, "c_ps")
                for c in range(NCH):
                    if c < NCH - 1:
                        pe.wait_ge(S["db_done"], j * NCH + c + 1)
                        spread(0, ps_b, c + 1, "b_ps")
                    pe.wait_ge(S["hc_done"], j * NCH + c + 1)
                    if c < NCH - 1:
                        spread(1, ps_c, c + 1, "c_ps")
                    for n in range(CH):
                        last = pe.matmul(ps_zy[:, L:2 * L], ident[:, :], hC[:, c % 2, n, :],
                                         start=(c == 0 and n == 0), stop=(c == NCH - 1 and n == CH - 1))
                    last.then_inc(S["n_summed"], 1)
                pe.matmul(ps_t[:, :], ones[0:1, :], bd_row[0:1, :, :].rearrange("o t d -> o (t d)"), start=True, stop=False, skip_group_check=True)
                pe.wait_ge(S["gated_ready"], j + 1)
                for t in range(4):
                    last = pe.matmul(ps_t[:, t * D:(t + 1) * D], gated[:, (t % 2) * P:(t % 2) * P + P], w_dn[:, t // 2, :],
                                     start=False, stop=True, skip_group_check=True)
                last.then_inc(S["o_ps"], 1)

        @block.scalar
        def _(act):
            act.preload_act_table_set("natural_log_exp_and_others")
            act.wait_ge(S["w_in"], 16 * N_IN)
            act.activation(a_exp[:, :], a_log[:, :], ACT.Exp).then_inc(S["a_done"], 1)
            act.wait_ge(S["ve_ready"], 1)
            act.activation(lnv[:, :], ve[:, :], ACT.Ln).then_inc(S["rs_ln"], 1)
            act.wait_ge(S["rs_ln"], 1)
            act.activation(r0[:, :], lnv[:, :], ACT.Exp, scale=-0.5).then_inc(S["rs_exp"], 1)
            act.wait_ge(S["beta_add"], 1)
            act.wait_ge(S["a_ready"], 1)
            act.wait_ge(S["set_done"], 1)
            with act.Fori(0, PAIRS) as j:
                act.wait_ge(S["yt_ps"], j + 1)
                act.activation(yT[:, :], ps_t[:, :], ACT.Copy).then_inc(S["yt_sb"], 1)
                act.wait_ge(S["up_ps"], j + 1)
                act.activation(left[:, KC - 1:], ps_up[:, 0:L], ACT.Identity, bias=b_eff[:, 0:1]).then_inc(S["up_sb"], 1)
                act.activation(right[:, :], ps_up[:, L:2 * L], ACT.Identity, bias=b_eff[:, 1:2]).then_inc(S["up_sb"], 1)
                act.wait_ge(S["conv"], j * 3 + 3)
                act.activation(e_c[:, :], c3[:, :], ACT.Exp, scale=-1.0).then_inc(S["conv_exp"], 1)
                act.wait_ge(S["up_sb"], j * 2 + 2)
                act.activation(e_r[:, :], right[:, :], ACT.Exp, scale=-1.0).then_inc(S["right_exp"], 1)
                act.wait_ge(S["nz_ready"], j * 2 + 2)
                act.activation(e_z[:, :], nz[:, :], ACT.Exp).then_inc(S["z_exp"], 1)
                act.wait_ge(S["delta_ready"], j + 1)
                for c in range(NCH):
                    if c >= 2:
                        act.wait_ge(S["scanned"], j * NCH + c - 1)
                    for n in range(CH):
                        k = c * CH + n
                        last = act.activation(dA[:, c % 2, n, 1:], delta[:, 1:], ACT.Exp, scale=a_neg[:, k:k + 1])
                    last.then_inc(S["da_ready"], 1)
                act.wait_ge(S["ve_ready"], j + 2)
                act.activation(lnv2[:, :], ve2[:, :], ACT.Ln).then_inc(S["ve_ln"], 1)
                act.wait_ge(S["ve_ln"], j + 1)
                act.activation(rr[:, 0, :], lnv2[:, :], ACT.Exp, scale=-0.5).then_inc(S["r_ready"], 1)

        @block.vector
        def _(dve):
            dve.memset(dA[:, :, :, 0:1], 0.0)
            dve.memset(left[:, 0:KC - 1], 0.0)
            dve.memset(ones[:, :], 1.0)
            dve.memset(lo_rows[0:DI, :], 0.0)
            dve.memset(lo_rows[DI:P, :], -1.0).then_inc(S["set_done"], 1)
            dve.wait_ge(S["x_in"], 16)
            for t in range(NT):
                last = dve.bn_stats(stats[:, t, :], X[:, PAD + t, :])
            last.then_inc(S["small"], 1)
            dve.wait_ge(S["small"], 1)
            variance(dve, stats, mom, mean, ve, S["small"], 1, S["ve_ready"])
            dve.wait_ge(S["w_in"], 16 * N_IN)
            dve.tensor_scalar(w_up[:, :, :], w_raw[:, :, :], gam[:, 0:1], None, ALU.mult).then_inc(S["w_scaled"], 1)
            for t in range(1, 4):
                last = dve.tensor_copy(bd_row[:, t, :], bd_row[:, 0, :])
            last.then_inc(S["bd_done"], 1)
            dve.wait_ge(S["beta_ps"], 1)
            dve.tensor_tensor(out=b_eff[:, :], in0=ps_up[:, 0:2], in1=b_up[:, :], op=ALU.add).then_inc(S["beta_add"], 1)
            dve.wait_ge(S["a_done"], 1)
            dve.tensor_scalar(a_neg[:, :], a_exp[:, :], -1.0, None, ALU.mult).then_inc(S["a_ready"], 1)
            dve.wait_ge(S["rs_exp"], 1)
            newton(dve, rstd[:, :], ve[:, :], r0[:, :], r1[:, :], lnv[:, :], S["small"], 3)
            with dve.Fori(0, PAIRS) as j:
                for t in range(4):
                    dve.tensor_scalar(y4[:, t, :], X[:, j * 4 + t + PAD, :], mean[:, bass.ds(j * 4 + t, 1)], rstd[:, bass.ds(j * 4 + t, 1)],
                                      ALU.subtract, ALU.mult).then_inc(S["y_ready"], 1)
                dve.wait_ge(S["up_sb"], j * 2 + 1)
                dve.tensor_scalar(c1[:, :], left[:, 2:2 + L], conv_w[:, 2:3], conv_b[:, 0:1], ALU.mult, ALU.add).then_inc(S["conv"], 1)
                dve.wait_ge(S["conv"], j * 3 + 1)
                dve.scalar_tensor_tensor(out=c2[:, :], in0=left[:, 1:1 + L], scalar=conv_w[:, 1:2], in1=c1[:, :],
                                         op0=ALU.mult, op1=ALU.add).then_inc(S["conv"], 1)
                dve.wait_ge(S["conv"], j * 3 + 2)
                dve.scalar_tensor_tensor(out=c3[:, :], in0=left[:, 0:L], scalar=conv_w[:, 0:1], in1=c2[:, :],
                                         op0=ALU.mult, op1=ALU.add).then_inc(S["conv"], 1)
                dve.wait_ge(S["conv_exp"], j + 1)
                dve.tensor_scalar(e_c1[:, :], e_c[:, :], 1.0, None, ALU.add).then_inc(S["usteps"], 1)
                dve.wait_ge(S["usteps"], j * 2 + 1)
                dve.reciprocal(s_c[:, :], e_c1[:, :]).then_inc(S["usteps"], 1)
                dve.wait_ge(S["usteps"], j * 2 + 2)
                dve.tensor_tensor(out=u[:, :], in0=c3[:, :], in1=s_c[:, :], op=ALU.mult).then_inc(S["u_ready"], 1)
                dve.wait_ge(S["z_ps"], j + 1)
                dve.tensor_scalar(z[:, :], ps_zy[:, 0:L], b_dl[:, 0:1], None, ALU.add).then_inc(S["nz_ready"], 1)
                dve.wait_ge(S["nz_ready"], j * 2 + 1)
                dve.scalar_tensor_tensor(out=nz[:, :], in0=z[:, :], scalar=-1.0, in1=z[:, :],
                                         op0=ALU.mult, op1=ALU.min).then_inc(S["nz_ready"], 1)
                dve.wait_ge(S["bc_ps"], j + 1)
                dve.tensor_copy(bc_hi[:, :], ps_bc[:, :]).then_inc(S["zsteps"], 1)
                dve.wait_ge(S["zsteps"], j + 1)
                dve.scalar_tensor_tensor(out=bc[:, :, :].rearrange("p s l -> p (s l)"), in0=bc_hi[:, :].bitcast(F32), scalar=lo_rows[:, 0:1],
                                         in1=ps_bc[:, :], op0=ALU.mult, op1=ALU.add).then_inc(S["bc_ready"], 1)
                dve.wait_ge(S["right_exp"], j + 1)
                dve.tensor_scalar(e_r1[:, :], e_r[:, :], 1.0, None, ALU.add).then_inc(S["gsteps"], 1)
                dve.wait_ge(S["gsteps"], j * 4 + 1)
                dve.reciprocal(s_r[:, :], e_r1[:, :]).then_inc(S["gsteps"], 1)
                dve.wait_ge(S["gsteps"], j * 4 + 2)
                dve.tensor_tensor(out=gate[:, :], in0=right[:, :], in1=s_r[:, :], op=ALU.mult).then_inc(S["gsteps"], 1)
                dve.wait_ge(S["z_exp"], j + 1)
                dve.tensor_scalar(w_z[:, :], e_z[:, :], 2.0, None, ALU.add).then_inc(S["dsteps"], 1)
                dve.wait_ge(S["dsteps"], j * ND + 1)
                dve.reciprocal(s_r[:, :], w_z[:, :]).then_inc(S["rsteps"], 1)
                dve.wait_ge(S["rsteps"], j + 1)
                dve.tensor_tensor(out=s_z[:, :], in0=e_z[:, :], in1=s_r[:, :], op=ALU.mult).then_inc(S["s_ready"], 1)
                dve.wait_ge(S["s_ready"], j + 1)
                dve.tensor_tensor(out=s2[:, :], in0=s_z[:, :], in1=s_z[:, :], op=ALU.mult).then_inc(S["dsteps"], 1)
                dve.wait_ge(S["dsteps"], j * ND + 2)
                dve.tensor_scalar(pz[:, 0, :], s2[:, :], 1.0 / SERIES[0], None, ALU.mult).then_inc(S["dsteps"], 1)
                for k, odd in enumerate(SERIES[1:]):
                    dve.wait_ge(S["dsteps"], j * ND + 3 + k)
                    dve.scalar_tensor_tensor(out=pz[:, (k + 1) % 2, :], in0=pz[:, k % 2, :], scalar=1.0 / odd, in1=s2[:, :],
                                             op0=ALU.add, op1=ALU.mult).then_inc(S["dsteps"], 1)
                dve.wait_ge(S["dsteps"], j * ND + 2 + len(SERIES))
                dve.scalar_tensor_tensor(out=w_m[:, :], in0=pz[:, (len(SERIES) - 1) % 2, :], scalar=1.0, in1=s_z[:, :],
                                         op0=ALU.add, op1=ALU.mult).then_inc(S["dsteps"], 1)
                dve.wait_ge(S["dsteps"], j * ND + ND - 1)
                dve.tensor_scalar(q_z[:, :], w_m[:, :], 2.0, None, ALU.mult).then_inc(S["dsteps"], 1)
                dve.wait_ge(S["dsteps"], j * ND + ND)
                dve.scalar_tensor_tensor(out=delta[:, :], in0=z[:, :], scalar=0.0, in1=q_z[:, :],
                                         op0=ALU.max, op1=ALU.add).then_inc(S["delta_ready"], 1)
                dve.wait_ge(S["delta_ready"], j + 1)
                dve.tensor_tensor(out=du[:, :], in0=delta[:, :], in1=u[:, :], op=ALU.mult).then_inc(S["du_ready"], 1)
                dve.wait_ge(S["du_ready"], j + 1)
                du_b = du[:, :].unsqueeze(1).to_broadcast([P, CH, L])
                for c in range(NCH):
                    dve.wait_ge(S["b_ps"], j * NCH + c + 1)
                    dve.tensor_tensor(out=dB[:, :, :], in0=du_b, in1=ps_b[:, :, :], op=ALU.mult).then_inc(S["db_done"], 1)
                    dve.wait_ge(S["da_ready"], j * NCH + c + 1)
                    dve.wait_ge(S["db_done"], j * NCH + c + 1)
                    dve.tensor_tensor_scan(h[:, :, :].rearrange("p n l -> p (n l)"), dA[:, c % 2, :, :].rearrange("p n l -> p (n l)"),
                                           dB[:, :, :].rearrange("p n l -> p (n l)"), 0.0, ALU.mult, ALU.add).then_inc(S["scanned"], 1)
                    dve.wait_ge(S["c_ps"], j * NCH + c + 1)
                    dve.wait_ge(S["scanned"], j * NCH + c + 1)
                    if c >= 2:
                        dve.wait_ge(S["n_summed"], j * NCH + c - 1)
                    dve.tensor_tensor(out=hC[:, c % 2, :, :], in0=h[:, :, :], in1=ps_c[:, :, :], op=ALU.mult).then_inc(S["hc_done"], 1)
                dve.wait_ge(S["n_summed"], j * NCH + NCH)
                dve.scalar_tensor_tensor(out=y2[:, :], in0=u[:, :], scalar=d_skip[:, 0:1], in1=ps_zy[:, L:2 * L],
                                         op0=ALU.mult, op1=ALU.add).then_inc(S["gsteps"], 1)
                dve.wait_ge(S["gsteps"], j * 4 + 4)
                dve.tensor_tensor(out=gated[:, :], in0=y2[:, :], in1=gate[:, :], op=ALU.mult).then_inc(S["gated_ready"], 1)
                dve.wait_ge(S["o_ps"], j + 1)
                dve.scalar_tensor_tensor(out=xn[:, :, :].rearrange("p t d -> p (t d)"), in0=X[:, bass.ds(j * 4 + PAD, 4), :].rearrange("p t d -> p (t d)"), scalar=2.0,
                                         in1=ps_t[:, :], op0=ALU.mult, op1=ALU.add).then_inc(S["xn_steps"], 1)
                dve.wait_ge(S["xn_steps"], j * 8 + 1)
                for t in range(4):
                    last = dve.bn_stats(st2[:, t, :], xn[:, t, :])
                last.then_inc(S["xn_steps"], 1)
                dve.wait_ge(S["xn_steps"], j * 8 + 2)
                variance(dve, st2, mom2, mean2, ve2, S["xn_steps"], j * 8 + 2, S["ve_ready"])
                dve.wait_ge(S["r_ready"], j + 1)
                newton(dve, rstd2[:, :], ve2[:, :], rr[:, 0, :], rr[:, 1, :], rr[:, 2, :], S["xn_steps"], j * 8 + 4)
                for t in range(4):
                    last = dve.tensor_scalar(X[:, j * 4 + t + PAD, :], xn[:, t, :], mean2[:, t:t + 1], rstd2[:, t:t + 1],
                                             ALU.subtract, ALU.mult)
                last.then_inc(S["x_done"], 1)


H, DK = 16, 8
LK, DC = 1601, 64
KT = -(-LK // P)
KR = LK - (KT - 1) * P
HG, G4 = 4, H // 4
STEPS = G4 * KT
UNITS = 32
BUNITS = G4 * UNITS
AHEAD = UNITS + 7
QUARTER = [(0, 400), (400, 400), (800, 400), (LK - 402, 402)]
KCH = [(c * 512, min(512, LK - c * 512)) for c in range(4)]
SR = 3 * 32

FIRST_ROUNDS = ([("ctx", c) for c in range(4)] + [("x", 0)] + [("k", c) for c in range(4)] + [("q", 0)]
                + [("v", c) for c in range(4)] + [("max", 0)])
ROUNDS = {1: ("norm", 3), 3: ("concat", 0), 5: ("out", 0), 6: ("x", 0), 7: ("q", 0), 8: ("ctx", 0), 9: ("ctx", 1),
          10: ("max", 1), 11: ("ctx", 2), 12: ("ctx", 3), 14: ("k", 0), 15: ("k", 1), 16: ("norm", 0), 17: ("k", 2),
          18: ("k", 3), 20: ("v", 0), 21: ("v", 1), 23: ("max", 2), 24: ("v", 2), 25: ("v", 3), 28: ("norm", 1),
          36: ("max", 3), 41: ("norm", 2), 49: ("max", 4)}
ORDER = [ROUNDS[s] for s in sorted(ROUNDS)]


def first_round(kind, n):
    return FIRST_ROUNDS.index((kind, n)) + 1


def round_of(b, kind, n):
    return b * len(ORDER) + len(FIRST_ROUNDS) + ORDER.index((kind, n)) + 1


def units_at(s):
    return [AHEAD + v for v in range(BUNITS * s // STEPS, BUNITS * (s + 1) // STEPS)]


def attention_stage(nc, a, X, ident):
    with ExitStack() as ctx:
        def sb(name, shape, dt=F32):
            return ctx.enter_context(nc.sbuf_tensor(name, shape, dt))

        def pb(name, shape):
            return ctx.enter_context(nc.psum_tensor(name, shape, F32))

        wq = sb("wq", [P, P])
        wk = sb("wk", [DC, P])
        wv = sb("wv", [DC, P])
        wo = sb("wo", [P, P])
        bq = sb("bq", [P, 1])
        bk = sb("bk", [P, 1])
        bv = sb("bv", [P, P])
        bo = sb("bo", [P, D])
        keys = sb("keys", [P, KT + 1, DC])
        ctxT = sb("ctxT", [DC, LK])
        xs = sb("xs", [P, 2, D])
        xT = sb("xT", [P, L])
        kq = sb("kq", [P, LK + L])
        parts = sb("parts", [P, 2 * (LK + L)], F32R)
        k_lo, q_hi = parts[:, 0:LK], parts[:, LK:LK + L]
        k_hi, q_lo = parts[:, LK + L:2 * LK + L], parts[:, 2 * LK + L:]
        stack = sb("stack", [P, G4, LK + L], F32R)
        qblk = sb("qblk", [P, G4, HG, L], F32R)
        own = sb("own", [SR, HG, 1])
        unit_col = sb("unit_col", [P, 1])
        vn = sb("vn", [P, KT, P])
        V = sb("V", [P, KT, H, 32])
        pT = sb("pT", [P, 2, HG, L])
        mx = sb("mx", [P, 2, 2 * HG, 4])
        neg = sb("neg", [P, 2, 2 * HG])
        negT = sb("negT", [2 * HG, P], F32R)
        oS = sb("oS", [P, L])
        rden = sb("rden", [P, 2, HG])
        cc = sb("cc", [P, 2, H, DK])
        ccT = sb("ccT", [P, L])
        xa = sb("xa", [P, 2, D])
        xb = sb("xb", [P, 2, D])
        st = sb("a_st", [P, 2, 6])
        mom = sb("a_mom", [P, 5, 2])
        mean = sb("a_mean", [P, 2])
        ve = sb("a_ve", [P, 2])
        lnv = sb("a_lnv", [P, 2])
        rr = sb("a_rr", [P, 3, 2])
        rstd = sb("a_rstd", [P, 2])

        ps_s = pb("ps_s", [P, 3, 2, L])
        ps_m = pb("ps_m", [P, 3, 512])
        ps_o = pb("ps_o", [P, 2, L])
        ps_x = pb("ps_x", [P, 512])

        names = ("w_in zero_done set_done own_done scores exps pv units reduced neg_ready bank_full bank_free row_in "
                 "xs_ready parts_ready qblk_ready v_ready keys_in o_copied o_rec xa_done ln_steps ve_ready lnv_done "
                 "r_ready x_done").split()
        S = {n: ctx.enter_context(nc.semaphore("a_" + n)) for n in names}
        stack_in = [ctx.enter_context(nc.semaphore(f"a_stack_in{g}")) for g in range(G4)]
        block = ctx.enter_context(nc.Block())
        N_W = 8
        CREDIT = 2
        CREDIT3 = 3
        LN_STEPS, END_AT = 10, 6
        HALVES = 2 * STEPS

        def released(b, per_batch, n):
            return b * per_batch + n - 3 + 1 + CREDIT3 + (1 if n < 2 else 0)

        def m_buf(w):
            return (w - AHEAD + BUNITS) % BUNITS % 3

        @block.sync
        def _(sp):
            row = lambda v: v.rearrange("(o d) -> o d", o=1)
            col = lambda v: v.rearrange("(p o) -> p o", o=1)
            for dst, src in ((wq[:, :], a["L0_xattn_Wq"]), (wk[:, :], a["L0_xattn_Wk"]), (wv[:, :], a["L0_xattn_Wv"]),
                             (wo[:, :], a["L0_xattn_Wo"]), (bq[:, :], col(a["L0_xattn_bq"])),
                             (bk[:, :], col(a["L0_xattn_bk"])),
                             (bv[:, :], row(a["L0_xattn_bv"]).to_broadcast([P, P])),
                             (bo[:, :], row(a["L0_xattn_bo"]).to_broadcast([P, D]))):
                sp.dma_start(dst, src).then_inc(S["w_in"], 16)

            def load_keys(n):
                c = a["ctx_512"][n, :, :] if isinstance(n, int) else a["ctx_512"][bass.ds(n, 1), :, :].rearrange("o k d -> (o k) d")
                sp.dma_start(keys[:, 0:KT - 1, :], c[0:(KT - 1) * P, :].rearrange("(t p) d -> p t d", p=P)).then_inc(S["keys_in"], 16)
                sp.dma_start(keys[0:KR, KT - 1, :], c[(KT - 1) * P:LK, :]).then_inc(S["keys_in"], 16)

            def fill_stack(n, g):
                stack_w = stack[:, :, :].bitcast(F32)
                rows = slice(32 * g, 32 * g + 32)
                sp.dma_start(stack_w[0:32, g, 0:LK], k_hi[rows, :].bitcast(F32)).then_inc(stack_in[g], 16)
                sp.dma_start(stack_w[0:32, g, LK:], q_hi[rows, :].bitcast(F32)).then_inc(stack_in[g], 16)
                sp.dma_start(stack_w[32:64, g, :], parts[rows, 0:LK + L].bitcast(F32)).then_inc(stack_in[g], 16)
                sp.dma_start(stack_w[64:96, g, :], parts[rows, LK + L:].bitcast(F32)).then_inc(stack_in[g], 16)

            def fill_row(rounds, g):
                sp.wait_ge(S["bank_free"], rounds)
                sp.dma_start(qblk[SR:SR + 1, g, :, :].rearrange("o h l -> o (h l)").bitcast(F32), negT[:, :].bitcast(F32)).then_inc(S["row_in"], 16)

            load_keys(0)
            sp.wait_ge(S["bank_full"], first_round("ctx", 3))
            load_keys(1)
            sp.wait_ge(S["parts_ready"], 4)
            for g in range(G4):
                fill_stack(0, g)
            fill_row(first_round("max", 0), 0)
            with sp.Fori(0, NB) as b:
                fill_row_at = lambda k: fill_row(round_of(b, "max", k), k % G4)
                fill_row_at(1)
                sp.wait_ge(S["bank_full"], round_of(b, "ctx", 3))
                load_keys(nc_mod(sp, b + 2))
                fill_row_at(2)
                sp.wait_ge(S["parts_ready"], b * 4 + 8)
                fill_stack(b + 1, 0)
                sp.wait_ge(S["scores"], b * HALVES + 4 * KT)
                fill_stack(b + 1, 1)
                fill_row_at(3)
                sp.wait_ge(S["scores"], b * HALVES + 6 * KT)
                fill_stack(b + 1, 2)
                fill_row_at(4)
                sp.wait_ge(S["scores"], b * HALVES + 8 * KT)
                fill_stack(b + 1, 3)
            for g in range(G4):
                sp.wait_ge(stack_in[g], 64 * (NB + 1))
            sp.wait_ge(S["row_in"], 16 * (G4 * NB + 1))
            sp.wait_ge(S["keys_in"], 32 * (NB + 2))

        @block.gpsimd
        def _(pool):
            pool.memset(own[:, :, :], 0.0).then_inc(S["own_done"], 1)
            pool.wait_ge(S["own_done"], 1)
            for part in range(3):
                v = own[32 * part:32 * part + 32, :, 0]
                pool.affine_select(out=v, in_=v, compare_op=ALU.is_gt, fill=1.0, base=0,
                                   pattern=[[DK, HG]], channel_multiplier=-1).then_inc(S["own_done"], 1)
                pool.wait_ge(S["own_done"], 2 + 2 * part)
                pool.affine_select(out=v, in_=v, compare_op=ALU.is_gt, fill=0.0, base=DK,
                                   pattern=[[DK, HG]], channel_multiplier=-1).then_inc(S["own_done"], 1)
                pool.wait_ge(S["own_done"], 3 + 2 * part)
            pool.wait_ge(S["set_done"], 1)

            def copy_x(n, count):
                src = X[:, PAD:PAD + 2, :] if isinstance(n, int) else X[:, bass.ds(n * 2 + PAD, 2), :]
                pool.tensor_tensor(out=xs[:, :, :], in0=src, in1=unit_col[:, 0:1].unsqueeze(2).to_broadcast([P, 2, D]),
                                   op=ALU.mult).then_inc(S["xs_ready"], 1)
                pool.wait_ge(S["xs_ready"], count)

            def split(base):
                for n, (dst, src, hi) in enumerate((
                    (k_hi, kq[:, 0:LK], None), (q_hi, kq[:, LK:], None),
                    (k_lo, kq[:, 0:LK], k_hi), (q_lo, kq[:, LK:], q_hi),
                )):
                    if hi is None:
                                pool.tensor_tensor(out=dst, in0=src, in1=unit_col[:, 0:1].to_broadcast([P, src.shape[1]]), op=ALU.mult).then_inc(S["parts_ready"], 1)
                    else:
                        pool.tensor_tensor(out=dst, in0=src, in1=hi.bitcast(F32), op=ALU.subtract).then_inc(S["parts_ready"], 1)
                    pool.wait_ge(S["parts_ready"], base + n + 1)

            def spread_q(g, count):
                pool.tensor_tensor(out=qblk[0:SR, g, :, :], in0=stack[0:SR, g, LK:].bitcast(F32).unsqueeze(1).to_broadcast([SR, HG, L]),
                                   in1=own[:, :, :].to_broadcast([SR, HG, L]), op=ALU.mult).then_inc(S["qblk_ready"], 1)
                pool.wait_ge(S["qblk_ready"], count)

            def spread_v(g, count):
                heads = slice(HG * g, HG * g + HG)
                cols = slice(32 * g, 32 * g + 32)
                b_v = bv[:, cols].rearrange("p (h d) -> p h d", d=DK)
                for t0, t1, p in ((0, KT - 1, P), (KT - 1, KT, KR)):
                    for t in range(t0, t1):
                        pool.tensor_tensor(out=V[0:p, t, heads, 0:DK], in0=vn[0:p, t, cols].rearrange("p (h d) -> p h d", d=DK),
                                           in1=b_v[0:p], op=ALU.add).then_inc(S["v_ready"], 1)
                pool.wait_ge(S["v_ready"], count)

            copy_x(0, 1)
            pool.wait_ge(S["bank_free"], first_round("q", 0))
            split(0)
            pool.wait_ge(S["bank_free"], first_round("v", 3))
            for g in range(G4):
                pool.wait_ge(stack_in[g], 64)
                spread_q(g, g + 1)
                spread_v(g, KT * (g + 1))
            with pool.Fori(0, NB) as b:
                pool.wait_ge(S["bank_full"], b * len(ORDER) + len(FIRST_ROUNDS))
                copy_x(nc_mod(pool, b + 1), b + 2)
                for g in range(G4):
                    pool.wait_ge(stack_in[g], b * 64 + 64)
                pool.wait_ge(S["bank_free"], round_of(b, "k", 3))
                split(b * 4 + 4)
                pool.wait_ge(S["bank_free"], round_of(b, "v", 3))
                for g in range(G4):
                    pool.wait_ge(stack_in[g], b * 64 + 128)
                    pool.wait_ge(S["scores"], b * HALVES + 2 * KT * (g + 1))
                    spread_q(g, b * 4 + g + 5)
                    pool.wait_ge(S["pv"], b * STEPS + KT * (g + 1) + CREDIT)
                    spread_v(g, b * (4 * KT) + KT * (g + 5))

        @block.tensor
        def _(pe):
            pe.wait_ge(S["w_in"], 16 * N_W)
            pe.wait_ge(S["set_done"], 1)
            pe.sem_inc(S["pv"], CREDIT)

            def bank_round(kind, n, rounds, b):
                if not (isinstance(rounds, int) and rounds == 1):
                    pe.wait_ge(S["bank_free"], rounds - 1)
                if kind == "ctx":
                    if n == 0:
                        pe.wait_ge(S["keys_in"], 32 if b is None else b * 32 + 64)
                    for i, t in enumerate(range(4 * n, min(4 * n + 4, KT))):
                        r = P if t < KT - 1 else KR
                        w = 1 if i else 2
                        last = pe.transpose(ps_x[0:w * DC, P * i:P * i + r], keys[0:r, t:t + w, :].rearrange("p t d -> p (t d)"), ident[0:r, 0:r])
                elif kind == "x":
                    pe.wait_ge(S["xs_ready"], 1 if b is None else b + 2)
                    for t in range(2):
                        last = pe.transpose(ps_x[:, P * t:P * t + P], xs[:, t, :], ident[:, :])
                elif kind == "k":
                    k0, w = KCH[n]
                    last = pe.matmul(ps_x[:, 0:w], wk[:, :], ctxT[:, k0:k0 + w], start=True, stop=True)
                elif kind == "q":
                    last = pe.matmul(ps_x[:, 0:L], wq[:, :], xT[:, :], start=True, stop=True)
                elif kind == "v":
                    for i, t in enumerate(range(4 * n, min(4 * n + 4, KT))):
                        r = P if t < KT - 1 else KR
                        last = pe.matmul(ps_x[0:r, P * i:P * i + P], ctxT[:, P * t:P * t + r], wv[:, :], start=True, stop=True)
                elif kind == "max":
                    pe.wait_ge(S["neg_ready"], 1 if b is None else b * G4 + n + 1)
                    last = pe.transpose(ps_x[0:2 * HG, 0:P], neg[:, n % 2, :], ident[:, :])
                elif kind == "norm":
                    pe.wait_ge(S["o_copied"], (b * G4 if n == 3 else b * G4 + n + 1) + CREDIT)
                    for t in range(2):
                        last = pe.transpose(ps_x[:, P * t:P * t + P], oS[:, P * t:P * t + P], ident[:, :])
                elif kind == "concat":
                    for t in range(2):
                        last = pe.transpose(ps_x[:, P * t:P * t + P], cc[:, t, :, :].rearrange("p h d -> p (h d)"), ident[:, :])
                elif kind == "out":
                    for t in range(2):
                        last = pe.matmul(ps_x[:, D * t:D * t + D], ccT[:, P * t:P * t + P], wo[:, :], start=True, stop=True)
                last.then_inc(S["bank_full"], 1)

            def unit(w, b):
                g, u = w // UNITS % G4, w % UNITS
                head, tile, quarter = u // 8, u // 4 % 2, u % 4
                k0, cols = QUARTER[quarter]
                if u == 0:
                    pe.wait_ge(S["qblk_ready"], b * G4 + w // UNITS + 1)
                pe.wait_ge(S["reduced"], w + 1 if w < AHEAD else released(b, BUNITS, w - AHEAD) + AHEAD)
                pe.matmul(ps_m[:, m_buf(w), 0:cols], qblk[0:SR, g, head, P * tile:P * tile + P], stack[0:SR, g, k0:k0 + cols],
                          start=True, stop=True).then_inc(S["units"], 1)

            def attend(b, g, kt):
                s = KT * g + kt
                r = P if kt < KT - 1 else KR
                if kt == 0:
                    pe.wait_ge(S["v_ready"], b * (4 * KT) + KT * (g + 1))
                    pe.wait_ge(S["o_copied"], b * G4 + g + CREDIT)
                pe.wait_ge(S["exps"], b * HALVES + 2 * s + 2 + CREDIT3)
                for h in range(HG):
                    last = pe.matmul(ps_o[32 * h:32 * h + 32, g % 2, :], V[0:r, kt, HG * g + h, :], pT[0:r, s % 2, h, :],
                                     start=(kt == 0), stop=(kt == KT - 1))
                last.then_inc(S["pv"], 1)

            for kind, n in FIRST_ROUNDS[:-1]:
                bank_round(kind, n, first_round(kind, n), None)
            for w in range(AHEAD):
                unit(w, 0)
                if w == UNITS:
                    bank_round("max", 0, first_round("max", 0), None)
            with pe.Fori(0, NB) as b:
                for s in range(STEPS):
                    g, kt = s // KT, s % KT
                    r = P if kt < KT - 1 else KR
                    if kt == 0:
                        pe.wait_ge(S["row_in"], b * (16 * G4) + 16 * (g + 1))
                    todo = units_at(s)
                    for i in range(2):
                        half = 2 * s + i
                        pe.wait_ge(S["exps"], released(b, HALVES, half))
                        pe.matmul(ps_s[0:r, half % 3, :, :], stack[0:SR + 1, g, P * kt:P * kt + r],
                                  qblk[0:SR + 1, g, 2 * i:2 * i + 2, :], start=True, stop=True).then_inc(S["scores"], 1)
                        if todo:
                            unit(todo.pop(0), b)
                    if s:
                        attend(b, (s - 1) // KT, (s - 1) % KT)
                    for w in todo:
                        unit(w, b)
                    if s in ROUNDS:
                        kind, n = ROUNDS[s]
                        bank_round(kind, n, round_of(b, kind, n), b)
                attend(b, G4 - 1, KT - 1)
            for kind, n in ORDER[:3]:
                bank_round(kind, n, round_of(NB, kind, n), NB)

        @block.scalar
        def _(act):
            act.preload_act_table_set("natural_log_exp_and_others")
            act.wait_ge(S["w_in"], 16 * N_W)
            act.wait_ge(S["set_done"], 1)
            act.sem_inc(S["exps"], CREDIT3)
            act.sem_inc(S["o_copied"], CREDIT)

            def drain(kind, n, rounds, b):
                if kind not in ("ctx", "x", "k", "q", "v", "concat"):
                    return
                if kind == "v" and n == 0 and b is not None:
                    act.wait_ge(S["v_ready"], b * (4 * KT) + 4 * KT)
                act.wait_ge(S["bank_full"], rounds)
                if kind == "ctx":
                    k0, w = KCH[n]
                    last = act.activation(ctxT[:, k0:k0 + w], ps_x[0:DC, 0:w], ACT.Copy)
                elif kind == "x":
                    last = act.activation(xT[:, :], ps_x[:, 0:L], ACT.Copy)
                elif kind == "k":
                    k0, w = KCH[n]
                    last = act.activation(kq[:, k0:k0 + w], ps_x[:, 0:w], ACT.Identity, bias=bk[:, 0:1])
                elif kind == "q":
                    last = act.activation(kq[:, LK:], ps_x[:, 0:L], ACT.Identity, bias=bq[:, 0:1])
                elif kind == "v":
                    if n < 3:
                        last = act.activation(vn[:, 4 * n:4 * n + 4, :].rearrange("p t c -> p (t c)"), ps_x[:, :], ACT.Copy)
                    else:
                        last = act.activation(vn[0:KR, KT - 1, :], ps_x[0:KR, 0:P], ACT.Copy)
                elif kind == "concat":
                    last = act.activation(ccT[:, :], ps_x[:, 0:L], ACT.Copy)
                last.then_inc(S["bank_free"], 1)

            def copy_o(b, g):
                act.wait_ge(S["pv"], b * STEPS + KT * (g + 1) + CREDIT)
                act.wait_ge(S["bank_full"], round_of(b, "out", 0) if g == 0 else round_of(b, "norm", g - 1))
                act.activation(oS[:, :], ps_o[:, g % 2, :], ACT.Copy).then_inc(S["o_copied"], 1)

            def root(b):
                act.wait_ge(S["ln_steps"], b * LN_STEPS + 5)
                act.activation(lnv[:, :], ve[:, :], ACT.Ln).then_inc(S["lnv_done"], 1)
                act.wait_ge(S["lnv_done"], b + 1)
                act.activation(rr[:, 0, :], lnv[:, :], ACT.Exp, scale=-0.5).then_inc(S["r_ready"], 1)

            for kind, n in FIRST_ROUNDS[:-1]:
                drain(kind, n, first_round(kind, n), None)
            with act.Fori(0, NB) as b:
                for s in range(STEPS):
                    kt = s % KT
                    r = P if kt < KT - 1 else KR
                    act.wait_ge(S["pv"], b * STEPS + s + 1)
                    for i in range(2):
                        half = 2 * s + i
                        act.wait_ge(S["scores"], b * HALVES + half + 1)
                        act.activation(pT[0:r, s % 2, 2 * i:2 * i + 2, :], ps_s[0:r, half % 3, :, :], ACT.Exp,
                                       scale=DK ** -0.5).then_inc(S["exps"], 1)
                    if kt == 0 and s:
                        copy_o(b, s // KT - 1)
                    if s == END_AT + 4:
                        root(b)
                    if s in ROUNDS:
                        kind, n = ROUNDS[s]
                        drain(kind, n, round_of(b, kind, n), b)
                copy_o(b, G4 - 1)
            for kind, n in ORDER[:3]:
                drain(kind, n, round_of(NB, kind, n), NB)
            root(NB)

        @block.vector
        def _(dve):
            dve.memset(V[:, :, :, :].rearrange("p t h c -> p (t h c)"), 0.0).then_inc(S["zero_done"], 1)
            dve.memset(oS[:, :], 1.0)
            dve.memset(unit_col[:, :], 1.0)
            dve.memset(keys[:, KT, :], 0.0)
            dve.memset(X[:, 0:PAD, :], 0.0)
            dve.wait_ge(S["zero_done"], 1)
            dve.memset(V[:, :, :, DK:DK + 1], 1.0)
            for g in range(G4):
                dve.memset(stack[SR:SR + 1, g, 0:LK].bitcast(F32), 1.0)
            dve.sem_inc(S["reduced"], CREDIT3)
            dve.memset(cc[:, :, :, :], 1.0).then_inc(S["set_done"], 1)
            dve.wait_ge(S["set_done"], 1)

            def reduce(w, b):
                par, u = w // UNITS % 2, w % UNITS
                quarter = u % 4
                dve.wait_ge(S["units"], b * BUNITS + w + 1)
                dve.reduce_max(mx[:, par, u // 4, quarter:quarter + 1], ps_m[:, m_buf(w), 0:QUARTER[quarter][1]], AX.X).then_inc(S["reduced"], 1)
                if u == UNITS - 1:
                    dve.wait_ge(S["reduced"], b * BUNITS + w + 1 + CREDIT3)
                    dve.tensor_reduce(out=neg[:, par, :], in_=mx[:, par, :, :], op=ALU.max, axis=AX.X, negate=True).then_inc(S["neg_ready"], 1)

            def drain(kind, n, rounds, b):
                if kind not in ("max", "norm", "out"):
                    return
                if kind == "max" and b is not None:
                    dve.wait_ge(S["row_in"], b * (16 * G4) + 16 * n)
                dve.wait_ge(S["bank_full"], rounds)
                if kind == "max":
                    dve.tensor_copy(negT[:, :], ps_x[0:2 * HG, 0:P]).then_inc(S["bank_free"], 1)
                elif kind == "norm":
                    v = ps_x[:, 0:L].rearrange("p (t h c) -> p t h c", t=2, h=HG)
                    dve.reciprocal(rden[:, :, :], v[:, :, :, DK]).then_inc(S["o_rec"], 1)
                    dve.wait_ge(S["o_rec"], b * G4 + (1 if n == 3 else n + 2))
                    dve.tensor_tensor(out=cc[:, :, HG * n:HG * n + HG, :], in0=v[:, :, :, 0:DK],
                                      in1=rden[:, :, :].unsqueeze(3).to_broadcast([P, 2, HG, DK]), op=ALU.mult).then_inc(S["bank_free"], 1)
                elif kind == "out":
                    tiles = X[:, bass.ds(b * 2, 2), :] if not isinstance(b, int) else X[:, 2 * b:2 * b + 2, :]
                    dve.tensor_tensor(out=xa[:, :, :], in0=tiles, in1=ps_x[:, 0:L].rearrange("p (t d) -> p t d", t=2),
                                      op=ALU.add).then_inc(S["bank_free"], 1)

            def end_batch(b, n):
                steps = S["ln_steps"]
                base = b * LN_STEPS + n
                if n:
                    dve.wait_ge(steps, base)
                if n == 0:
                    dve.wait_ge(S["bank_free"], round_of(b, "out", 0))
                    last = dve.tensor_tensor(out=xb[:, :, :], in0=xa[:, :, :], in1=bo[:, :].unsqueeze(1).to_broadcast([P, 2, D]), op=ALU.add)
                elif n == 1:
                    for t in range(2):
                        last = dve.bn_stats(st[:, t, :], xb[:, t, :])
                elif n == 2:
                    dve.tensor_tensor(out=mom[:, 0, :], in0=st[:, :, 1], in1=st[:, :, 4], op=ALU.add)
                    dve.tensor_tensor(out=mom[:, 1, :], in0=st[:, :, 1], in1=st[:, :, 4], op=ALU.subtract)
                    last = dve.tensor_tensor(out=mom[:, 2, :], in0=st[:, :, 2], in1=st[:, :, 5], op=ALU.add)
                elif n == 3:
                    dve.tensor_scalar(mean[:, :], mom[:, 0, :], 0.5, None, ALU.mult)
                    dve.tensor_tensor(out=mom[:, 3, :], in0=mom[:, 1, :], in1=mom[:, 1, :], op=ALU.mult)
                    last = dve.tensor_scalar(mom[:, 4, :], mom[:, 2, :], 1.0 / D, EPS, ALU.mult, ALU.add)
                elif n == 4:
                    last = dve.scalar_tensor_tensor(out=ve[:, :], in0=mom[:, 3, :], scalar=0.25, in1=mom[:, 4, :],
                                                    op0=ALU.mult, op1=ALU.add)
                elif n == 5:
                    dve.wait_ge(S["r_ready"], b + 1)
                    last = dve.tensor_tensor(out=rr[:, 1, :], in0=rr[:, 0, :], in1=rr[:, 0, :], op=ALU.mult)
                elif n == 6:
                    last = dve.tensor_tensor(out=rr[:, 2, :], in0=rr[:, 1, :], in1=ve[:, :], op=ALU.mult)
                elif n == 7:
                    last = dve.tensor_scalar(rr[:, 1, :], rr[:, 2, :], -0.5, 1.5, ALU.mult, ALU.add)
                elif n == 8:
                    last = dve.tensor_tensor(out=rstd[:, :], in0=rr[:, 0, :], in1=rr[:, 1, :], op=ALU.mult)
                elif n == 9:
                    for t in range(2):
                        last = dve.tensor_scalar(X[:, b * 2 + t, :], xb[:, t, :], mean[:, t:t + 1], rstd[:, t:t + 1], ALU.subtract, ALU.mult)
                last.then_inc(steps, 1)

            for w in range(AHEAD):
                reduce(w, 0)
                if w == UNITS:
                    drain("max", 0, first_round("max", 0), None)
            with dve.Fori(0, NB) as b:
                for s in range(STEPS):
                    for w in units_at(s):
                        reduce(w, b)
                    if s in ROUNDS:
                        kind, n = ROUNDS[s]
                        drain(kind, n, round_of(b, kind, n), b)
                    if END_AT <= s < END_AT + LN_STEPS:
                        end_batch(b, s - END_AT)
            for kind, n in ORDER[:3]:
                drain(kind, n, round_of(NB, kind, n), NB)
            for n in range(LN_STEPS):
                end_batch(NB, n)


def nc_mod(eng, n):
    return n % NB


UT = 3
BODY = 6
GT = 4


def experts_stage(nc, a, X, ident, pre, out):
    assert (TE - UT) % BODY == 0 and BODY % UT == 0 and BODY % 2 == 0
    with ExitStack() as ctx:
        def sb(name, shape, dt=F32):
            return ctx.enter_context(nc.sbuf_tensor(name, shape, dt))

        def pb(name, shape):
            return ctx.enter_context(nc.psum_tensor(name, shape, F32))

        x_slots, w1, w2, b_parts = pre.x_slots, pre.w1, pre.w2, pre.b_parts
        y_slots = nc.dram_tensor("y_slots", (TE * P, D), F32, kind="Internal").ap()

        b1 = sb("b1", [2, E, 2 * HID], F32R)
        b2 = sb("b2", [2, E, D], F32R)
        two0 = sb("two0", [2, P])
        two = sb("two", [2, P], F32R)
        wr = sb("wr", [P, E])
        br = sb("br", [P, E])
        tri = sb("tri", [P, P])
        allone = sb("allone", [P, P])
        numi = sb("numi", [P, 64], I32)
        num = sb("num", [P, 64])
        xTr = sb("xTr", [P, 2, 4 * P])
        lg = sb("lg", [P, E, NT])
        best = sb("best", [P, NT])
        hit = sb("hit", [P, E, NT])
        first = sb("first", [P, NT])
        oh = sb("oh", [P, E, NT])
        more = sb("more", [P, E, NT])
        tot = sb("tot", [P, E, NT])
        incl = sb("incl", [P, E, NT])
        place = sb("place", [P, E, NT])
        full = sb("full", [P, E, NT])
        nt = sb("nt", [P, E])
        end = sb("end", [P, E])
        start = sb("start", [P, E])
        slotf = sb("slotf", [P, NT])
        slot = sb("slot", [P, NT], I32)
        past = sb("past", [P, TE, E])
        idf = sb("idf", [P, TE])
        tile_expert = sb("tile_expert", [P, TE], I32)
        xt = sb("xt", [P, UT, D])
        xT = sb("e_xT", [P, UT, P])
        sg = sb("sg", [P, UT, HID])
        act_ = sb("act_", [P, UT, HID])
        aT = sb("aT", [P, UT, HID // P, P])
        yt = sb("yt", [P, UT, D])
        Y = sb("Y", [P, NT, D])
        stt = sb("e_st", [P, NT, 6])
        mom = sb("e_mom", [P, 5, NT])
        mean = sb("e_mean", [P, NT])
        ve = sb("e_ve", [P, NT])
        lnv = sb("e_lnv", [P, NT])
        rr = sb("e_rr", [P, 3, NT])
        rstd = sb("e_rstd", [P, NT])

        ps_t = pb("e_ps_t", [P, 2, 512])
        ps_h = pb("e_ps_h", [P, 2, 2, HID])
        ps_y = pb("e_ps_y", [P, 512])
        ps_l = pb("e_ps_l", [P, 512])

        names = ("w_in b_in consts set_done xtr_ps xtr_sb logits steps oh_ready counts "
                 "slots_ready scattered xt_in xt_ps xt_sb h_ps sg_done act_done at_ps at_sb y_ps y_sb y_out "
                 "yt_free sums stats_done ve_ready lnv_done r_ready z_done out_done").split()
        S = {n: ctx.enter_context(nc.semaphore("e_" + n)) for n in names}
        gathered = [ctx.enter_context(nc.semaphore(f"e_gathered{g}")) for g in range(NT // GT)]
        xt_in = [ctx.enter_context(nc.semaphore(f"e_xt_in{g}")) for g in range(UT)]
        y_out = [ctx.enter_context(nc.semaphore(f"e_y_out{g}")) for g in range(UT)]
        block = ctx.enter_context(nc.Block())

        @block.sync
        def _(sp):
            row = lambda v: v.rearrange("(o d) -> o d", o=1)
            sp.dma_start(wr[:, :], a["L0_ffn_router_w"]).then_inc(S["w_in"], 16)
            sp.dma_start(br[:, :], row(a["L0_ffn_router_b"]).to_broadcast([P, E])).then_inc(S["w_in"], 16)
            for part in range(2):
                for dst, c0, c1 in ((b1, 0, BC1), (b2, BC1, BC)):
                    sp.dma_start(dst[part:part + 1, :, :].rearrange("o e n -> o (e n)").bitcast(F32),
                                 b_parts[:, part, c0:c1].bitcast(F32)).then_inc(S["b_in"], 16)
            sp.wait_ge(S["scattered"], 16 * NT)
            for k in range(UT):
                sp.dma_start(xt[:, k, :], x_slots[P * k:P * k + P, :]).then_inc(xt_in[k], 16)
                sp.sem_inc(y_out[k], 16)

            def load(n, k):
                sp.wait_ge(S["xt_ps"], n + 1)
                sp.dma_start(xt[:, k, :], x_slots[bass.ds(((n + UT) % TE) * P, P), :]).then_inc(xt_in[k], 16)

            def store(n, k):
                sp.wait_ge(S["y_sb"], n + 1)
                sp.dma_start(y_slots[bass.ds(n * P, P), :], yt[:, k, :]).then_inc(y_out[k], 16)

            for n in range(UT):
                load(n, n)
                if n >= 2:
                    store(n - 2, n - 2)
            with sp.Fori(0, (TE - UT) // BODY) as i:
                for m in range(BODY):
                    n = i * BODY + UT + m
                    load(n, m % UT)
                    store(n - 2, (m - 2) % UT)
            for n in (TE - 2, TE - 1):
                store(n, n % UT)
            for k in range(UT):
                sp.wait_ge(xt_in[k], 16 * (TE // UT + 1))
            for g in range(NT // GT):
                sp.wait_ge(S["z_done"], g + 1)
                sp.dma_start(tokens(out)[:, GT * g:GT * g + GT, :], Y[:, GT * g:GT * g + GT, :]).then_inc(S["out_done"], 16)
            sp.wait_ge(S["out_done"], 16 * (NT // GT))

        @block.gpsimd
        def _(pool):
            pool.iota(numi[:, :], pattern=[[1, 64]], base=0, channel_multiplier=0).then_inc(S["consts"], 1)
            pool.wait_ge(S["consts"], 1)
            pool.memset(tri[:, :], 1.0).then_inc(S["consts"], 1)
            pool.wait_ge(S["consts"], 2)
            pool.affine_select(out=tri[:, :], in_=tri[:, :], compare_op=ALU.is_gt, fill=0.0, base=0,
                               pattern=[[1, P]], channel_multiplier=-1).then_inc(S["consts"], 1)
            pool.wait_ge(pre.sems["slots_zeroed"], 64)
            pool.wait_ge(S["slots_ready"], 1)
            for t in range(NT):
                pool.indirect_dma_start(x_slots[:, :], bass.IndirectOffsetOnAxis(ap=slot[:, t:t + 1], axis=0),
                                        X[:, PAD + t, :], None).then_inc(S["scattered"], 16)
            for k in range(UT):
                pool.wait_ge(y_out[k], 16 * (TE // UT + 1))
            for t in range(NT):
                pool.indirect_dma_start(Y[:, t, :], None, y_slots[:, :],
                                        bass.IndirectOffsetOnAxis(ap=slot[:, t:t + 1], axis=0)).then_inc(gathered[t // GT], 16)

        @block.tensor
        def _(pe):
            pe.wait_ge(S["w_in"], 32)
            for r in range(NT // 4):
                if r >= 2:
                    pe.wait_ge(S["xtr_sb"], r - 1)
                for t in range(4):
                    last = pe.transpose(ps_t[:, r % 2, P * t:P * t + P], X[:, PAD + 4 * r + t, :], ident[:, :])
                last.then_inc(S["xtr_ps"], 1)
                pe.wait_ge(S["xtr_sb"], r + 1)
                for t in range(4):
                    c = (4 * r + t) * E
                    last = pe.matmul(ps_l[:, c:c + E], xTr[:, r % 2, P * t:P * t + P], wr[:, :], start=True, stop=True)
                last.then_inc(S["logits"], 1)
            pe.wait_ge(S["consts"], 3)
            pe.wait_ge(S["set_done"], 1)
            pe.wait_ge(S["oh_ready"], 1)
            ohf = oh[:, :, :].rearrange("p e t -> p (e t)")
            pe.matmul(ps_l[:, 0:E * NT], tri[:, :], ohf, start=True, stop=True)
            pe.matmul(ps_l[:, E * NT:], allone[:, :], ohf, start=True, stop=True).then_inc(S["counts"], 1)
            pe.wait_ge(pre.sems["weights_in"], 16 * 2 * E)
            pe.wait_ge(S["b_in"], 64)
            pe.wait_ge(S["slots_ready"], 1)

            def expert(n):
                return pe.value_load(tile_expert[0:1, bass.ds(n, 1)], min_val=0, max_val=E - 1)

            def turn_x(n, k, loads):
                pe.wait_ge(xt_in[k], loads)
                pe.transpose(ps_t[:, 0, 0:P], xt[:, k, :], ident[:, :]).then_inc(S["xt_ps"], 1)

            def up(n, k, h, first):
                e = expert(n)
                pe.wait_ge(S["xt_sb"], n + 1)
                if not first:
                    pe.wait_ge(S["act_done"], n - 1)
                for c in range(2):
                    cols = slice(HID * c, HID * c + HID)
                    pe.matmul(ps_h[:, h, c, :], two[:, :], b1[:, bass.ds(e, 1), cols], start=True, stop=False)
                    last = pe.matmul(ps_h[:, h, c, :], xT[:, k, :], w1[:, bass.ds(e, 1), cols], start=False, stop=True)
                last.then_inc(S["h_ps"], 1)

            def turn_act(n, k, first):
                pe.wait_ge(S["act_done"], n + 1)
                if not first:
                    pe.wait_ge(S["at_sb"], n)
                for j in range(HID // P):
                    last = pe.transpose(ps_t[:, 1, P * j:P * j + P], act_[:, k, P * j:P * j + P], ident[:, :])
                last.then_inc(S["at_ps"], 1)

            def down(n, k, first):
                e = expert(n)
                pe.wait_ge(S["at_sb"], n + 1)
                if not first:
                    pe.wait_ge(S["y_sb"], n)
                pe.matmul(ps_y[:, 0:D], two[:, :], b2[:, bass.ds(e, 1), :], start=True, stop=False)
                for j in range(HID // P):
                    last = pe.matmul(ps_y[:, 0:D], aT[:, k, j, :], w2[:, bass.ds(e, 1), j, :], start=False, stop=(j == HID // P - 1))
                last.then_inc(S["y_ps"], 1)

            turn_x(0, 0, 16)
            for n in range(UT):
                up(n, n, n % 2, n < 2)
                if n >= 1:
                    turn_act(n - 1, n - 1, n == 1)
                turn_x(n + 1, (n + 1) % UT, 16 * ((n + 1) // UT + 1))
                if n >= 2:
                    down(n - 2, n - 2, n == 2)
            with pe.Fori(0, (TE - UT) // BODY) as i:
                for m in range(BODY):
                    n = i * BODY + UT + m
                    up(n, m % UT, (UT + m) % 2, False)
                    turn_act(n - 1, (m - 1) % UT, False)
                    turn_x(n + 1, (m + 1) % UT, i * (16 * BODY // UT) + 16 * ((m + 1) // UT + 2))
                    down(n - 2, (m - 2) % UT, False)
            turn_act(TE - 1, (TE - 1) % UT, False)
            down(TE - 2, (TE - 2) % UT, False)
            down(TE - 1, (TE - 1) % UT, False)

        @block.scalar
        def _(act):
            for r in range(NT // 4):
                act.wait_ge(S["xtr_ps"], r + 1)
                if r >= 2:
                    act.wait_ge(S["logits"], r - 1)
                act.activation(xTr[:, r % 2, :], ps_t[:, r % 2, :], ACT.Copy).then_inc(S["xtr_sb"], 1)
            act.preload_act_table(ACT.Sigmoid)

            def x_copy(n, k):
                act.wait_ge(S["xt_ps"], n + 1)
                act.activation(xT[:, k, :], ps_t[:, 0, 0:P], ACT.Copy).then_inc(S["xt_sb"], 1)

            def gate(n, k, h):
                act.wait_ge(S["h_ps"], n + 1)
                act.activation(sg[:, k, :], ps_h[:, h, 1, :], ACT.Sigmoid).then_inc(S["sg_done"], 1)

            def act_copy(n, k):
                act.wait_ge(S["at_ps"], n + 1)
                act.activation(aT[:, k, :, :].rearrange("p j t -> p (j t)"), ps_t[:, 1, :], ACT.Copy).then_inc(S["at_sb"], 1)

            x_copy(0, 0)
            for n in range(UT):
                gate(n, n, n % 2)
                if n >= 1:
                    act_copy(n - 1, n - 1)
                x_copy(n + 1, (n + 1) % UT)
            with act.Fori(0, (TE - UT) // BODY) as i:
                for m in range(BODY):
                    n = i * BODY + UT + m
                    gate(n, m % UT, (UT + m) % 2)
                    act_copy(n - 1, (m - 1) % UT)
                    x_copy(n + 1, (m + 1) % UT)
            act_copy(TE - 1, (TE - 1) % UT)
            act.preload_act_table_set("natural_log_exp_and_others")
            for g in range(NT // GT):
                act.wait_ge(S["ve_ready"], g + 1)
                act.activation(lnv[:, GT * g:GT * g + GT], ve[:, GT * g:GT * g + GT], ACT.Ln).then_inc(S["lnv_done"], 1)
                act.wait_ge(S["lnv_done"], g + 1)
                act.activation(rr[:, 0, GT * g:GT * g + GT], lnv[:, GT * g:GT * g + GT], ACT.Exp, scale=-0.5).then_inc(S["r_ready"], 1)

        @block.vector
        def _(dve):
            steps = [0]

            def link(ins):
                steps[0] += 1
                ins.then_inc(S["steps"], 1)
                dve.wait_ge(S["steps"], steps[0])

            def over(v):
                return v.unsqueeze(1).to_broadcast([P, E, NT])

            def along(v):
                return v.unsqueeze(2).to_broadcast([P, E, NT])

            dve.memset(allone[:, :], 1.0)
            dve.memset(two0[:, :], 1.0)
            link(dve.memset(more[:, :, :], 1.0))
            dve.memset(more[:, :, 0:1], 0.0)
            dve.tensor_copy(two[:, :], two0[:, :]).then_inc(S["set_done"], 1)
            dve.wait_ge(S["consts"], 1)
            link(dve.tensor_copy(num[:, :], numi[:, :]))
            dve.wait_ge(S["logits"], NT // 4)
            dve.wait_ge(S["w_in"], 32)
            link(dve.tensor_tensor(out=lg[:, :, :], in0=ps_l[:, 0:E * NT].rearrange("p (t e) -> p e t", e=E), in1=along(br[:, :]), op=ALU.add))
            link(dve.tensor_reduce(out=best[:, :], in_=lg[:, :, :].rearrange("p e t -> p t e"), op=ALU.max, axis=AX.X))
            link(dve.tensor_tensor(out=hit[:, :, :], in0=lg[:, :, :], in1=over(best[:, :]), op=ALU.is_lt))
            link(dve.scalar_tensor_tensor(out=place[:, :, :], in0=hit[:, :, :], scalar=float(E), in1=along(num[:, 0:E]),
                                          op0=ALU.mult, op1=ALU.add))
            link(dve.tensor_reduce(out=first[:, :], in_=place[:, :, :].rearrange("p e t -> p t e"), op=ALU.min, axis=AX.X))
            dve.tensor_tensor(out=oh[:, :, :], in0=along(num[:, 0:E]), in1=over(first[:, :]), op=ALU.is_equal).then_inc(S["oh_ready"], 1)
            dve.wait_ge(S["counts"], 1)
            link(dve.tensor_copy(tot[:, :, :].rearrange("p e t -> p (e t)"), ps_l[:, E * NT:]))
            link(dve.tensor_tensor_scan(incl[:, :, :].rearrange("p e t -> p (e t)"), more[:, :, :].rearrange("p e t -> p (e t)"),
                                        tot[:, :, :].rearrange("p e t -> p (e t)"), 0.0, ALU.mult, ALU.add))
            link(dve.tensor_tensor(out=place[:, :, :], in0=incl[:, :, :], in1=tot[:, :, :], op=ALU.subtract))
            link(dve.tensor_tensor(out=hit[:, :, :].rearrange("p e t -> p (e t)"), in0=place[:, :, :].rearrange("p e t -> p (e t)"), in1=ps_l[:, 0:E * NT], op=ALU.add))
            link(dve.tensor_scalar(full[:, :, :], num[:, 0:NT].unsqueeze(1).to_broadcast([P, E, NT]), float(P), None, ALU.mult))
            link(dve.tensor_tensor(out=full[:, :, :], in0=full[:, :, :], in1=along(incl[:, :, NT - 1]), op=ALU.is_lt))
            link(dve.tensor_reduce(out=nt[:, :], in_=full[:, :, :], op=ALU.add, axis=AX.X))
            link(dve.tensor_tensor_scan(end[:, :], allone[:, 0:E], nt[:, :], 0.0, ALU.mult, ALU.add))
            link(dve.tensor_tensor(out=start[:, :], in0=end[:, :], in1=nt[:, :], op=ALU.subtract))
            link(dve.tensor_scalar(start[:, :], start[:, :], float(P), None, ALU.mult))
            link(dve.tensor_tensor(out=hit[:, :, :], in0=hit[:, :, :], in1=along(start[:, :]), op=ALU.add))
            link(dve.tensor_tensor(out=hit[:, :, :], in0=hit[:, :, :], in1=oh[:, :, :], op=ALU.mult))
            link(dve.tensor_reduce(out=slotf[:, :], in_=hit[:, :, :].rearrange("p e t -> p t e"), op=ALU.add, axis=AX.X))
            link(dve.tensor_copy(slot[:, :], slotf[:, :]))
            link(dve.tensor_tensor(out=past[:, :, :], in0=num[:, 0:TE].unsqueeze(2).to_broadcast([P, TE, E]),
                                   in1=end[:, :].unsqueeze(1).to_broadcast([P, TE, E]), op=ALU.is_ge))
            link(dve.tensor_reduce(out=idf[:, :], in_=past[:, :, :], op=ALU.add, axis=AX.X))
            link(dve.tensor_scalar(idf[:, :], idf[:, :], float(E - 1), None, ALU.min))
            dve.tensor_copy(tile_expert[:, :], idf[:, :]).then_inc(S["slots_ready"], 1)

            def gated(n, k, h):
                dve.wait_ge(S["sg_done"], n + 1)
                dve.tensor_tensor(out=act_[:, k, :], in0=sg[:, k, :], in1=ps_h[:, h, 0, :], op=ALU.mult).then_inc(S["act_done"], 1)

            def y_copy(n, k, stores):
                dve.wait_ge(S["y_ps"], n + 1)
                dve.wait_ge(y_out[k], stores)
                dve.tensor_copy(yt[:, k, :], ps_y[:, 0:D]).then_inc(S["y_sb"], 1)

            for n in range(UT):
                gated(n, n, n % 2)
                if n >= 2:
                    y_copy(n - 2, n - 2, 16)
            with dve.Fori(0, (TE - UT) // BODY) as i:
                for m in range(BODY):
                    n = i * BODY + UT + m
                    gated(n, m % UT, (UT + m) % 2)
                    y_copy(n - 2, (m - 2) % UT, i * (16 * BODY // UT) + 16 * ((m + 1) // UT + 1))
            for n in (TE - 2, TE - 1):
                y_copy(n, n % UT, 16 * (n // UT + 1))
            for g in range(NT // GT):
                s = slice(GT * g, GT * g + GT)
                dve.wait_ge(gathered[g], 16 * GT)
                dve.tensor_tensor(out=Y[:, s, :], in0=Y[:, s, :], in1=X[:, PAD + GT * g:PAD + GT * g + GT, :], op=ALU.add).then_inc(S["sums"], 1)
                dve.wait_ge(S["sums"], g + 1)
                for t in range(GT * g, GT * g + GT):
                    last = dve.bn_stats(stt[:, t, :], Y[:, t, :])
                last.then_inc(S["stats_done"], 1)
                dve.wait_ge(S["stats_done"], g * 7 + 1)
                variance(dve, stt[:, s, :], mom[:, :, s], mean[:, s], ve[:, s], S["stats_done"], g * 7 + 1, S["ve_ready"])
                dve.wait_ge(S["r_ready"], g + 1)
                newton(dve, rstd[:, s], ve[:, s], rr[:, 0, s], rr[:, 1, s], rr[:, 2, s], S["stats_done"], g * 7 + 3)
                for t in range(GT * g, GT * g + GT):
                    last = dve.tensor_scalar(Y[:, t, :], Y[:, t, :], mean[:, t:t + 1], rstd[:, t:t + 1], ALU.subtract, ALU.mult)
                last.then_inc(S["z_done"], 1)


_OUT = ((16, 256, 128), "float32")


def kernel(**inputs):
    import numpy as _np
    import concourse.bacc as _bacc
    from concourse import mybir as _mybir
    from concourse.bass_utils import run_bass_kernel_spmd as _run

    nc = _bacc.Bacc("TRN2", target_bir_lowering=False, num_devices=1)
    arrays, args = {}, {}
    for name, value in inputs.items():
        v = _np.ascontiguousarray(value)
        arrays[f"in_{name}_dram"] = v
        args[name] = nc.dram_tensor(f"in_{name}_dram", v.shape, _mybir.dt.from_np(v.dtype), kind="ExternalInput").ap()
    out = nc.dram_tensor("out_0_dram", _OUT[0], _mybir.dt.from_np(_np.dtype(_OUT[1])), kind="ExternalOutput").ap()
    build_program(nc, args, out)
    r = _run(nc, [arrays], core_ids=[0])
    return r.results[0]["out_0_dram"]
```

```python
import concourse.bass as bass
from concourse import mybir
from contextlib import ExitStack

F32 = mybir.dt.float32
F32R = mybir.dt.float32r
I32 = mybir.dt.int32
ALU = mybir.AluOpType
ACT = mybir.ActivationFunctionType
AX = mybir.AxisListType

P = 128
NB, L, D = 16, 256, 128
NT = NB * L // P
PAD = 2
DI, NS, KC = 64, 32, 3
EPS = 1e-5
SERIES = (15, 13, 11, 9, 7, 5, 3)
E, HID = 8, 512
TE = NT + E - 1
BC1, BC2 = E * 2 * HID // P, E * D // P
BC = BC1 + BC2


def build_program(nc, a, out):
    with ExitStack() as ctx:
        def sb(name, shape, dt=F32):
            return ctx.enter_context(nc.sbuf_tensor(name, shape, dt))

        X = sb("X", [P, PAD + NT, D])
        ident = sb("ident", [P, P])
        ones = sb("ones", [1, P])
        pre = Preloads()
        pre.w1 = sb("w1", [P, E, 2 * HID], F32R)
        pre.b_parts = sb("b_parts", [P, 2, BC], F32R)
        pre.wr = sb("wr", [P, E])
        pre.logits = sb("router_logits", [P, PAD + NT, E])
        pre.x_slots = nc.dram_tensor("x_slots", (TE * P, D), F32, kind="Internal").ap()
        for name in ("weights_in", "router_in", "slots_zeroed"):
            pre.sems[name] = ctx.enter_context(nc.semaphore(name))
        mamba_stage(nc, a, X, ident, ones, pre)
        attention_stage(nc, a, X, ident, pre)
        experts_stage(nc, a, X, ident, pre, out)


def tokens(ap):
    return ap.rearrange("b (h p) d -> p (b h) d", p=P)


def variance(dve, st, mom, mean, ve, step, base, ready):
    dve.tensor_tensor(out=mom[:, 0, :], in0=st[:, :, 1], in1=st[:, :, 4], op=ALU.add)
    dve.tensor_tensor(out=mom[:, 1, :], in0=st[:, :, 1], in1=st[:, :, 4], op=ALU.subtract)
    dve.tensor_tensor(out=mom[:, 2, :], in0=st[:, :, 2], in1=st[:, :, 5], op=ALU.add).then_inc(step, 1)
    dve.wait_ge(step, base + 1)
    dve.tensor_scalar(mean[:, :], mom[:, 0, :], 0.5, None, ALU.mult)
    dve.tensor_tensor(out=mom[:, 3, :], in0=mom[:, 1, :], in1=mom[:, 1, :], op=ALU.mult)
    dve.tensor_scalar(mom[:, 4, :], mom[:, 2, :], 1.0 / D, EPS, ALU.mult, ALU.add).then_inc(step, 1)
    dve.wait_ge(step, base + 2)
    dve.scalar_tensor_tensor(out=ve[:, :], in0=mom[:, 3, :], scalar=0.25, in1=mom[:, 4, :],
                             op0=ALU.mult, op1=ALU.add).then_inc(ready, 1)


def newton(dve, out, v, r, t1, t2, step, base):
    dve.tensor_tensor(out=t1, in0=r, in1=r, op=ALU.mult).then_inc(step, 1)
    dve.wait_ge(step, base + 1)
    dve.tensor_tensor(out=t2, in0=t1, in1=v, op=ALU.mult).then_inc(step, 1)
    dve.wait_ge(step, base + 2)
    dve.tensor_scalar(t1, t2, -0.5, 1.5, ALU.mult, ALU.add).then_inc(step, 1)
    dve.wait_ge(step, base + 3)
    dve.tensor_tensor(out=out, in0=r, in1=t1, op=ALU.mult).then_inc(step, 1)
    dve.wait_ge(step, base + 4)


class Preloads:
    def __init__(self):
        self.sems = {}


def mamba_stage(nc, a, X, ident, ones, pre):
    PAIRS = NB // 2
    CH = 4
    NCH = NS // CH
    NS2 = len(SERIES)
    ND = 6 + NS2
    LN_STEPS = 8
    HALF = NCH // 2
    SUMS = (0, 2, 1, 4, 3, 6, 5, 7)
    SUMS_AT = {1: (0,), 3: (2,), 4: (1,), 5: (4,), 6: (3,), 7: (6, 5)}

    def hc_buf(c):
        return 1 + c // 2 % 2 if c % 2 else 0

    def summed(j, c):
        return j * NCH + SUMS.index(c) + 1 if c >= 0 else j * NCH + SUMS.index(c + NCH) + 1 - NCH
    with ExitStack() as ctx:
        def sb(name, shape, dt=F32):
            return ctx.enter_context(nc.sbuf_tensor(name, shape, dt))

        def pb(name, shape):
            return ctx.enter_context(nc.psum_tensor(name, shape, F32))

        def sem(name):
            return ctx.enter_context(nc.semaphore(name))

        w_raw = sb("w_raw", [P, 4, DI])
        w_up = sb("w_up", [P, 4, DI])
        gam = sb("gam", [P, 1])
        bet = sb("bet", [P, 1])
        b_up = sb("b_up", [P, 2])
        b_eff = sb("b_eff", [P, 2])
        conv_w = sb("conv_w", [P, KC])
        conv_b = sb("conv_b", [P, 1])
        b_dl = sb("b_dl", [P, 1])
        d_skip = sb("d_skip", [P, 1])
        a_log = sb("a_log", [P, NS])
        a_exp = sb("a_exp", [P, NS])
        a_neg = sb("a_neg", [P, NS])
        w_dl = sb("w_dl", [P, P])
        w_bc = sb("w_bc", [P, 2, 2, 2, NS])
        w_dn = sb("w_dn", [P, 2, D])
        bd_row = sb("bd_row", [1, 4, D])
        pick0 = sb("pick0", [P, NS, P])
        pick = sb("pick", [P, NS, P], F32R)
        lo_rows = sb("lo_rows", [P, 1])
        stats = sb("stats", [P, NT, 6])
        mom = sb("mom", [P, 5, NT])
        mean = sb("mean", [P, NT])
        ve = sb("ve", [P, NT])
        lnv = sb("lnv", [P, NT])
        r0 = sb("r0", [P, NT])
        r1 = sb("r1", [P, NT])
        rstd = sb("rstd", [P, NT])
        y4 = sb("y4", [P, 4, D])
        yT = sb("yT", [P, 4 * P])
        left = sb("left", [P, L + KC - 1])
        right = sb("right", [P, L])
        c1 = sb("c1", [P, L])
        c2 = sb("c2", [P, L])
        c3 = sb("c3", [P, L])
        one_col = sb("one_col", [P, 1])
        n_c = sb("n_c", [P, L])
        e_c = sb("e_c", [P, L])
        l_c = sb("l_c", [P, L])
        d_c = sb("d_c", [P, L])
        s_c = sb("s_c", [P, L])
        u = sb("u", [P, 2, L])
        n_r = sb("n_r", [P, L])
        e_r = sb("e_r", [P, L])
        l_r = sb("l_r", [P, L])
        d_r = sb("d_r", [P, L])
        s_r = sb("s_r", [P, L])
        r_z = sb("r_z", [P, L])
        gate = sb("gate", [P, 2, L])
        z = sb("z", [P, L])
        nz = sb("nz", [P, L])
        e_z = sb("e_z", [P, L])
        w_z = sb("w_z", [P, L])
        w_m = sb("w_m", [P, L])
        s_z = sb("s_z", [P, L])
        s2 = sb("s2", [P, L])
        pz = sb("pz", [P, 2, L])
        delta = sb("delta", [P, L])
        du = sb("du", [P, L])
        bc_hi = sb("bc_hi", [P, 2 * L], F32R)
        bc = sb("bc", [P, 2, 2, L], F32R)
        dA = sb("dA", [P, 2, CH, L])
        b_sb = sb("b_sb", [P, 2, CH, L])
        dB = sb("dB", [P, 2, CH, L])
        h = sb("h", [P, 2, CH, L])
        c_sb = sb("c_sb", [P, CH, L])
        hC = sb("hC", [P, 3, CH, L])
        y2 = sb("y2", [P, L])
        gated = sb("gated", [P, L])
        xn = sb("xn", [P, 4, D])
        st2 = sb("st2", [P, 4, 6])
        mom2 = sb("mom2", [P, 5, 4])
        mean2 = sb("mean2", [P, 4])
        ve2 = sb("ve2", [P, 4])
        lnv2 = sb("lnv2", [P, 4])
        rr = sb("rr", [P, 3, 4])
        rstd2 = sb("rstd2", [P, 4])

        zero = sb("zero", [P, TE, D // 4])
        b_raw = sb("b_raw", [P, BC])

        ps_t = pb("ps_t", [P, 512])
        ps_up = pb("ps_up", [P, 512])
        ps_y = pb("ps_y", [P, 512])
        ps_bc = pb("ps_bc", [P, 512])
        ps_b = pb("ps_b", [P, CH, L])
        ps_c = pb("ps_c", [P, CH, L])

        names = ("zero_ready braw_in b_split zeroed set_done bd_done x_in w_in w_in2 id_done pick_done pick_r w_scaled "
                 "beta_ps beta_add a_done a_ready small rs_ln rs_exp y_ready yt_ps yt_sb up_ps up_sb conv c_exp c_log c_sig r_exp r_log r_sig "
                 "silu_steps r_steps u_ready gate_ready z_ps bc_ps z_ready nz_ready z_exp bc_hi_ready bc_ready dsteps "
                 "du_ready b_ps b_copied db_done db0_done da_ready scanned c_ps c_copied hc_even hc_odd n_summed y2_ready gated_ready o_ps "
                 "xn_ready x_written ln_steps ve_ready ve_ln r_ready").split()
        S = {n: sem("m_" + n) for n in names}
        block = ctx.enter_context(nc.Block())
        N_IN = 21

        @block.sync
        def _(sp):
            sp.dma_start(X[:, PAD:, :], tokens(a["x"])).then_inc(S["x_in"], 16)
            n = 0
            W = a["L0_attn_W_up"]
            col = lambda v: v.rearrange("(p o) -> p o", o=1)
            for dst, src in (
                (w_raw[:, 0, :], W[:, 0:DI]), (w_raw[:, 1, :], W[:, 0:DI]),
                (w_raw[:, 2, :], W[:, DI:2 * DI]), (w_raw[:, 3, :], W[:, DI:2 * DI]),
                (gam[:, :], col(a["L0_attn_ln_gamma"])), (bet[:, :], col(a["L0_attn_ln_beta"])),
            ):
                sp.dma_start(dst, src).then_inc(S["w_in"], 16)
                n += 1
            for k in range(2):
                rows = slice(DI * k, DI * k + DI)
                for dst, src in (
                    (b_up[rows, 0:1], col(a["L0_attn_b_up"][0:DI])),
                    (b_up[rows, 1:2], col(a["L0_attn_b_up"][DI:2 * DI])),
                    (conv_w[rows, :], a["L0_attn_conv_w"].rearrange("d o k -> d (o k)")),
                    (conv_b[rows, :], col(a["L0_attn_conv_b"])),
                    (b_dl[rows, :], col(a["L0_attn_b_delta"])),
                    (d_skip[rows, :], col(a["L0_attn_D"])),
                    (a_log[rows, :], a["L0_attn_A_log"]),
                ):
                    sp.dma_start(dst, src).then_inc(S["w_in"], 16)
                    n += 1
            sp.dma_start(bd_row[:, 0, :], a["L0_attn_b_down"].rearrange("(o d) -> o d", o=1)).then_inc(S["w_in"], 16)
            n += 1
            assert n == N_IN
            sp.wait_ge(S["zeroed"], 4)
            for k in range(2):
                rows = slice(DI * k, DI * k + DI)
                sp.dma_start(w_dl[rows, DI * k:DI * k + DI], a["L0_attn_W_delta"]).then_inc(S["w_in2"], 16)
                sp.dma_start(w_dn[rows, k, :], a["L0_attn_W_down"]).then_inc(S["w_in2"], 16)
                for s, w in enumerate((a["L0_attn_W_B"], a["L0_attn_W_C"])):
                    for part in range(2):
                        sp.dma_start(w_bc[rows, s, part, k, :], w).then_inc(S["w_in2"], 16)
            sp.dma_start(pre.wr[:, :], a["L0_ffn_router_w"]).then_inc(pre.sems["router_in"], 16)
            sp.dma_start(b_raw[:, 0:BC1], a["L0_ffn_b1"].rearrange("e n -> (e n)").rearrange("(p c) -> p c", p=P)).then_inc(S["braw_in"], 16)
            sp.dma_start(b_raw[:, BC1:], a["L0_ffn_b2"].rearrange("e n -> (e n)").rearrange("(p c) -> p c", p=P)).then_inc(S["braw_in"], 16)
            for e in range(E):
                sp.dma_start(pre.w1[:, e, :].bitcast(F32), a["L0_ffn_w1"][e]).then_inc(pre.sems["weights_in"], 16)
            sp.wait_ge(S["zero_ready"], 1)
            v = pre.x_slots.rearrange("(p t) (q c) -> p t q c", p=P, q=4)
            for q in range(4):
                sp.dma_start(v[:, :, q, :], zero[:, :, :]).then_inc(pre.sems["slots_zeroed"], 16)
            sp.wait_ge(pre.sems["slots_zeroed"], 64)
        N_IN2 = 12

        @block.gpsimd
        def _(pool):
            for n, m in enumerate((w_dl[:, :], w_dn[:, :, :], w_bc[:, :, :, :, :], ident[:, :], pick0[:, :, :])):
                if n:
                    pool.wait_ge(S["zeroed"], n)
                pool.memset(m, 0.0).then_inc(S["zeroed"], 1)
            pool.wait_ge(S["zeroed"], 5)
            pool.affine_select(out=ident[:, :], in_=ident[:, :], compare_op=ALU.not_equal, fill=1.0,
                               base=0, pattern=[[-1, P]], channel_multiplier=1).then_inc(S["id_done"], 1)
            pool.wait_ge(S["id_done"], 1)
            for q in range(4):
                v = pick0[NS * q:NS * q + NS, :, DI * (q % 2):DI * (q % 2) + DI]
                pool.affine_select(out=v, in_=v, compare_op=ALU.not_equal, fill=1.0, base=0,
                                   pattern=[[-1, NS], [0, DI]], channel_multiplier=1).then_inc(S["pick_done"], 1)
                pool.wait_ge(S["pick_done"], q + 1)
            pool.memset(zero[:, :, :], 0.0).then_inc(S["zero_ready"], 1)
            pool.wait_ge(S["zero_ready"], 1)
            pool.wait_ge(S["braw_in"], 32)
            pool.tensor_copy(pre.b_parts[:, 0, :], b_raw[:, :]).then_inc(S["b_split"], 1)
            pool.wait_ge(S["b_split"], 1)
            pool.tensor_tensor(out=pre.b_parts[:, 1, :], in0=b_raw[:, :], in1=pre.b_parts[:, 0, :].bitcast(F32),
                               op=ALU.subtract).then_inc(S["b_split"], 1)
            pool.wait_ge(S["b_split"], 2)

            def delta_u_b(j, c, waits=True):
                pool.wait_ge(S["du_ready"], j + 1)
                pool.wait_ge(S["b_copied"], j * NCH + c + 1)
                if waits:
                    pool.wait_ge(S["scanned"], j * NCH + c - 1)
                pool.tensor_tensor(out=dB[:, c % 2, :, :], in0=du[:, :].unsqueeze(1).to_broadcast([P, CH, L]),
                                   in1=b_sb[:, c % 2, :, :], op=ALU.mult).then_inc(S["db_done"], 1)
                pool.wait_ge(S["db_done"], j * (NCH - 1) + c)

            def h_c(j, c):
                pool.wait_ge(S["scanned"], j * NCH + c + 1)
                pool.wait_ge(S["c_copied"], j * HALF + c // 2 + 1)
                if not (isinstance(j, int) and j == 0 and c < 4):
                    pool.wait_ge(S["n_summed"], summed(j, c - 4))
                pool.tensor_tensor(out=hC[:, hc_buf(c), :, :], in0=h[:, 1, :, :], in1=c_sb[:, :, :], op=ALU.mult).then_inc(S["hc_odd"], 1)
                pool.wait_ge(S["hc_odd"], j * HALF + c // 2 + 1)

            def pair(j, par, first, left_over):
                for c in range(NCH):
                    if c < NCH - 1:
                        delta_u_b(j, c + 1, not (first and c == 0))
                    if c % 2:
                        h_c(j, c)

            in_turn(pool, PAIRS, pair)

        @block.tensor
        def _(pe):
            pe.wait_ge(S["w_in"], 16 * N_IN)
            for s in range(2):
                last = pe.matmul(ps_up[:, s:s + 1], w_raw[:, 2 * s:2 * s + 2, :].rearrange("p k c -> p (k c)"), bet[:, :],
                                 start=True, stop=True)
            last.then_inc(S["beta_ps"], 1)
            pe.wait_ge(S["id_done"], 1)
            pe.wait_ge(S["w_scaled"], 1)
            pe.wait_ge(S["set_done"], 1)
            pe.wait_ge(S["beta_add"], 1)
            pe.wait_ge(S["bd_done"], 1)

            def turn(j):
                pe.wait_ge(S["y_ready"], j + 1)
                for t in range(4):
                    last = pe.transpose(ps_t[:, t * P:(t + 1) * P], y4[:, t, :], ident[:, :])
                last.then_inc(S["yt_ps"], 1)

            def up(j):
                pe.wait_ge(S["yt_sb"], j + 1)
                for s in range(2):
                    for k in range(2):
                        last = pe.matmul(ps_up[DI * k:DI * k + DI, L * s:L * s + L], w_up[:, 2 * s + k, :],
                                         yT[:, L * k:L * k + L], start=True, stop=True)
                last.then_inc(S["up_ps"], 1)

            def project(j, par):
                pe.wait_ge(S["u_ready"], j + 1)
                pe.matmul(ps_up[:, 0:L], w_dl[:, :], u[:, par, :], start=True, stop=True).then_inc(S["z_ps"], 1)
                for s in range(2):
                    last = pe.matmul(ps_bc[:, L * s:L * s + L],
                                     w_bc[:, s, :, :, :].rearrange("p a b n -> p (a b n)"), u[:, par, :],
                                     start=True, stop=True)
                last.then_inc(S["bc_ps"], 1)

            def spread(s, ps, par, c, done):
                for n in range(CH):
                    last = pe.matmul(ps[:, n, :], pick[:, c * CH + n, :], bc[:, par, s, :], start=True, stop=True)
                last.then_inc(S[done], 1)

            def n_sum(j, c):
                pe.wait_ge(S["hc_odd" if c % 2 else "hc_even"], j * HALF + c // 2 + 1)
                for n in range(CH):
                    last = pe.matmul(ps_y[:, 0:L], ident[:, :], hC[:, hc_buf(c), n, :],
                                     start=(c == 0 and n == 0), stop=(c == NCH - 1 and n == CH - 1))
                last.then_inc(S["n_summed"], 1)

            def down(j):
                pe.matmul(ps_t[:, :], ones[0:1, :], bd_row[0:1, :, :].rearrange("o t d -> o (t d)"), start=True, stop=False, skip_group_check=True)
                pe.wait_ge(S["gated_ready"], j + 1)
                for t in range(4):
                    last = pe.matmul(ps_t[:, t * D:(t + 1) * D], gated[:, (t % 2) * P:(t % 2) * P + P], w_dn[:, t // 2, :],
                                     start=False, stop=True, skip_group_check=True)
                last.then_inc(S["o_ps"], 1)

            turn(0)
            up(0)
            turn(1)
            pe.wait_ge(S["w_in2"], 16 * N_IN2)
            project(0, 0)
            pe.wait_ge(S["z_ready"], 1)
            up(1)
            pe.wait_ge(S["pick_r"], 1)
            pe.wait_ge(S["bc_ready"], 1)
            spread(0, ps_b, 0, 0, "b_ps")

            def pair(j, par, first, left_over):
                for c in range(NCH):
                    if c < NCH - 1 or left_over:
                        pe.wait_ge(S["b_copied"], j * NCH + c + 1)
                        if c < NCH - 1:
                            spread(0, ps_b, par, c + 1, "b_ps")
                        else:
                            pe.wait_ge(S["bc_ready"], j + 2)
                            spread(0, ps_b, 1 - par, 0, "b_ps")
                    if c == 1 and not first:
                        n_sum(j - 1, NCH - 1)
                    if c % 2:
                        pe.wait_ge(S["hc_even"], j * HALF + c // 2 + 1)
                    elif c or not first:
                        pe.wait_ge(S["c_copied"], j * HALF + c // 2)
                    spread(1, ps_c, par, c, "c_ps")
                    if c == 4 and left_over:
                        project(j + 1, 1 - par)
                    if c == NCH - 2 and left_over > 1:
                        if not first:
                            pe.wait_ge(S["xn_ready"], j)
                        turn(j + 2)
                    if c == NCH - 1 and left_over > 1:
                        pe.wait_ge(S["z_ready"], j + 2)
                        up(j + 2)
                    if c == 1 and not first:
                        pe.wait_ge(S["y2_ready"], j)
                    for summand in SUMS_AT.get(c, ()):
                        n_sum(j, summand)
                    if c == 2 and not first:
                        down(j - 1)

            in_turn(pe, PAIRS, pair)
            n_sum(PAIRS - 1, NCH - 1)
            down(PAIRS - 1)

        @block.scalar
        def _(act):
            act.preload_act_table_set("natural_log_exp_and_others")
            act.wait_ge(S["w_in"], 16 * N_IN)
            act.activation(a_exp[:, :], a_log[:, :], ACT.Exp).then_inc(S["a_done"], 1)
            act.wait_ge(S["ve_ready"], 1)
            act.activation(lnv[:, :], ve[:, :], ACT.Ln).then_inc(S["rs_ln"], 1)
            act.wait_ge(S["rs_ln"], 1)
            act.activation(r0[:, :], lnv[:, :], ACT.Exp, scale=-0.5).then_inc(S["rs_exp"], 1)
            act.wait_ge(S["pick_done"], 4)
            act.activation(pick[:, :, :].rearrange("p n c -> p (n c)"), pick0[:, :, :].rearrange("p n c -> p (n c)"),
                           ACT.Copy).then_inc(S["pick_r"], 1)
            act.wait_ge(S["beta_add"], 1)
            act.wait_ge(S["a_ready"], 1)
            act.wait_ge(S["set_done"], 1)

            def y_copy(j):
                act.wait_ge(S["yt_ps"], j + 1)
                act.activation(yT[:, :], ps_t[:, :], ACT.Copy).then_inc(S["yt_sb"], 1)

            def up_copy(j):
                act.wait_ge(S["up_ps"], j + 1)
                if not (isinstance(j, int) and j == 0):
                    act.wait_ge(S["gate_ready"], j)
                act.activation(left[:, KC - 1:], ps_up[:, 0:L], ACT.Identity, bias=b_eff[:, 0:1]).then_inc(S["up_sb"], 1)
                act.activation(right[:, :], ps_up[:, L:2 * L], ACT.Identity, bias=b_eff[:, 1:2]).then_inc(S["up_sb"], 1)

            def conv_log(j):
                act.wait_ge(S["silu_steps"], j * 2 + 1)
                act.activation(e_c[:, :], n_c[:, :], ACT.Exp).then_inc(S["c_exp"], 1)
                act.wait_ge(S["c_exp"], j + 1)
                act.activation(l_c[:, :], e_c[:, :], ACT.Ln, bias=one_col[:, 0:1]).then_inc(S["c_log"], 1)

            def conv_sigmoid(j):
                act.wait_ge(S["silu_steps"], j * 2 + 2)
                act.activation(s_c[:, :], d_c[:, :], ACT.Exp).then_inc(S["c_sig"], 1)

            def right_log(j):
                act.wait_ge(S["r_steps"], j * 2 + 1)
                act.activation(e_r[:, :], n_r[:, :], ACT.Exp).then_inc(S["r_exp"], 1)
                act.wait_ge(S["r_exp"], j + 1)
                act.activation(l_r[:, :], e_r[:, :], ACT.Ln, bias=one_col[:, 0:1]).then_inc(S["r_log"], 1)

            def right_sigmoid(j):
                act.wait_ge(S["r_steps"], j * 2 + 2)
                act.activation(s_r[:, :], d_r[:, :], ACT.Exp).then_inc(S["r_sig"], 1)

            def z_exp(j):
                act.wait_ge(S["nz_ready"], j + 1)
                act.activation(e_z[:, :], nz[:, :], ACT.Exp).then_inc(S["z_exp"], 1)

            def prepare(j, c, waits=True):
                copy_b(j, c, waits)
                exp_da(j, c, waits)

            def copy_b(j, c, waits=True):
                act.wait_ge(S["b_ps"], j * NCH + c + 1)
                if waits:
                    if c == 2:
                        act.wait_ge(S["db0_done"], j + 1)
                    elif not (isinstance(j, int) and j == 0):
                        act.wait_ge(S["db_done"], j * (NCH - 1) + c - (2 if c > 2 else 1))
                    elif c > 2:
                        act.wait_ge(S["db_done"], c - 2)
                act.activation(b_sb[:, c % 2, :, :], ps_b[:, :, :], ACT.Copy).then_inc(S["b_copied"], 1)

            def exp_da(j, c, waits=True):
                if waits:
                    act.wait_ge(S["scanned"], j * NCH + c - 1)
                for n in range(CH):
                    k = c * CH + n
                    last = act.activation(dA[:, c % 2, n, 1:], delta[:, 1:], ACT.Exp, scale=a_neg[:, k:k + 1])
                last.then_inc(S["da_ready"], 1)

            def copy_c(j, c):
                act.wait_ge(S["c_ps"], j * NCH + c + 1)
                if not (isinstance(j, int) and j == 0 and c == 1):
                    act.wait_ge(S["hc_odd"], j * HALF + c // 2)
                act.activation(c_sb[:, :, :], ps_c[:, :, :], ACT.Copy).then_inc(S["c_copied"], 1)

            def root(j):
                act.wait_ge(S["ln_steps"], j * LN_STEPS + 4)
                act.activation(lnv2[:, :], ve2[:, :], ACT.Ln).then_inc(S["ve_ln"], 1)
                act.wait_ge(S["ve_ln"], j + 1)
                act.activation(rr[:, 0, :], lnv2[:, :], ACT.Exp, scale=-0.5).then_inc(S["r_ready"], 1)

            y_copy(0)
            up_copy(0)
            y_copy(1)
            conv_log(0)
            right_log(0)
            conv_sigmoid(0)
            right_sigmoid(0)
            z_exp(0)
            up_copy(1)
            copy_b(0, 0, False)
            act.wait_ge(S["du_ready"], 1)
            exp_da(0, 0, False)

            def pair(j, par, first, left_over):
                for c in range(NCH):
                    if c == NCH - 1 and left_over:
                        copy_b(j + 1, 0)
                    if c == NCH - 1 and left_over > 1:
                        up_copy(j + 2)
                    if c < NCH - 1:
                        prepare(j, c + 1, not (first and c == 0))
                    if c == NCH - 1:
                        copy_c(j, c)
                    if c == NCH - 1 and left_over:
                        act.wait_ge(S["du_ready"], j + 2)
                        exp_da(j + 1, 0)
                    if c % 2 and c < NCH - 1:
                        copy_c(j, c)
                    if left_over and c == 0:
                        right_log(j + 1)
                    elif left_over and c == 1:
                        right_sigmoid(j + 1)
                        conv_log(j + 1)
                    elif left_over and c == 2:
                        conv_sigmoid(j + 1)
                    if c == 4 and left_over:
                        z_exp(j + 1)
                    if c == 5 and not first:
                        root(j - 1)
                    if c == NCH - 2 and left_over > 1:
                        y_copy(j + 2)

            in_turn(act, PAIRS, pair)
            root(PAIRS - 1)

        @block.vector
        def _(dve):
            dve.memset(dA[:, :, :, 0:1], 0.0)
            dve.memset(left[:, 0:KC - 1], 0.0)
            dve.memset(ones[:, :], 1.0)
            dve.memset(one_col[:, :], 1.0)
            dve.memset(lo_rows[0:DI, :], 0.0)
            dve.memset(lo_rows[DI:P, :], -1.0).then_inc(S["set_done"], 1)
            dve.wait_ge(S["x_in"], 16)
            for t in range(NT):
                last = dve.bn_stats(stats[:, t, :], X[:, PAD + t, :])
            last.then_inc(S["small"], 1)
            dve.wait_ge(S["small"], 1)
            variance(dve, stats, mom, mean, ve, S["small"], 1, S["ve_ready"])
            dve.wait_ge(S["w_in"], 16 * N_IN)
            dve.tensor_scalar(w_up[:, :, :], w_raw[:, :, :], gam[:, 0:1], None, ALU.mult).then_inc(S["w_scaled"], 1)
            for t in range(1, 4):
                last = dve.tensor_copy(bd_row[:, t, :], bd_row[:, 0, :])
            last.then_inc(S["bd_done"], 1)
            dve.wait_ge(S["beta_ps"], 1)
            dve.tensor_tensor(out=b_eff[:, :], in0=ps_up[:, 0:2], in1=b_up[:, :], op=ALU.add).then_inc(S["beta_add"], 1)
            dve.wait_ge(S["a_done"], 1)
            dve.tensor_scalar(a_neg[:, :], a_exp[:, :], -1.0, None, ALU.mult).then_inc(S["a_ready"], 1)
            dve.wait_ge(S["rs_exp"], 1)
            newton(dve, rstd[:, :], ve[:, :], r0[:, :], r1[:, :], lnv[:, :], S["small"], 3)

            def normalise(j):
                for t in range(4):
                    n = j * 4 + t
                    col = slice(n, n + 1) if isinstance(n, int) else bass.ds(n, 1)
                    last = dve.tensor_scalar(y4[:, t, :], X[:, n + PAD, :], mean[:, col], rstd[:, col], ALU.subtract, ALU.mult)
                last.then_inc(S["y_ready"], 1)

            def conv(j, k):
                if k == 0:
                    dve.wait_ge(S["up_sb"], j * 2 + 1)
                    ins = dve.tensor_scalar(c1[:, :], left[:, 2:2 + L], conv_w[:, 2:3], conv_b[:, 0:1], ALU.mult, ALU.add)
                else:
                    dve.wait_ge(S["conv"], j * 3 + k)
                    src, dst = ((c1, c2), (c2, c3))[k - 1]
                    ins = dve.scalar_tensor_tensor(out=dst[:, :], in0=left[:, 2 - k:2 - k + L], scalar=conv_w[:, 2 - k:3 - k],
                                                   in1=src[:, :], op0=ALU.mult, op1=ALU.add)
                ins.then_inc(S["conv"], 1)

            def silu(j, par, k):
                steps = S["silu_steps"]
                if k == 0:
                    dve.wait_ge(S["conv"], j * 3 + 3)
                    dve.scalar_tensor_tensor(out=n_c[:, :], in0=c3[:, :], scalar=-1.0, in1=c3[:, :],
                                             op0=ALU.mult, op1=ALU.min).then_inc(steps, 1)
                elif k == 1:
                    dve.wait_ge(S["c_log"], j + 1)
                    dve.scalar_tensor_tensor(out=d_c[:, :], in0=c3[:, :], scalar=0.0, in1=l_c[:, :],
                                             op0=ALU.min, op1=ALU.subtract).then_inc(steps, 1)
                elif k == 2:
                    dve.wait_ge(S["c_sig"], j + 1)
                    dve.tensor_tensor(out=u[:, par, :], in0=c3[:, :], in1=s_c[:, :], op=ALU.mult).then_inc(S["u_ready"], 1)

            def silu_right(j, par, k, waits=False):
                steps = S["r_steps"]
                if k == 0:
                    dve.wait_ge(S["up_sb"], j * 2 + 2)
                    dve.scalar_tensor_tensor(out=n_r[:, :], in0=right[:, :], scalar=-1.0, in1=right[:, :],
                                             op0=ALU.mult, op1=ALU.min).then_inc(steps, 1)
                elif k == 1:
                    dve.wait_ge(S["r_log"], j + 1)
                    dve.scalar_tensor_tensor(out=d_r[:, :], in0=right[:, :], scalar=0.0, in1=l_r[:, :],
                                             op0=ALU.min, op1=ALU.subtract).then_inc(steps, 1)
                elif k == 2:
                    dve.wait_ge(S["r_sig"], j + 1)
                    if waits:
                        dve.wait_ge(S["gated_ready"], j - 1)
                    dve.tensor_tensor(out=gate[:, par, :], in0=right[:, :], in1=s_r[:, :], op=ALU.mult).then_inc(S["gate_ready"], 1)

            def z_step(j, k):
                if k == 0:
                    dve.wait_ge(S["z_ps"], j + 1)
                    dve.tensor_scalar(z[:, :], ps_up[:, 0:L], b_dl[:, 0:1], None, ALU.add).then_inc(S["z_ready"], 1)
                else:
                    dve.wait_ge(S["z_ready"], j + 1)
                    dve.scalar_tensor_tensor(out=nz[:, :], in0=z[:, :], scalar=-1.0, in1=z[:, :],
                                             op0=ALU.mult, op1=ALU.min).then_inc(S["nz_ready"], 1)

            def bc_step(j, par, k):
                if k == 0:
                    dve.wait_ge(S["bc_ps"], j + 1)
                    dve.tensor_copy(bc_hi[:, :], ps_bc[:, :]).then_inc(S["bc_hi_ready"], 1)
                else:
                    dve.wait_ge(S["bc_hi_ready"], j + 1)
                    dve.scalar_tensor_tensor(out=bc[:, par, :, :].rearrange("p s l -> p (s l)"), in0=bc_hi[:, :].bitcast(F32),
                                             scalar=lo_rows[:, 0:1], in1=ps_bc[:, :], op0=ALU.mult, op1=ALU.add).then_inc(S["bc_ready"], 1)

            def delta_step(j, par, k):
                steps, base = S["dsteps"], j * ND
                if k:
                    dve.wait_ge(steps, base + k)
                if k == 0:
                    dve.wait_ge(S["z_exp"], j + 1)
                    ins = dve.tensor_scalar(w_z[:, :], e_z[:, :], 2.0, None, ALU.add)
                elif k == 1:
                    ins = dve.reciprocal(r_z[:, :], w_z[:, :])
                elif k == 2:
                    ins = dve.scalar_tensor_tensor(out=s_z[:, :], in0=e_z[:, :], scalar=2.0, in1=r_z[:, :], op0=ALU.mult, op1=ALU.mult)
                elif k == 3:
                    ins = dve.scalar_tensor_tensor(out=s2[:, :], in0=s_z[:, :], scalar=0.25, in1=s_z[:, :], op0=ALU.mult, op1=ALU.mult)
                elif k == 4:
                    ins = dve.tensor_scalar(pz[:, 0, :], s2[:, :], 1.0 / SERIES[0], None, ALU.mult)
                elif k < 4 + NS2:
                    i = k - 4
                    ins = dve.scalar_tensor_tensor(out=pz[:, i % 2, :], in0=pz[:, (i - 1) % 2, :], scalar=1.0 / SERIES[i], in1=s2[:, :],
                                                   op0=ALU.add, op1=ALU.mult)
                elif k == 4 + NS2:
                    ins = dve.scalar_tensor_tensor(out=w_m[:, :], in0=pz[:, (NS2 - 1) % 2, :], scalar=1.0, in1=s_z[:, :],
                                                   op0=ALU.add, op1=ALU.mult)
                elif k == 5 + NS2:
                    ins = dve.scalar_tensor_tensor(out=delta[:, :], in0=z[:, :], scalar=0.0, in1=w_m[:, :],
                                                   op0=ALU.max, op1=ALU.add)
                ins.then_inc(steps, 1)

            def delta_u(j, par):
                dve.wait_ge(S["dsteps"], j * ND + ND)
                dve.tensor_tensor(out=du[:, :], in0=delta[:, :], in1=u[:, par, :], op=ALU.mult).then_inc(S["du_ready"], 1)

            def skip(j, par):
                dve.wait_ge(S["n_summed"], j * NCH + NCH)
                dve.scalar_tensor_tensor(out=y2[:, :], in0=u[:, par, :], scalar=d_skip[:, 0:1], in1=ps_y[:, 0:L],
                                         op0=ALU.mult, op1=ALU.add).then_inc(S["y2_ready"], 1)

            def apply_gate(j, par):
                dve.wait_ge(S["y2_ready"], j + 1)
                dve.tensor_tensor(out=gated[:, :], in0=y2[:, :], in1=gate[:, par, :], op=ALU.mult).then_inc(S["gated_ready"], 1)

            def residual(j):
                dve.wait_ge(S["o_ps"], j + 1)
                tiles = X[:, j * 4 + PAD:j * 4 + PAD + 4, :] if isinstance(j, int) else X[:, bass.ds(j * 4 + PAD, 4), :]
                dve.scalar_tensor_tensor(out=xn[:, :, :].rearrange("p t d -> p (t d)"), in0=tiles.rearrange("p t d -> p (t d)"), scalar=2.0,
                                         in1=ps_t[:, :], op0=ALU.mult, op1=ALU.add).then_inc(S["xn_ready"], 1)

            def norm_step(j, k):
                steps, base = S["ln_steps"], j * LN_STEPS
                if k:
                    dve.wait_ge(steps, base + k)
                if k == 0:
                    dve.wait_ge(S["xn_ready"], j + 1)
                    for t in range(4):
                        last = dve.bn_stats(st2[:, t, :], xn[:, t, :])
                elif k == 1:
                    dve.tensor_tensor(out=mom2[:, 0, :], in0=st2[:, :, 1], in1=st2[:, :, 4], op=ALU.add)
                    dve.tensor_tensor(out=mom2[:, 1, :], in0=st2[:, :, 1], in1=st2[:, :, 4], op=ALU.subtract)
                    last = dve.tensor_tensor(out=mom2[:, 2, :], in0=st2[:, :, 2], in1=st2[:, :, 5], op=ALU.add)
                elif k == 2:
                    dve.tensor_scalar(mean2[:, :], mom2[:, 0, :], 0.5, None, ALU.mult)
                    dve.tensor_tensor(out=mom2[:, 3, :], in0=mom2[:, 1, :], in1=mom2[:, 1, :], op=ALU.mult)
                    last = dve.tensor_scalar(mom2[:, 4, :], mom2[:, 2, :], 1.0 / D, EPS, ALU.mult, ALU.add)
                elif k == 3:
                    last = dve.scalar_tensor_tensor(out=ve2[:, :], in0=mom2[:, 3, :], scalar=0.25, in1=mom2[:, 4, :],
                                                    op0=ALU.mult, op1=ALU.add)
                elif k == 4:
                    dve.wait_ge(S["r_ready"], j + 1)
                    last = dve.tensor_tensor(out=rr[:, 1, :], in0=rr[:, 0, :], in1=rr[:, 0, :], op=ALU.mult)
                elif k == 5:
                    last = dve.tensor_tensor(out=rr[:, 2, :], in0=rr[:, 1, :], in1=ve2[:, :], op=ALU.mult)
                elif k == 6:
                    last = dve.tensor_scalar(rr[:, 1, :], rr[:, 2, :], -0.5, 1.5, ALU.mult, ALU.add)
                elif k == 7:
                    last = dve.tensor_tensor(out=rstd2[:, :], in0=rr[:, 0, :], in1=rr[:, 1, :], op=ALU.mult)
                last.then_inc(steps, 1)

            def write_x(j, t):
                if t == 0:
                    dve.wait_ge(S["ln_steps"], j * LN_STEPS + LN_STEPS)
                dve.tensor_scalar(X[:, j * 4 + t + PAD, :], xn[:, t, :], mean2[:, t:t + 1], rstd2[:, t:t + 1],
                                  ALU.subtract, ALU.mult).then_inc(S["x_written"], 1)

            normalise(0)
            dve.wait_ge(S["yt_ps"], 1)
            normalise(1)
            for k in range(KC):
                conv(0, k)
            for k in range(3):
                silu(0, 0, k)
                silu_right(0, 0, k)
            for k in range(2):
                z_step(0, k)
            for k in range(2):
                bc_step(0, 0, k)
            for k in range(ND):
                delta_step(0, 0, k)
            delta_u(0, 0)

            def scan(j, c, waits):
                dve.wait_ge(S["da_ready"], j * NCH + c + 1)
                if c:
                    dve.wait_ge(S["db_done"], j * (NCH - 1) + c)
                else:
                    dve.wait_ge(S["db0_done"], j + 1)
                if waits:
                    dve.wait_ge(S["hc_odd" if c % 2 else "hc_even"], j * HALF + c // 2)
                flat = lambda v: v.rearrange("p n l -> p (n l)")
                dve.tensor_tensor_scan(flat(h[:, c % 2, :, :]), flat(dA[:, c % 2, :, :]), flat(dB[:, c % 2, :, :]), 0.0,
                                       ALU.mult, ALU.add).then_inc(S["scanned"], 1)

            def h_c(j, c, waits):
                dve.wait_ge(S["c_ps"], j * NCH + c + 1)
                dve.wait_ge(S["scanned"], j * NCH + c + 1)
                if waits:
                    dve.wait_ge(S["n_summed"], summed(j, c - 2))
                dve.tensor_tensor(out=hC[:, 0, :, :], in0=h[:, 0, :, :], in1=ps_c[:, :, :], op=ALU.mult).then_inc(S["hc_even"], 1)

            def delta_u_b(j):
                dve.wait_ge(S["du_ready"], j + 1)
                dve.wait_ge(S["b_copied"], j * NCH + 1)
                dve.tensor_tensor(out=dB[:, 0, :, :], in0=du[:, :].unsqueeze(1).to_broadcast([P, CH, L]),
                                  in1=b_sb[:, 0, :, :], op=ALU.mult).then_inc(S["db0_done"], 1)

            def pair(j, par, first, left_over):
                nxt, prev, other = j + 1, j - 1, 1 - par
                old, new = not first, left_over > 0
                for c in range(NCH):
                    if c == 0:
                        delta_u_b(j)
                        if new:
                            silu_right(nxt, other, 0)
                    scan(j, c, not (first and c < 2))
                    if c == 0:
                        if new:
                            conv(nxt, 0)
                    elif c == 1:
                        if new:
                            conv(nxt, 2)
                        if old:
                            apply_gate(prev, other)
                        if new:
                            silu(nxt, other, 0)
                            silu_right(nxt, other, 1)
                    elif c == 2:
                        if new:
                            silu_right(nxt, other, 2, old)
                    elif c == 3:
                        if old:
                            norm_step(prev, 1)
                        if new:
                            silu(nxt, other, 2)
                    elif c == 4:
                        if new:
                            z_step(nxt, 0)
                        if old:
                            norm_step(prev, 2)
                        if new:
                            z_step(nxt, 1)
                        if old:
                            norm_step(prev, 3)
                        if new:
                            bc_step(nxt, other, 0)
                    elif c == 5:
                        if new:
                            delta_step(nxt, other, 2)
                            if left_over > 1:
                                normalise(j + 2)
                            delta_step(nxt, other, 3)
                        if old:
                            norm_step(prev, 4)
                        if new:
                            delta_step(nxt, other, 4)
                        if old:
                            norm_step(prev, 5)
                        if new:
                            delta_step(nxt, other, 5)
                        if old:
                            norm_step(prev, 6)
                    elif c == 6:
                        if new:
                            delta_step(nxt, other, 6)
                        if old:
                            norm_step(prev, 7)
                        if new:
                            delta_step(nxt, other, 7)
                    if c % 2 == 0:
                        h_c(j, c, not (first and c == 0))
                    if c == 0:
                        if new:
                            conv(nxt, 1)
                        if old:
                            skip(prev, other)
                    elif c == 2:
                        if new:
                            silu(nxt, other, 1)
                        if old:
                            residual(prev)
                        if old:
                            norm_step(prev, 0)
                    elif c == 4 and new:
                        delta_step(nxt, other, 0)
                        bc_step(nxt, other, 1)
                        delta_step(nxt, other, 1)
                    elif c == 6 and not new:
                        for t in range(4):
                            write_x(prev, t)
                    elif c == 6:
                        for k in (8, 9, 10, 11):
                            delta_step(nxt, other, k)
                            if old:
                                write_x(prev, k - 8)
                        dve.wait_ge(S["da_ready"], (j + 1) * NCH)
                        dve.wait_ge(S["db_done"], (j + 1) * (NCH - 1))
                        delta_step(nxt, other, 12)
                        delta_u(nxt, other)

            in_turn(dve, PAIRS, pair)
            last = PAIRS - 1
            skip(last, last % 2)
            apply_gate(last, last % 2)
            residual(last)
            for k in range(LN_STEPS):
                norm_step(last, k)
            for t in range(4):
                write_x(last, t)


def in_turn(eng, pairs, pair):
    pair(0, 0, True, pairs - 1)
    with eng.Fori(0, (pairs - 4) // 2) as i:
        for m in (1, 2):
            pair(i * 2 + m, m % 2, False, 9)
    for j in range(pairs - 3, pairs):
        pair(j, j % 2, False, pairs - 1 - j)


H, DK = 16, 8
LK, DC = 1601, 64
KT = -(-LK // P)
KR = LK - (KT - 1) * P
HG, G4 = 4, H // 4
STEPS = G4 * KT
UNITS = 32
BUNITS = G4 * UNITS
AHEAD = UNITS + 9
QUARTER = [(0, 400), (400, 400), (800, 400), (LK - 402, 402)]
KCH = [(c * 512, min(512, LK - c * 512)) for c in range(4)]
SR = 3 * 32

FIRST_ROUNDS = ([("ctx", c) for c in range(4)] + [("x", 0)] + [("k", c) for c in range(4)] + [("q", 0)]
                + [("v", c) for c in range(4)] + [("max", 0)])
ROUNDS = {1: ("norm", 3), 3: ("concat", 0), 5: ("out", 0), 6: ("x", 0), 7: ("q", 0), 8: ("ctx", 0), 9: ("ctx", 1),
          10: ("max", 1), 11: ("ctx", 2), 12: ("ctx", 3), 14: ("k", 0), 15: ("k", 1), 16: ("norm", 0), 17: ("k", 2),
          18: ("k", 3), 20: ("v", 0), 21: ("v", 1), 23: ("max", 2), 24: ("v", 2), 25: ("v", 3), 28: ("norm", 1), 33: ("turn", 0), 38: ("logit", 0),
          36: ("max", 3), 41: ("norm", 2), 49: ("max", 4)}
ORDER = [ROUNDS[s] for s in sorted(ROUNDS)]


def first_round(kind, n):
    return FIRST_ROUNDS.index((kind, n)) + 1


def round_of(b, kind, n):
    return b * len(ORDER) + len(FIRST_ROUNDS) + ORDER.index((kind, n)) + 1


STEP_COST, SUMS_COST = 1024, 1280
ROUND_COST = {"ctx": 512, "x": 256, "k": 512, "q": 112, "v": 1024, "max": 64, "norm": 512, "concat": 256, "out": 768,
              "turn": 256, "logit": 128}
COST = [STEP_COST + (SUMS_COST if s else 0) + (ROUND_COST[ROUNDS[s][0]] if s in ROUNDS else 0) for s in range(STEPS)]


def units_at(s):
    return [AHEAD + v for v in range(BUNITS * sum(COST[:s]) // sum(COST), BUNITS * sum(COST[:s + 1]) // sum(COST))]


def attention_stage(nc, a, X, ident, pre):
    with ExitStack() as ctx:
        def sb(name, shape, dt=F32):
            return ctx.enter_context(nc.sbuf_tensor(name, shape, dt))

        def pb(name, shape):
            return ctx.enter_context(nc.psum_tensor(name, shape, F32))

        wq = sb("wq", [P, P])
        w_raw = sb("a_w_raw", [2 * DC, 2, P])
        w_kv = sb("w_kv", [2 * DC, 2, 2, P], F32R)
        wo = sb("wo", [P, P])
        bq = sb("bq", [P, 1])
        bk = sb("bk", [P, 1])
        bv = sb("bv", [P, P])
        bo = sb("bo", [P, D])
        keys = sb("keys", [P, KT, DC])
        keys2 = sb("keys2", [P, KT, 2, DC], F32R)
        ctxT = sb("ctxT", [2 * DC, LK], F32R)
        xs = sb("xs", [P, 2, D])
        xT = sb("xT", [P, L])
        xf = sb("xf", [P, L])
        kq = sb("kq", [P, LK + L])
        parts = sb("parts", [P, 2 * (LK + L)], F32R)
        k_lo, q_hi = parts[:, 0:LK], parts[:, LK:LK + L]
        k_hi, q_lo = parts[:, LK + L:2 * LK + L], parts[:, 2 * LK + L:]
        stack = sb("stack", [P, G4, LK + L], F32R)
        qblk = sb("qblk", [P, G4, HG, L], F32R)
        own = sb("own", [SR, HG, 1])
        unit_col = sb("unit_col", [P, 1])
        vn = sb("vn", [P, KT, P])
        V = sb("V", [P, KT, H, 32])
        pT = sb("pT", [P, 2, HG, L])
        mx = sb("mx", [P, 2, 2 * HG, 4])
        neg = sb("neg", [P, 2, 2 * HG])
        negT = sb("negT", [2 * HG, P], F32R)
        oS = sb("oS", [P, L])
        rden = sb("rden", [P, 2, HG])
        cc = sb("cc", [P, 2, H, DK])
        ccT = sb("ccT", [P, L])
        xa = sb("xa", [P, 2, D])
        xb = sb("xb", [P, 2, D])
        st = sb("a_st", [P, 2, 6])
        mom = sb("a_mom", [P, 5, 2])
        mean = sb("a_mean", [P, 2])
        ve = sb("a_ve", [P, 2])
        lnv = sb("a_lnv", [P, 2])
        rr = sb("a_rr", [P, 3, 2])
        rstd = sb("a_rstd", [P, 2])

        ps_s = pb("ps_s", [P, 3, 2, L])
        ps_m = pb("ps_m", [P, 3, 512])
        ps_o = pb("ps_o", [P, 2, L])
        ps_x = pb("ps_x", [P, 512])

        names = ("w_in w_split keys2_ready first_split zero_done small_done set_done own_done scores exps pv "
                 "units reduced neg_ready bank_full bank_free row_in "
                 "xs_ready parts_ready qblk_ready v_ready keys_in o_copied o_rec ln_steps lnv_done r_ready").split()
        S = {n: ctx.enter_context(nc.semaphore("a_" + n)) for n in names}
        stack_in = [ctx.enter_context(nc.semaphore(f"a_stack_in{g}")) for g in range(G4)]
        block = ctx.enter_context(nc.Block())
        N_W = 10
        CREDIT = 2
        CREDIT3 = 3
        LN_STEPS, END_AT = 10, 6
        HALVES = 2 * STEPS

        def released(b, per_batch, n):
            return b * per_batch + n - 3 + 1 + CREDIT3 + (1 if n < 2 else 0)

        def bank_of(kind, rounds, b):
            return ps_o[:, :, :].rearrange("p t l -> p (t l)") if b is None and kind != "max" and rounds % 2 == 0 else ps_x

        def m_buf(w):
            return (w - AHEAD + BUNITS) % BUNITS % 3

        @block.sync
        def _(sp):
            row = lambda v: v.rearrange("(o d) -> o d", o=1)
            col = lambda v: v.rearrange("(p o) -> p o", o=1)
            for dst, src in ((wq[:, :], a["L0_xattn_Wq"]), (w_raw[0:DC, 0, :], a["L0_xattn_Wk"]), (w_raw[DC:, 0, :], a["L0_xattn_Wk"]),
                             (w_raw[0:DC, 1, :], a["L0_xattn_Wv"]), (w_raw[DC:, 1, :], a["L0_xattn_Wv"]),
                             (wo[:, :], a["L0_xattn_Wo"]), (bq[:, :], col(a["L0_xattn_bq"])),
                             (bk[:, :], col(a["L0_xattn_bk"])),
                             (bv[:, :], row(a["L0_xattn_bv"]).to_broadcast([P, P])),
                             (bo[:, :], row(a["L0_xattn_bo"]).to_broadcast([P, D]))):
                sp.dma_start(dst, src).then_inc(S["w_in"], 16)

            def load_keys(n):
                c = a["ctx_512"][n, :, :] if isinstance(n, int) else a["ctx_512"][bass.ds(n, 1), :, :].rearrange("o k d -> (o k) d")
                sp.dma_start(keys[:, 0:KT - 1, :], c[0:(KT - 1) * P, :].rearrange("(t p) d -> p t d", p=P)).then_inc(S["keys_in"], 16)
                sp.dma_start(keys[0:KR, KT - 1, :], c[(KT - 1) * P:LK, :]).then_inc(S["keys_in"], 16)

            def fill_stack(n, g):
                stack_w = stack[:, :, :].bitcast(F32)
                rows = slice(32 * g, 32 * g + 32)
                sp.dma_start(stack_w[0:32, g, 0:LK], k_hi[rows, :].bitcast(F32)).then_inc(stack_in[g], 16)
                sp.dma_start(stack_w[0:32, g, LK:], q_hi[rows, :].bitcast(F32)).then_inc(stack_in[g], 16)
                sp.dma_start(stack_w[32:64, g, :], parts[rows, 0:LK + L].bitcast(F32)).then_inc(stack_in[g], 16)
                sp.dma_start(stack_w[64:96, g, :], parts[rows, LK + L:].bitcast(F32)).then_inc(stack_in[g], 16)

            def fill_row(rounds, g):
                sp.wait_ge(S["bank_free"], rounds)
                sp.dma_start(qblk[SR:SR + 1, g, :, :].rearrange("o h l -> o (h l)").bitcast(F32), negT[:, :].bitcast(F32)).then_inc(S["row_in"], 16)

            load_keys(0)
            sp.wait_ge(S["keys2_ready"], 4)
            load_keys(1)
            sp.wait_ge(S["parts_ready"], 4)
            for g in range(G4):
                fill_stack(0, g)
            fill_row(first_round("max", 0), 0)
            with sp.Fori(0, NB) as b:
                fill_row_at = lambda k: fill_row(round_of(b, "max", k), k % G4)
                fill_row_at(1)
                sp.wait_ge(S["keys2_ready"], b * 4 + 8)
                load_keys((b + 2) % NB)
                fill_row_at(2)
                sp.wait_ge(S["parts_ready"], b * 4 + 8)
                fill_stack(b + 1, 0)
                sp.wait_ge(S["scores"], b * HALVES + 4 * KT)
                fill_stack(b + 1, 1)
                fill_row_at(3)
                sp.wait_ge(S["scores"], b * HALVES + 6 * KT)
                fill_stack(b + 1, 2)
                fill_row_at(4)
                sp.wait_ge(S["scores"], b * HALVES + 8 * KT)
                fill_stack(b + 1, 3)
            for g in range(G4):
                sp.wait_ge(stack_in[g], 64 * (NB + 1))
            sp.wait_ge(S["row_in"], 16 * (G4 * NB + 1))
            sp.wait_ge(S["keys_in"], 32 * (NB + 2))

        @block.gpsimd
        def _(pool):
            pool.memset(own[:, :, :], 0.0).then_inc(S["own_done"], 1)
            pool.wait_ge(S["own_done"], 1)
            for part in range(3):
                v = own[32 * part:32 * part + 32, :, 0]
                pool.affine_select(out=v, in_=v, compare_op=ALU.is_gt, fill=1.0, base=0,
                                   pattern=[[DK, HG]], channel_multiplier=-1).then_inc(S["own_done"], 1)
                pool.wait_ge(S["own_done"], 2 + 2 * part)
                pool.affine_select(out=v, in_=v, compare_op=ALU.is_gt, fill=0.0, base=DK,
                                   pattern=[[DK, HG]], channel_multiplier=-1).then_inc(S["own_done"], 1)
                pool.wait_ge(S["own_done"], 3 + 2 * part)
            pool.wait_ge(S["small_done"], 1)

            def copy_x(n, count):
                src = X[:, PAD:PAD + 2, :] if isinstance(n, int) else X[:, bass.ds(n * 2 + PAD, 2), :]
                pool.tensor_tensor(out=xs[:, :, :], in0=src, in1=unit_col[:, 0:1].unsqueeze(2).to_broadcast([P, 2, D]),
                                   op=ALU.mult).then_inc(S["xs_ready"], 1)
                pool.wait_ge(S["xs_ready"], count)

            def split_keys(n):
                pool.wait_ge(S["keys_in"], n * 32 + 32)
                for i, (part, rows, tiles) in enumerate((
                    (0, slice(0, P), slice(0, KT - 1)), (0, slice(0, KR), slice(KT - 1, KT)),
                    (1, slice(0, P), slice(0, KT - 1)), (1, slice(0, KR), slice(KT - 1, KT)),
                )):
                    src, dst = keys[rows, tiles, :], keys2[rows, tiles, part, :]
                    if part == 0:
                        pool.tensor_tensor(out=dst, in0=src, in1=unit_col[rows, 0:1].unsqueeze(2).to_broadcast(list(src.shape)),
                                           op=ALU.mult).then_inc(S["keys2_ready"], 1)
                    else:
                        pool.tensor_tensor(out=dst, in0=src, in1=keys2[rows, tiles, 0, :].bitcast(F32),
                                           op=ALU.subtract).then_inc(S["keys2_ready"], 1)
                    pool.wait_ge(S["keys2_ready"], n * 4 + i + 1)

            def split(base):
                for n, (dst, src, hi) in enumerate((
                    (k_hi, kq[:, 0:LK], None), (q_hi, kq[:, LK:], None),
                    (k_lo, kq[:, 0:LK], k_hi), (q_lo, kq[:, LK:], q_hi),
                )):
                    if hi is None:
                        pool.tensor_tensor(out=dst, in0=src, in1=unit_col[:, 0:1].to_broadcast([P, src.shape[1]]),
                                           op=ALU.mult).then_inc(S["parts_ready"], 1)
                    else:
                        pool.tensor_tensor(out=dst, in0=src, in1=hi.bitcast(F32), op=ALU.subtract).then_inc(S["parts_ready"], 1)
                    pool.wait_ge(S["parts_ready"], base + n + 1)

            def spread_q(g, count):
                pool.tensor_tensor(out=qblk[0:SR, g, :, :], in0=stack[0:SR, g, LK:].bitcast(F32).unsqueeze(1).to_broadcast([SR, HG, L]),
                                   in1=own[:, :, :].to_broadcast([SR, HG, L]), op=ALU.mult).then_inc(S["qblk_ready"], 1)
                pool.wait_ge(S["qblk_ready"], count)

            def spread_v(g, count):
                heads = slice(HG * g, HG * g + HG)
                cols = slice(32 * g, 32 * g + 32)
                b_v = bv[:, cols].rearrange("p (h d) -> p h d", d=DK)
                for t0, t1, p in ((0, KT - 1, P), (KT - 1, KT, KR)):
                    for t in range(t0, t1):
                        pool.tensor_tensor(out=V[0:p, t, heads, 0:DK], in0=vn[0:p, t, cols].rearrange("p (h d) -> p h d", d=DK),
                                           in1=b_v[0:p], op=ALU.add).then_inc(S["v_ready"], 1)
                pool.wait_ge(S["v_ready"], count)

            split_keys(0)
            copy_x(0, 1)
            pool.wait_ge(S["set_done"], 1)
            pool.wait_ge(S["bank_free"], first_round("v", 3))
            for g in range(G4):
                pool.wait_ge(stack_in[g], 64)
                spread_q(g, g + 1)
                spread_v(g, KT * (g + 1))
            with pool.Fori(0, NB) as b:
                pool.wait_ge(S["bank_full"], b * len(ORDER) + len(FIRST_ROUNDS))
                copy_x((b + 1) % NB, b * 2 + 2)
                split_keys(b + 1)
                for g in range(G4):
                    pool.wait_ge(stack_in[g], b * 64 + 64)
                pool.wait_ge(S["bank_free"], round_of(b, "k", 3))
                split(b * 4 + 4)
                pool.wait_ge(S["bank_free"], round_of(b, "v", 3))
                for g in range(G4):
                    if g == 1:
                        pool.wait_ge(S["bank_full"], round_of(b, "x", 0))
                        pool.wait_ge(S["ln_steps"], b * LN_STEPS + LN_STEPS)
                        copy_x(b - 1, b * 2 + 3)
                    pool.wait_ge(stack_in[g], b * 64 + 128)
                    pool.wait_ge(S["scores"], b * HALVES + 2 * KT * (g + 1))
                    spread_q(g, b * 4 + g + 5)
                    pool.wait_ge(S["pv"], b * STEPS + KT * (g + 1) + CREDIT)
                    spread_v(g, b * (4 * KT) + KT * (g + 5))

        @block.tensor
        def _(pe):
            pe.wait_ge(S["w_in"], 16 * N_W)
            pe.wait_ge(S["small_done"], 1)
            pe.wait_ge(pre.sems["router_in"], 16)
            pe.sem_inc(S["pv"], CREDIT)

            def bank_round(kind, n, rounds, b):
                bank = bank_of(kind, rounds, b)
                if b is not None or kind == "max":
                    pe.wait_ge(S["bank_free"], rounds - 1)
                elif rounds > 2:
                    pe.wait_ge(S["bank_free"], rounds - 2)
                if kind == "ctx":
                    if n == 0:
                        pe.wait_ge(S["keys2_ready"], 4 if b is None else b * 4 + 8)
                    for i, t in enumerate(range(4 * n, min(4 * n + 4, KT))):
                        r = P if t < KT - 1 else KR
                        last = pe.transpose(bank[0:2 * DC, P * i:P * i + r], keys2[0:r, t, :, :].rearrange("p s d -> p (s d)").bitcast(F32), ident[0:r, 0:r])
                elif kind == "x":
                    pe.wait_ge(S["xs_ready"], 1 if b is None else b * 2 + 2)
                    for t in range(2):
                        last = pe.transpose(bank[:, P * t:P * t + P], xs[:, t, :], ident[:, :])
                elif kind == "turn":
                    pe.wait_ge(S["xs_ready"], b * 2 + 3)
                    for t in range(2):
                        last = pe.transpose(bank[:, P * t:P * t + P], xs[:, t, :], ident[:, :])
                elif kind == "logit":
                    for t in range(2):
                        last = pe.matmul(bank[:, E * t:E * t + E], xf[:, P * t:P * t + P], pre.wr[:, :], start=True, stop=True)
                elif kind == "k":
                    if b is None and n == 0:
                        pe.wait_ge(S["w_split"], 2)
                    k0, w = KCH[n]
                    k0, w = k0 - w % 2, w + w % 2
                    for part in range(2):
                        last = pe.matmul(bank[:, 0:w], w_kv[:, 0, part, :], ctxT[:, k0:k0 + w], start=(part == 0), stop=(part == 1))
                elif kind == "q":
                    last = pe.matmul(bank[:, 0:L], wq[:, :], xT[:, :], start=True, stop=True)
                elif kind == "v":
                    for i, t in enumerate(range(4 * n, min(4 * n + 4, KT))):
                        r = P if t < KT - 1 else KR
                        for part in range(2):
                            last = pe.matmul(bank[0:r, P * i:P * i + P], ctxT[:, P * t:P * t + r], w_kv[:, 1, part, :],
                                             start=(part == 0), stop=(part == 1))
                elif kind == "max":
                    pe.wait_ge(S["neg_ready"], 1 if b is None else b * G4 + n + 1)
                    last = pe.transpose(bank[0:2 * HG, 0:P], neg[:, n % 2, :], ident[:, :])
                elif kind == "norm":
                    pe.wait_ge(S["o_copied"], (b * G4 if n == 3 else b * G4 + n + 1) + CREDIT)
                    for t in range(2):
                        last = pe.transpose(bank[:, P * t:P * t + P], oS[:, P * t:P * t + P], ident[:, :])
                elif kind == "concat":
                    for t in range(2):
                        last = pe.transpose(bank[:, P * t:P * t + P], cc[:, t, :, :].rearrange("p h d -> p (h d)"), ident[:, :])
                elif kind == "out":
                    for t in range(2):
                        last = pe.matmul(bank[:, D * t:D * t + D], ccT[:, P * t:P * t + P], wo[:, :], start=True, stop=True)
                last.then_inc(S["bank_full"], 1)

            def unit(w, b):
                g, u = w // UNITS % G4, w % UNITS
                head, tile, quarter = u // 8, u // 4 % 2, u % 4
                k0, cols = QUARTER[quarter]
                if u == 0:
                    pe.wait_ge(S["qblk_ready"], b * G4 + w // UNITS + 1)
                pe.wait_ge(S["reduced"], w + 1 if w < AHEAD else released(b, BUNITS, w - AHEAD) + AHEAD)
                pe.matmul(ps_m[:, m_buf(w), 0:cols], qblk[0:SR, g, head, P * tile:P * tile + P], stack[0:SR, g, k0:k0 + cols],
                          start=True, stop=True).then_inc(S["units"], 1)

            def attend(b, g, kt):
                s = KT * g + kt
                r = P if kt < KT - 1 else KR
                if kt == 0:
                    pe.wait_ge(S["v_ready"], b * (4 * KT) + KT * (g + 1))
                    pe.wait_ge(S["o_copied"], b * G4 + g + CREDIT)
                pe.wait_ge(S["exps"], b * HALVES + 2 * s + 2 + CREDIT3)
                for h in range(HG):
                    last = pe.matmul(ps_o[32 * h:32 * h + 32, g % 2, :], V[0:r, kt, HG * g + h, :], pT[0:r, s % 2, h, :],
                                     start=(kt == 0), stop=(kt == KT - 1))
                last.then_inc(S["pv"], 1)

            for kind, n in FIRST_ROUNDS[:-1]:
                bank_round(kind, n, first_round(kind, n), None)
            pe.wait_ge(S["set_done"], 1)
            for w in range(AHEAD):
                unit(w, 0)
                if w == UNITS:
                    bank_round("max", 0, first_round("max", 0), None)
            with pe.Fori(0, NB) as b:
                for s in range(STEPS):
                    g, kt = s // KT, s % KT
                    r = P if kt < KT - 1 else KR
                    if kt == 0:
                        pe.wait_ge(S["row_in"], b * (16 * G4) + 16 * (g + 1))
                    todo = units_at(s)
                    for i in range(2):
                        half = 2 * s + i
                        pe.wait_ge(S["exps"], released(b, HALVES, half))
                        pe.matmul(ps_s[0:r, half % 3, :, :], stack[0:SR + 1, g, P * kt:P * kt + r],
                                  qblk[0:SR + 1, g, 2 * i:2 * i + 2, :], start=True, stop=True).then_inc(S["scores"], 1)
                        if todo:
                            unit(todo.pop(0), b)
                    if s:
                        attend(b, (s - 1) // KT, (s - 1) % KT)
                    for w in todo:
                        unit(w, b)
                    if s in ROUNDS:
                        kind, n = ROUNDS[s]
                        bank_round(kind, n, round_of(b, kind, n), b)
                attend(b, G4 - 1, KT - 1)
            for kind, n in ORDER[:3]:
                bank_round(kind, n, round_of(NB, kind, n), NB)

        @block.scalar
        def _(act):
            act.preload_act_table_set("natural_log_exp_and_others")
            act.wait_ge(S["w_in"], 16 * N_W)
            act.sem_inc(S["exps"], CREDIT3)
            act.sem_inc(S["o_copied"], CREDIT)

            def drain(kind, n, rounds, b):
                if kind not in ("ctx", "x", "k", "q", "v", "concat", "turn"):
                    return
                if kind == "v" and n == 0 and b is not None:
                    act.wait_ge(S["v_ready"], b * (4 * KT) + 4 * KT)
                act.wait_ge(S["bank_full"], rounds)
                bank = bank_of(kind, rounds, b)
                if kind == "ctx":
                    k0, w = KCH[n]
                    last = act.activation(ctxT[:, k0:k0 + w], bank[0:2 * DC, 0:w], ACT.Copy)
                elif kind == "x":
                    last = act.activation(xT[:, :], bank[:, 0:L], ACT.Copy)
                elif kind == "k":
                    k0, w = KCH[n]
                    last = act.activation(kq[:, k0:k0 + w], bank[:, w % 2:w % 2 + w], ACT.Identity, bias=bk[:, 0:1])
                elif kind == "q":
                    last = act.activation(kq[:, LK:], bank[:, 0:L], ACT.Identity, bias=bq[:, 0:1])
                elif kind == "v":
                    if n < 3:
                        last = act.activation(vn[:, 4 * n:4 * n + 4, :].rearrange("p t c -> p (t c)"), bank[:, :], ACT.Copy)
                    else:
                        last = act.activation(vn[0:KR, KT - 1, :], bank[0:KR, 0:P], ACT.Copy)
                elif kind == "turn":
                    last = act.activation(xf[:, :], bank[:, 0:L], ACT.Copy)
                elif kind == "concat":
                    last = act.activation(ccT[:, :], bank[:, 0:L], ACT.Copy)
                last.then_inc(S["bank_free"], 1)

            def copy_o(b, g):
                act.wait_ge(S["pv"], b * STEPS + KT * (g + 1) + CREDIT)
                act.wait_ge(S["bank_full"], round_of(b, "out", 0) if g == 0 else round_of(b, "norm", g - 1))
                act.activation(oS[:, :], ps_o[:, g % 2, :], ACT.Copy).then_inc(S["o_copied"], 1)

            def root(b):
                act.wait_ge(S["ln_steps"], b * LN_STEPS + 5)
                act.activation(lnv[:, :], ve[:, :], ACT.Ln).then_inc(S["lnv_done"], 1)
                act.wait_ge(S["lnv_done"], b + 1)
                act.activation(rr[:, 0, :], lnv[:, :], ACT.Exp, scale=-0.5).then_inc(S["r_ready"], 1)

            for kind, n in FIRST_ROUNDS[:-1]:
                drain(kind, n, first_round(kind, n), None)
            with act.Fori(0, NB) as b:
                for s in range(STEPS):
                    kt = s % KT
                    r = P if kt < KT - 1 else KR
                    act.wait_ge(S["pv"], b * STEPS + s + 1)
                    for i in range(2):
                        half = 2 * s + i
                        act.wait_ge(S["scores"], b * HALVES + half + 1)
                        act.activation(pT[0:r, s % 2, 2 * i:2 * i + 2, :], ps_s[0:r, half % 3, :, :], ACT.Exp,
                                       scale=DK ** -0.5).then_inc(S["exps"], 1)
                    if kt == 0 and s:
                        copy_o(b, s // KT - 1)
                    if s == END_AT + 4:
                        root(b)
                    if s in ROUNDS:
                        kind, n = ROUNDS[s]
                        drain(kind, n, round_of(b, kind, n), b)
                copy_o(b, G4 - 1)
            for kind, n in ORDER[:3]:
                drain(kind, n, round_of(NB, kind, n), NB)
            root(NB)

        @block.vector
        def _(dve):
            dve.memset(unit_col[:, :], 1.0).then_inc(S["small_done"], 1)
            dve.memset(V[:, :, :, :].rearrange("p t h c -> p (t h c)"), 0.0).then_inc(S["zero_done"], 1)
            dve.memset(oS[:, :], 1.0)
            dve.memset(X[:, 0:PAD, :], 0.0)
            dve.wait_ge(S["w_in"], 16 * N_W)
            dve.tensor_copy(w_kv[:, :, 0, :], w_raw[:, :, :]).then_inc(S["w_split"], 1)
            dve.wait_ge(S["w_split"], 1)
            dve.tensor_tensor(out=w_kv[:, :, 1, :], in0=w_raw[:, :, :], in1=w_kv[:, :, 0, :].bitcast(F32), op=ALU.subtract).then_inc(S["w_split"], 1)
            dve.wait_ge(S["zero_done"], 1)
            dve.memset(V[:, :, :, DK:DK + 1], 1.0)
            for g in range(G4):
                dve.memset(stack[SR:SR + 1, g, 0:LK].bitcast(F32), 1.0)
            dve.sem_inc(S["reduced"], CREDIT3)
            dve.memset(cc[:, :, :, :], 1.0).then_inc(S["set_done"], 1)
            dve.wait_ge(S["set_done"], 1)
            for c, (k0, w) in enumerate(KCH):
                dve.wait_ge(S["bank_free"], first_round("k", c))
                dve.tensor_copy(k_hi[:, k0:k0 + w], kq[:, k0:k0 + w]).then_inc(S["first_split"], 1)
                dve.wait_ge(S["first_split"], c + 1)
                last = dve.tensor_tensor(out=k_lo[:, k0:k0 + w], in0=kq[:, k0:k0 + w], in1=k_hi[:, k0:k0 + w].bitcast(F32), op=ALU.subtract)
            last.then_inc(S["parts_ready"], 2)
            dve.wait_ge(S["bank_free"], first_round("q", 0))
            dve.tensor_copy(q_hi, kq[:, LK:]).then_inc(S["first_split"], 1)
            dve.wait_ge(S["first_split"], len(KCH) + 1)
            dve.tensor_tensor(out=q_lo, in0=kq[:, LK:], in1=q_hi.bitcast(F32), op=ALU.subtract).then_inc(S["parts_ready"], 2)

            def reduce(w, b):
                par, u = w // UNITS % 2, w % UNITS
                quarter = u % 4
                dve.wait_ge(S["units"], b * BUNITS + w + 1)
                dve.reduce_max(mx[:, par, u // 4, quarter:quarter + 1], ps_m[:, m_buf(w), 0:QUARTER[quarter][1]], AX.X).then_inc(S["reduced"], 1)
                if u == UNITS - 1:
                    dve.wait_ge(S["reduced"], b * BUNITS + w + 1 + CREDIT3)
                    dve.tensor_reduce(out=neg[:, par, :], in_=mx[:, par, :, :], op=ALU.max, axis=AX.X, negate=True).then_inc(S["neg_ready"], 1)

            def drain(kind, n, rounds, b):
                if kind not in ("max", "norm", "out", "logit"):
                    return
                if kind == "max" and b is not None:
                    dve.wait_ge(S["row_in"], b * (16 * G4) + 16 * n)
                dve.wait_ge(S["bank_full"], rounds)
                if kind == "max":
                    dve.tensor_copy(negT[:, :], ps_x[0:2 * HG, 0:P]).then_inc(S["bank_free"], 1)
                elif kind == "logit":
                    dve.tensor_copy(pre.logits[:, bass.ds(b * 2, 2), :], ps_x[:, 0:2 * E].rearrange("p (t e) -> p t e", e=E)).then_inc(S["bank_free"], 1)
                elif kind == "norm":
                    v = ps_x[:, 0:L].rearrange("p (t h c) -> p t h c", t=2, h=HG)
                    dve.reciprocal(rden[:, :, :], v[:, :, :, DK]).then_inc(S["o_rec"], 1)
                    dve.wait_ge(S["o_rec"], b * G4 + (1 if n == 3 else n + 2))
                    dve.tensor_tensor(out=cc[:, :, HG * n:HG * n + HG, :], in0=v[:, :, :, 0:DK],
                                      in1=rden[:, :, :].unsqueeze(3).to_broadcast([P, 2, HG, DK]), op=ALU.mult).then_inc(S["bank_free"], 1)
                elif kind == "out":
                    tiles = X[:, bass.ds(b * 2, 2), :] if not isinstance(b, int) else X[:, 2 * b:2 * b + 2, :]
                    dve.tensor_tensor(out=xa[:, :, :], in0=tiles, in1=ps_x[:, 0:L].rearrange("p (t d) -> p t d", t=2),
                                      op=ALU.add).then_inc(S["bank_free"], 1)

            def end_batch(b, n):
                steps = S["ln_steps"]
                base = b * LN_STEPS + n
                if n:
                    dve.wait_ge(steps, base)
                if n == 0:
                    dve.wait_ge(S["bank_free"], round_of(b, "out", 0))
                    last = dve.tensor_tensor(out=xb[:, :, :], in0=xa[:, :, :], in1=bo[:, :].unsqueeze(1).to_broadcast([P, 2, D]), op=ALU.add)
                elif n == 1:
                    for t in range(2):
                        last = dve.bn_stats(st[:, t, :], xb[:, t, :])
                elif n == 2:
                    dve.tensor_tensor(out=mom[:, 0, :], in0=st[:, :, 1], in1=st[:, :, 4], op=ALU.add)
                    dve.tensor_tensor(out=mom[:, 1, :], in0=st[:, :, 1], in1=st[:, :, 4], op=ALU.subtract)
                    last = dve.tensor_tensor(out=mom[:, 2, :], in0=st[:, :, 2], in1=st[:, :, 5], op=ALU.add)
                elif n == 3:
                    dve.tensor_scalar(mean[:, :], mom[:, 0, :], 0.5, None, ALU.mult)
                    dve.tensor_tensor(out=mom[:, 3, :], in0=mom[:, 1, :], in1=mom[:, 1, :], op=ALU.mult)
                    last = dve.tensor_scalar(mom[:, 4, :], mom[:, 2, :], 1.0 / D, EPS, ALU.mult, ALU.add)
                elif n == 4:
                    last = dve.scalar_tensor_tensor(out=ve[:, :], in0=mom[:, 3, :], scalar=0.25, in1=mom[:, 4, :],
                                                    op0=ALU.mult, op1=ALU.add)
                elif n == 5:
                    dve.wait_ge(S["r_ready"], b + 1)
                    last = dve.tensor_tensor(out=rr[:, 1, :], in0=rr[:, 0, :], in1=rr[:, 0, :], op=ALU.mult)
                elif n == 6:
                    last = dve.tensor_tensor(out=rr[:, 2, :], in0=rr[:, 1, :], in1=ve[:, :], op=ALU.mult)
                elif n == 7:
                    last = dve.tensor_scalar(rr[:, 1, :], rr[:, 2, :], -0.5, 1.5, ALU.mult, ALU.add)
                elif n == 8:
                    last = dve.tensor_tensor(out=rstd[:, :], in0=rr[:, 0, :], in1=rr[:, 1, :], op=ALU.mult)
                elif n == 9:
                    for t in range(2):
                        last = dve.tensor_scalar(X[:, b * 2 + t, :], xb[:, t, :], mean[:, t:t + 1], rstd[:, t:t + 1], ALU.subtract, ALU.mult)
                last.then_inc(steps, 1)

            for w in range(AHEAD):
                reduce(w, 0)
                if w == UNITS:
                    drain("max", 0, first_round("max", 0), None)
            with dve.Fori(0, NB) as b:
                for s in range(STEPS):
                    for w in units_at(s):
                        reduce(w, b)
                    if s in ROUNDS:
                        kind, n = ROUNDS[s]
                        drain(kind, n, round_of(b, kind, n), b)
                    if END_AT <= s < END_AT + LN_STEPS:
                        end_batch(b, s - END_AT)
            for kind, n in ORDER[:3]:
                drain(kind, n, round_of(NB, kind, n), NB)
            for n in range(LN_STEPS):
                end_batch(NB, n)


UT = 3
BODY = 6
GT = 4


def experts_stage(nc, a, X, ident, pre, out):
    assert (TE - UT) % BODY == 0 and BODY % UT == 0 and BODY % 2 == 0
    with ExitStack() as ctx:
        def sb(name, shape, dt=F32):
            return ctx.enter_context(nc.sbuf_tensor(name, shape, dt))

        def pb(name, shape):
            return ctx.enter_context(nc.psum_tensor(name, shape, F32))

        x_slots, w1_lo, b_parts, wr = pre.x_slots, pre.w1, pre.b_parts, pre.wr
        y_slots = nc.dram_tensor("y_slots", (TE * P, D), F32, kind="Internal").ap()

        w2 = sb("w2", [P, E, HID // P, D])
        w1_hi = sb("w1_hi", [P, E, 2 * HID], F32R)
        b1 = sb("b1", [2, E, 2 * HID], F32R)
        b2 = sb("b2", [2, E, D], F32R)
        two0 = sb("two0", [2, P])
        two = sb("two", [2, P], F32R)
        br = sb("br", [P, E])
        tri = sb("tri", [P, P])
        allone = sb("allone", [P, P])
        numi = sb("numi", [P, 64], I32)
        num = sb("num", [P, 64])
        xTr = sb("xTr", [P, 2 * P])
        lg = sb("lg", [P, E, NT])
        best = sb("best", [P, NT])
        hit = sb("hit", [P, E, NT])
        first = sb("first", [P, NT])
        oh = sb("oh", [P, E, NT])
        more = sb("more", [P, E, NT])
        tot = sb("tot", [P, E, NT])
        incl = sb("incl", [P, E, NT])
        place = sb("place", [P, E, NT])
        full = sb("full", [P, E, NT])
        nt = sb("nt", [P, E])
        end = sb("end", [P, E])
        start = sb("start", [P, E])
        slotf = sb("slotf", [P, NT])
        slot = sb("slot", [P, NT], I32)
        past = sb("past", [P, TE, E])
        idf = sb("idf", [P, TE])
        tile_expert = sb("tile_expert", [P, TE], I32)
        xt = sb("xt", [P, UT, D])
        x_hi = sb("x_hi", [P, UT, P], F32R)
        x_lo = sb("x_lo", [P, UT, P], F32R)
        sg = sb("sg", [P, UT, HID])
        act_ = sb("act_", [P, UT, HID])
        aT = sb("aT", [P, UT, HID // P, P])
        yt = sb("yt", [P, UT, D])
        Y = sb("Y", [P, NT, D])
        stt = sb("e_st", [P, NT, 6])
        mom = sb("e_mom", [P, 5, NT])
        mean = sb("e_mean", [P, NT])
        ve = sb("e_ve", [P, NT])
        lnv = sb("e_lnv", [P, NT])
        rr = sb("e_rr", [P, 3, NT])
        rstd = sb("e_rstd", [P, NT])

        ps_t = pb("e_ps_t", [P, 2, 512])
        ps_h = pb("e_ps_h", [P, 2, 2, HID])
        ps_y = pb("e_ps_y", [P, 512])
        ps_l = pb("e_ps_l", [P, 512])

        names = ("w_in w2_in b_in consts set_done xtr_ps xtr_sb logits steps oh_ready counts "
                 "slots_ready scattered xt_ps w_split x_split xt_sb h_ps sg_done act_done at_ps at_sb y_ps y_sb "
                 "sums moments root_steps stats_done ve_ready lnv_done r_ready z_done out_done").split()
        S = {n: ctx.enter_context(nc.semaphore("e_" + n)) for n in names}
        gathered = [ctx.enter_context(nc.semaphore(f"e_gathered{g}")) for g in range(NT // GT)]
        xt_in = [ctx.enter_context(nc.semaphore(f"e_xt_in{g}")) for g in range(UT)]
        y_out = [ctx.enter_context(nc.semaphore(f"e_y_out{g}")) for g in range(UT)]
        block = ctx.enter_context(nc.Block())

        @block.sync
        def _(sp):
            row = lambda v: v.rearrange("(o d) -> o d", o=1)
            sp.dma_start(br[:, :], row(a["L0_ffn_router_b"]).to_broadcast([P, E])).then_inc(S["w_in"], 16)
            for e in range(E):
                sp.dma_start(w2[:, e, :, :], a["L0_ffn_w2"][e].rearrange("(j p) d -> p j d", p=P)).then_inc(S["w2_in"], 16)
            for part in range(2):
                for dst, c0, c1 in ((b1, 0, BC1), (b2, BC1, BC)):
                    sp.dma_start(dst[part:part + 1, :, :].rearrange("o e n -> o (e n)").bitcast(F32),
                                 b_parts[:, part, c0:c1].bitcast(F32)).then_inc(S["b_in"], 16)
            sp.wait_ge(S["scattered"], 16 * NT)
            for k in range(UT):
                sp.dma_start(xt[:, k, :], x_slots[P * k:P * k + P, :]).then_inc(xt_in[k], 16)
                sp.sem_inc(y_out[k], 16)

            def load(n, k):
                sp.wait_ge(S["xt_ps"], n + 1)
                sp.dma_start(xt[:, k, :], x_slots[bass.ds(((n + UT) % TE) * P, P), :]).then_inc(xt_in[k], 16)

            def store(n, k):
                sp.wait_ge(S["y_sb"], n + 1)
                sp.dma_start(y_slots[bass.ds(n * P, P), :], yt[:, k, :]).then_inc(y_out[k], 16)

            for n in range(UT):
                load(n, n)
                if n >= 2:
                    store(n - 2, n - 2)
            with sp.Fori(0, (TE - UT) // BODY) as i:
                for m in range(BODY):
                    n = i * BODY + UT + m
                    load(n, m % UT)
                    store(n - 2, (m - 2) % UT)
            for n in (TE - 2, TE - 1):
                store(n, n % UT)
            for k in range(UT):
                sp.wait_ge(xt_in[k], 16 * (TE // UT + 1))
            for g in range(NT // GT):
                sp.wait_ge(S["z_done"], g + 1)
                sp.dma_start(tokens(out)[:, GT * g:GT * g + GT, :], Y[:, GT * g:GT * g + GT, :]).then_inc(S["out_done"], 16)
            sp.wait_ge(S["out_done"], 16 * (NT // GT))

        @block.gpsimd
        def _(pool):
            pool.iota(numi[:, :], pattern=[[1, 64]], base=0, channel_multiplier=0).then_inc(S["consts"], 1)
            pool.wait_ge(S["consts"], 1)
            pool.memset(tri[:, :], 1.0).then_inc(S["consts"], 1)
            pool.wait_ge(S["consts"], 2)
            pool.affine_select(out=tri[:, :], in_=tri[:, :], compare_op=ALU.is_gt, fill=0.0, base=0,
                               pattern=[[1, P]], channel_multiplier=-1).then_inc(S["consts"], 1)
            pool.wait_ge(pre.sems["slots_zeroed"], 64)
            pool.wait_ge(S["slots_ready"], 1)
            for t in range(NT):
                pool.indirect_dma_start(x_slots[:, :], bass.IndirectOffsetOnAxis(ap=slot[:, t:t + 1], axis=0),
                                        X[:, PAD + t, :], None).then_inc(S["scattered"], 16)
            for k in range(UT):
                pool.wait_ge(y_out[k], 16 * (TE // UT + 1))
            for t in range(NT):
                pool.indirect_dma_start(Y[:, t, :], None, y_slots[:, :],
                                        bass.IndirectOffsetOnAxis(ap=slot[:, t:t + 1], axis=0)).then_inc(gathered[t // GT], 16)

        @block.tensor
        def _(pe):
            for t in range(2):
                last = pe.transpose(ps_t[:, 0, P * t:P * t + P], X[:, PAD + NT - 2 + t, :], ident[:, :])
            last.then_inc(S["xtr_ps"], 1)
            pe.wait_ge(S["xtr_sb"], 1)
            for t in range(2):
                last = pe.matmul(ps_l[:, E * t:E * t + E], xTr[:, P * t:P * t + P], wr[:, :], start=True, stop=True)
            last.then_inc(S["logits"], 1)
            pe.wait_ge(S["consts"], 3)
            pe.wait_ge(S["set_done"], 1)
            pe.wait_ge(S["oh_ready"], 1)
            ohf = oh[:, :, :].rearrange("p e t -> p (e t)")
            pe.matmul(ps_l[:, 0:E * NT], tri[:, :], ohf, start=True, stop=True)
            pe.matmul(ps_l[:, E * NT:], allone[:, :], ohf, start=True, stop=True).then_inc(S["counts"], 1)
            pe.wait_ge(S["w_split"], 2 * E)
            pe.wait_ge(S["w2_in"], 16 * E)
            pe.wait_ge(S["b_in"], 64)
            pe.wait_ge(S["slots_ready"], 1)

            def expert(n):
                return pe.value_load(tile_expert[0:1, bass.ds(n, 1)], min_val=0, max_val=E - 1)

            def turn_x(n, k, loads):
                pe.wait_ge(xt_in[k], loads)
                pe.transpose(ps_t[:, 0, 0:P], xt[:, k, :], ident[:, :]).then_inc(S["xt_ps"], 1)

            def up(n, k, h, first):
                e = expert(n)
                if not first:
                    pe.wait_ge(S["act_done"], n - 1)
                for c in range(2):
                    cols = slice(HID * c, HID * c + HID)
                    pe.matmul(ps_h[:, h, c, :], two[:, :], b1[:, bass.ds(e, 1), cols], start=True, stop=False)
                    for x, w in ((x_hi, w1_hi), (x_lo, w1_hi), (x_hi, w1_lo)):
                        last = pe.matmul(ps_h[:, h, c, :], x[:, k, :], w[:, bass.ds(e, 1), cols], start=False, stop=(w is w1_lo))
                last.then_inc(S["h_ps"], 1)

            def turn_act(n, k, first):
                pe.wait_ge(S["act_done"], n + 1)
                if not first:
                    pe.wait_ge(S["at_sb"], n)
                for j in range(HID // P):
                    last = pe.transpose(ps_t[:, 1, P * j:P * j + P], act_[:, k, P * j:P * j + P], ident[:, :])
                last.then_inc(S["at_ps"], 1)

            def down(n, k, first):
                e = expert(n)
                pe.wait_ge(S["at_sb"], n + 1)
                if not first:
                    pe.wait_ge(S["y_sb"], n)
                pe.matmul(ps_y[:, 0:D], two[:, :], b2[:, bass.ds(e, 1), :], start=True, stop=False)
                for j in range(HID // P):
                    last = pe.matmul(ps_y[:, 0:D], aT[:, k, j, :], w2[:, bass.ds(e, 1), j, :], start=False, stop=(j == HID // P - 1))
                last.then_inc(S["y_ps"], 1)

            turn_x(0, 0, 16)
            for n in range(UT):
                pe.wait_ge(S["x_split"], n + 1)
                turn_x(n + 1, (n + 1) % UT, 16 * ((n + 1) // UT + 1))
                up(n, n, n % 2, n < 2)
                if n >= 1:
                    turn_act(n - 1, n - 1, n == 1)
                if n >= 2:
                    down(n - 2, n - 2, n == 2)
            with pe.Fori(0, (TE - UT) // BODY) as i:
                for m in range(BODY):
                    n = i * BODY + UT + m
                    pe.wait_ge(S["x_split"], n + 1)
                    turn_x(n + 1, (m + 1) % UT, i * (16 * BODY // UT) + 16 * ((m + 1) // UT + 2))
                    up(n, m % UT, (UT + m) % 2, False)
                    turn_act(n - 1, (m - 1) % UT, False)
                    down(n - 2, (m - 2) % UT, False)
            turn_act(TE - 1, (TE - 1) % UT, False)
            down(TE - 2, (TE - 2) % UT, False)
            down(TE - 1, (TE - 1) % UT, False)

        @block.scalar
        def _(act):
            act.wait_ge(S["xtr_ps"], 1)
            act.activation(xTr[:, :], ps_t[:, 0, 0:2 * P], ACT.Copy).then_inc(S["xtr_sb"], 1)
            act.preload_act_table(ACT.Sigmoid)

            def x_copy(n, k):
                act.wait_ge(S["xt_ps"], n + 1)
                act.activation(x_hi[:, k, :], ps_t[:, 0, 0:P], ACT.Copy).then_inc(S["xt_sb"], 1)

            def gate(n, k, h):
                act.wait_ge(S["h_ps"], n + 1)
                act.activation(sg[:, k, :], ps_h[:, h, 1, :], ACT.Sigmoid).then_inc(S["sg_done"], 1)

            def act_copy(n, k):
                act.wait_ge(S["at_ps"], n + 1)
                act.activation(aT[:, k, :, :].rearrange("p j t -> p (j t)"), ps_t[:, 1, :], ACT.Copy).then_inc(S["at_sb"], 1)

            x_copy(0, 0)
            for n in range(UT):
                x_copy(n + 1, (n + 1) % UT)
                gate(n, n, n % 2)
                if n >= 1:
                    act_copy(n - 1, n - 1)
            with act.Fori(0, (TE - UT) // BODY) as i:
                for m in range(BODY):
                    n = i * BODY + UT + m
                    x_copy(n + 1, (m + 1) % UT)
                    gate(n, m % UT, (UT + m) % 2)
                    act_copy(n - 1, (m - 1) % UT)
            act_copy(TE - 1, (TE - 1) % UT)
            act.preload_act_table_set("natural_log_exp_and_others")
            for g in range(NT // GT):
                act.wait_ge(S["ve_ready"], g + 1)
                act.activation(lnv[:, GT * g:GT * g + GT], ve[:, GT * g:GT * g + GT], ACT.Ln).then_inc(S["lnv_done"], 1)
                act.wait_ge(S["lnv_done"], g + 1)
                act.activation(rr[:, 0, GT * g:GT * g + GT], lnv[:, GT * g:GT * g + GT], ACT.Exp, scale=-0.5).then_inc(S["r_ready"], 1)

        @block.vector
        def _(dve):
            steps = [0]

            def link(ins):
                steps[0] += 1
                ins.then_inc(S["steps"], 1)
                dve.wait_ge(S["steps"], steps[0])

            def over(v):
                return v.unsqueeze(1).to_broadcast([P, E, NT])

            def along(v):
                return v.unsqueeze(2).to_broadcast([P, E, NT])

            dve.memset(allone[:, :], 1.0)
            dve.memset(two0[:, :], 1.0)
            link(dve.memset(more[:, :, :], 1.0))
            dve.memset(more[:, :, 0:1], 0.0)
            dve.tensor_copy(two[:, :], two0[:, :]).then_inc(S["set_done"], 1)
            dve.wait_ge(S["consts"], 1)
            link(dve.tensor_copy(num[:, :], numi[:, :]))
            dve.wait_ge(S["w_in"], 16)
            n = NT - 2
            dve.tensor_tensor(out=lg[:, :, 0:n], in0=pre.logits[:, PAD:PAD + n, :].rearrange("p t e -> p e t"),
                              in1=br[:, :].unsqueeze(2).to_broadcast([P, E, n]), op=ALU.add)
            dve.wait_ge(S["logits"], 1)
            link(dve.tensor_tensor(out=lg[:, :, n:], in0=ps_l[:, 0:2 * E].rearrange("p (t e) -> p e t", e=E),
                                   in1=br[:, :].unsqueeze(2).to_broadcast([P, E, 2]), op=ALU.add))
            link(dve.tensor_reduce(out=best[:, :], in_=lg[:, :, :].rearrange("p e t -> p t e"), op=ALU.max, axis=AX.X))
            link(dve.tensor_tensor(out=hit[:, :, :], in0=lg[:, :, :], in1=over(best[:, :]), op=ALU.is_lt))
            link(dve.scalar_tensor_tensor(out=place[:, :, :], in0=hit[:, :, :], scalar=float(E), in1=along(num[:, 0:E]),
                                          op0=ALU.mult, op1=ALU.add))
            link(dve.tensor_reduce(out=first[:, :], in_=place[:, :, :].rearrange("p e t -> p t e"), op=ALU.min, axis=AX.X))
            dve.tensor_tensor(out=oh[:, :, :], in0=along(num[:, 0:E]), in1=over(first[:, :]), op=ALU.is_equal).then_inc(S["oh_ready"], 1)
            dve.wait_ge(S["counts"], 1)
            link(dve.tensor_copy(tot[:, :, :].rearrange("p e t -> p (e t)"), ps_l[:, E * NT:]))
            link(dve.tensor_tensor_scan(incl[:, :, :].rearrange("p e t -> p (e t)"), more[:, :, :].rearrange("p e t -> p (e t)"),
                                        tot[:, :, :].rearrange("p e t -> p (e t)"), 0.0, ALU.mult, ALU.add))
            link(dve.tensor_tensor(out=place[:, :, :], in0=incl[:, :, :], in1=tot[:, :, :], op=ALU.subtract))
            link(dve.tensor_tensor(out=hit[:, :, :].rearrange("p e t -> p (e t)"), in0=place[:, :, :].rearrange("p e t -> p (e t)"), in1=ps_l[:, 0:E * NT], op=ALU.add))
            link(dve.tensor_scalar(full[:, :, :], num[:, 0:NT].unsqueeze(1).to_broadcast([P, E, NT]), float(P), None, ALU.mult))
            link(dve.tensor_tensor(out=full[:, :, :], in0=full[:, :, :], in1=along(incl[:, :, NT - 1]), op=ALU.is_lt))
            link(dve.tensor_reduce(out=nt[:, :], in_=full[:, :, :], op=ALU.add, axis=AX.X))
            link(dve.tensor_tensor_scan(end[:, :], allone[:, 0:E], nt[:, :], 0.0, ALU.mult, ALU.add))
            link(dve.tensor_tensor(out=start[:, :], in0=end[:, :], in1=nt[:, :], op=ALU.subtract))
            link(dve.tensor_scalar(start[:, :], start[:, :], float(P), None, ALU.mult))
            link(dve.tensor_tensor(out=hit[:, :, :], in0=hit[:, :, :], in1=along(start[:, :]), op=ALU.add))
            link(dve.tensor_tensor(out=hit[:, :, :], in0=hit[:, :, :], in1=oh[:, :, :], op=ALU.mult))
            link(dve.tensor_reduce(out=slotf[:, :], in_=hit[:, :, :].rearrange("p e t -> p t e"), op=ALU.add, axis=AX.X))
            link(dve.tensor_copy(slot[:, :], slotf[:, :]))
            link(dve.tensor_tensor(out=past[:, :, :], in0=num[:, 0:TE].unsqueeze(2).to_broadcast([P, TE, E]),
                                   in1=end[:, :].unsqueeze(1).to_broadcast([P, TE, E]), op=ALU.is_ge))
            link(dve.tensor_reduce(out=idf[:, :], in_=past[:, :, :], op=ALU.add, axis=AX.X))
            link(dve.tensor_scalar(idf[:, :], idf[:, :], float(E - 1), None, ALU.min))
            dve.tensor_copy(tile_expert[:, :], idf[:, :]).then_inc(S["slots_ready"], 1)

            dve.wait_ge(pre.sems["weights_in"], 16 * E)
            for e in range(E):
                dve.tensor_copy(w1_hi[:, e, :], w1_lo[:, e, :].bitcast(F32)).then_inc(S["w_split"], 1)
            for e in range(E):
                dve.wait_ge(S["w_split"], e + 1)
                dve.tensor_tensor(out=w1_lo[:, e, :], in0=w1_lo[:, e, :].bitcast(F32), in1=w1_hi[:, e, :].bitcast(F32),
                                  op=ALU.subtract).then_inc(S["w_split"], 1)

            def split_x(n, k):
                dve.wait_ge(S["xt_sb"], n + 1)
                dve.tensor_tensor(out=x_lo[:, k, :], in0=ps_t[:, 0, 0:P], in1=x_hi[:, k, :].bitcast(F32), op=ALU.subtract).then_inc(S["x_split"], 1)

            def gated(n, k, h):
                dve.wait_ge(S["sg_done"], n + 1)
                dve.tensor_tensor(out=act_[:, k, :], in0=sg[:, k, :], in1=ps_h[:, h, 0, :], op=ALU.mult).then_inc(S["act_done"], 1)

            def y_copy(n, k, stores):
                dve.wait_ge(S["y_ps"], n + 1)
                dve.wait_ge(y_out[k], stores)
                dve.tensor_copy(yt[:, k, :], ps_y[:, 0:D]).then_inc(S["y_sb"], 1)

            split_x(0, 0)
            for n in range(UT):
                split_x(n + 1, (n + 1) % UT)
                gated(n, n, n % 2)
                if n >= 2:
                    y_copy(n - 2, n - 2, 16)
            with dve.Fori(0, (TE - UT) // BODY) as i:
                for m in range(BODY):
                    n = i * BODY + UT + m
                    split_x(n + 1, (m + 1) % UT)
                    gated(n, m % UT, (UT + m) % 2)
                    y_copy(n - 2, (m - 2) % UT, i * (16 * BODY // UT) + 16 * ((m + 1) // UT + 1))
            for n in (TE - 2, TE - 1):
                y_copy(n, n % UT, 16 * (n // UT + 1))
            groups = NT // GT
            for g in range(groups + 1):
                if g < groups:
                    s = slice(GT * g, GT * g + GT)
                    dve.wait_ge(gathered[g], 16 * GT)
                    dve.tensor_tensor(out=Y[:, s, :], in0=Y[:, s, :], in1=X[:, PAD + GT * g:PAD + GT * g + GT, :], op=ALU.add).then_inc(S["sums"], 1)
                    dve.wait_ge(S["sums"], g + 1)
                    for t in range(GT * g, GT * g + GT):
                        last = dve.bn_stats(stt[:, t, :], Y[:, t, :])
                    last.then_inc(S["stats_done"], 1)
                    dve.wait_ge(S["stats_done"], g + 1)
                    variance(dve, stt[:, s, :], mom[:, :, s], mean[:, s], ve[:, s], S["moments"], g * 2, S["ve_ready"])
                if g:
                    s = slice(GT * (g - 1), GT * g)
                    dve.wait_ge(S["r_ready"], g)
                    newton(dve, rstd[:, s], ve[:, s], rr[:, 0, s], rr[:, 1, s], rr[:, 2, s], S["root_steps"], (g - 1) * 4)
                    for t in range(GT * (g - 1), GT * g):
                        last = dve.tensor_scalar(Y[:, t, :], Y[:, t, :], mean[:, t:t + 1], rstd[:, t:t + 1], ALU.subtract, ALU.mult)
                    last.then_inc(S["z_done"], 1)


_OUT = ((16, 256, 128), "float32")


def kernel(**inputs):
    import numpy as _np
    import concourse.bacc as _bacc
    from concourse import mybir as _mybir
    from concourse.bass_utils import run_bass_kernel_spmd as _run

    nc = _bacc.Bacc("TRN2", target_bir_lowering=False, num_devices=1)
    arrays, args = {}, {}
    for name, value in inputs.items():
        v = _np.ascontiguousarray(value)
        arrays[f"in_{name}_dram"] = v
        args[name] = nc.dram_tensor(f"in_{name}_dram", v.shape, _mybir.dt.from_np(v.dtype), kind="ExternalInput").ap()
    out = nc.dram_tensor("out_0_dram", _OUT[0], _mybir.dt.from_np(_np.dtype(_OUT[1])), kind="ExternalOutput").ap()
    build_program(nc, args, out)
    r = _run(nc, [arrays], core_ids=[0])
    return r.results[0]["out_0_dram"]
```
